# Optimizing a Trainium2 kernel written in Bass

```python
import numpy as np
import jax
import jax.numpy as jnp

def _softmax(x, axis=-1):
    return jax.nn.softmax(x, axis=axis)

def _gelu(x):
    return jax.nn.gelu(x, approximate=True)

def _silu(x):
    return jax.nn.silu(x)

def _sigmoid(x):
    return jax.nn.sigmoid(x)

def _layernorm(x, axis=-1, eps=1e-05):
    m = jnp.mean(x, axis=axis, keepdims=True)
    v = jnp.var(x, axis=axis, keepdims=True)
    return (x - m) / jnp.sqrt(v + eps)

def _scatter_add(tgt, idx, src, axis=0):
    return tgt.at[idx].add(src)

def _segment_sum(src, seg, n):
    return jax.ops.segment_sum(src, seg, n)
kernel_name = 'mk_gnn_preln_d4_gnn_r8_ed286a'

def setup_inputs(seed: int=0):
    np.random.seed(seed)
    _w = jnp.asarray

    def _rec_inputs():
        import jax
        import jax.numpy as jnp
        _gk = jax.random.key(seed)
        x = -0.0003713 + 1 * jax.random.normal(jax.random.fold_in(_gk, 1), (6250, 256), jnp.float32)
        src = jax.random.randint(jax.random.fold_in(_gk, 2), (100000,), 0, 6250, jnp.int32)
        dst = jax.random.randint(jax.random.fold_in(_gk, 3), (100000,), 0, 6250, jnp.int32)
        _o = jnp.argsort(dst, stable=True)
        src = src[_o]
        dst = dst[_o]
        edge_type_16 = jax.random.randint(jax.random.fold_in(_gk, 13), (100000,), 0, 16, jnp.int32)
        edge_weight = jax.random.uniform(jax.random.fold_in(_gk, 14), (100000,), jnp.float32, 0.0, 0.999998)
        edge_weight1 = jax.random.uniform(jax.random.fold_in(_gk, 15), (100000, 1), jnp.float32, 0.0, 1)
        return (x, src, dst, edge_type_16, edge_weight, edge_weight1)
    x, src, dst, edge_type_16, edge_weight, edge_weight1 = _rec_inputs()

    def _L0_gnn_setup():
        import jax, jax.numpy as jnp
        import numpy as np
        N_NODES = 6250
        N_EDGES = 100000
        F_IN = 256
        F_OUT = 256
        key = jax.random.key(seed)
        k_x, k_w, k_r, k_c, k_v = jax.random.split(key, 5)
        limit = np.sqrt(6.0 / (F_IN + F_OUT)).astype(np.float32)
        x = jax.random.normal(k_x, (N_NODES, F_IN), dtype=jnp.float32)
        weight = jax.random.uniform(k_w, (F_IN, F_OUT), dtype=jnp.float32, minval=-limit, maxval=limit)
        bias = jnp.zeros((F_OUT,), dtype=jnp.float32)
        rows = jax.random.randint(k_r, (N_EDGES,), 0, N_NODES, dtype=jnp.int64 if jax.config.jax_enable_x64 else jnp.int32)
        cols = jax.random.randint(k_c, (N_EDGES,), 0, N_NODES, dtype=jnp.int64 if jax.config.jax_enable_x64 else jnp.int32)
        vals = jax.random.uniform(k_v, (N_EDGES,), dtype=jnp.float32)
        return {'x': x, 'weight': weight, 'bias': bias, 'rows': rows, 'cols': cols, 'vals': vals}
    _L0_gnn_all = _L0_gnn_setup()
    _L0_gnn_in = {k: v for k, v in _L0_gnn_all.items() if k in ('weight', 'bias')}
    del _L0_gnn_all

    def _L1_gnn_setup():
        import jax, jax.numpy as jnp
        import numpy as np
        N_NODES = 6250
        N_EDGES = 100000
        NUM_RELS = 16
        FEAT = 256
        OUT = 256
        key = jax.random.key(seed)
        ks = jax.random.split(key, 7)
        h = jax.random.normal(ks[0], (N_NODES, FEAT), dtype=jnp.float32)
        norm = jax.random.uniform(ks[1], (N_EDGES, 1), dtype=jnp.float32)
        weight = jax.random.normal(ks[2], (NUM_RELS, FEAT, OUT), dtype=jnp.float32) * 0.05
        gate_weight = jax.random.normal(ks[3], (NUM_RELS, FEAT, 1), dtype=jnp.float32) * 0.05
        src = jax.random.randint(ks[4], (N_EDGES,), 0, N_NODES)
        dst = jax.random.randint(ks[5], (N_EDGES,), 0, N_NODES)
        rel_type = jax.random.randint(ks[6], (N_EDGES,), 0, NUM_RELS)
        return {'h': h, 'norm': norm, 'weight': weight, 'gate_weight': gate_weight, 'src': src, 'dst': dst, 'rel_type': rel_type}
    _L1_gnn_all = _L1_gnn_setup()
    _L1_gnn_in = {k: v for k, v in _L1_gnn_all.items() if k in ('weight', 'gate_weight')}
    del _L1_gnn_all

    def _L2_gnn_setup():
        import jax, jax.numpy as jnp
        import numpy as np
        N = 2500
        E = 40000
        IN_F = 256
        HEADS = 4
        OUT_F = 64
        NEG_SLOPE = 0.2

        def _leaky_relu(v):
            return jnp.where(v > 0, v, NEG_SLOPE * v)
        key = jax.random.key(seed)
        k1, k2, k3, k4 = jax.random.split(key, 4)
        x = jax.random.normal(k1, (N, IN_F), dtype=jnp.float32)
        edge_index = jax.random.randint(k2, (2, E), 0, N, dtype=jnp.int64)
        W = jax.random.normal(k3, (IN_F, HEADS * OUT_F), dtype=jnp.float32) * (1.0 / np.sqrt(IN_F))
        att = jax.random.normal(k4, (1, HEADS, 2 * OUT_F), dtype=jnp.float32) * 0.1
        b = jnp.zeros((HEADS * OUT_F,), dtype=jnp.float32)
        return {'x': x, 'W': W, 'att': att, 'b': b, 'edge_index': edge_index}
    _L2_gnn_all = _L2_gnn_setup()
    _L2_gnn_in = {k: v for k, v in _L2_gnn_all.items() if k in ('W', 'att', 'b')}
    del _L2_gnn_all

    def _L3_gnn_setup():
        import jax, jax.numpy as jnp
        import numpy as np
        N_NODES = 6250
        N_EDGES = 200000
        H_SIZE = 256
        HEADS = 8
        HEAD_DIM = H_SIZE // HEADS
        NEG_SLOPE = 0.2
        key = jax.random.key(seed)
        k_x, k_e, k_w, k_as, k_ad, k_b = jax.random.split(key, 6)
        x = jax.random.normal(k_x, (N_NODES, H_SIZE), dtype=jnp.float32)
        edge_index = jax.random.randint(k_e, (2, N_EDGES), 0, N_NODES, dtype=jnp.int64)
        scale = 1.0 / np.sqrt(H_SIZE)
        W = jax.random.normal(k_w, (H_SIZE, HEADS, HEAD_DIM), dtype=jnp.float32) * scale
        att_src = jax.random.normal(k_as, (HEADS, HEAD_DIM), dtype=jnp.float32) * scale
        att_dst = jax.random.normal(k_ad, (HEADS, HEAD_DIM), dtype=jnp.float32) * scale
        bias = jnp.zeros((H_SIZE,), dtype=jnp.float32)
        return {'x': x, 'edge_index': edge_index, 'W': W, 'att_src': att_src, 'att_dst': att_dst, 'bias': bias}
    _L3_gnn_all = _L3_gnn_setup()
    _L3_gnn_in = {k: v for k, v in _L3_gnn_all.items() if k in ('W', 'att_src', 'att_dst', 'bias')}
    del _L3_gnn_all
    return {'x': x, 'src': src, 'dst': dst, 'edge_type_16': edge_type_16, 'edge_weight': edge_weight, 'edge_weight1': edge_weight1, 'L0_gnn_weight': _L0_gnn_in['weight'], 'L0_gnn_bias': _L0_gnn_in['bias'], 'L1_gnn_weight': _L1_gnn_in['weight'], 'L1_gnn_gate_weight': _L1_gnn_in['gate_weight'], 'L2_gnn_W': _L2_gnn_in['W'], 'L2_gnn_att': _L2_gnn_in['att'], 'L2_gnn_b': _L2_gnn_in['b'], 'L3_gnn_W': _L3_gnn_in['W'], 'L3_gnn_att_src': _L3_gnn_in['att_src'], 'L3_gnn_att_dst': _L3_gnn_in['att_dst'], 'L3_gnn_bias': _L3_gnn_in['bias']}

def reference(x, src, dst, edge_type_16, edge_weight, edge_weight1, L0_gnn_weight, L0_gnn_bias, L1_gnn_weight, L1_gnn_gate_weight, L2_gnn_W, L2_gnn_att, L2_gnn_b, L3_gnn_W, L3_gnn_att_src, L3_gnn_att_dst, L3_gnn_bias):
    import jax
    import jax.numpy as jnp

    def _L0_gnn_ref(x, weight, bias, rows, cols, vals):
        import jax, jax.numpy as jnp
        import numpy as np
        N_NODES = 6250
        N_EDGES = 100000
        F_IN = 256
        F_OUT = 256
        support = jnp.matmul(x, weight)
        msgs = vals[:, None] * support[cols]
        out = jax.ops.segment_sum(msgs, rows, num_segments=x.shape[0])
        return out + bias

    def _L1_gnn_ref(h, norm, weight, gate_weight, src, dst, rel_type):
        import jax, jax.numpy as jnp
        import numpy as np
        N_NODES = 6250
        N_EDGES = 100000
        NUM_RELS = 16
        FEAT = 256
        OUT = 256
        n_nodes = h.shape[0]
        all_msg = jnp.einsum('nf,rfo->rno', h, weight)
        msg = all_msg[rel_type, src] * norm
        all_gate = jnp.einsum('nf,rf->rn', h, gate_weight[..., 0])
        gate = jax.nn.sigmoid(all_gate[rel_type, src])[:, None]
        msg = msg * gate
        agg = jax.ops.segment_sum(msg, dst, num_segments=n_nodes)
        return jax.nn.relu(agg)

    def _L2_gnn_ref(x, W, att, b, edge_index):
        import jax, jax.numpy as jnp
        import numpy as np
        N = 2500
        E = 40000
        IN_F = 256
        HEADS = 4
        OUT_F = 64
        NEG_SLOPE = 0.2

        def _leaky_relu(v):
            return jnp.where(v > 0, v, NEG_SLOPE * v)
        n = x.shape[0]
        heads = att.shape[1]
        d = att.shape[2] // 2
        loops = jnp.arange(n, dtype=edge_index.dtype)
        src = jnp.concatenate([edge_index[0], loops])
        dst = jnp.concatenate([edge_index[1], loops])
        h = (x @ W).reshape(n, heads, d)
        a_src = att[0, :, :d]
        a_dst = att[0, :, d:]
        h_src = h[src]
        scores = jnp.einsum('ehd,hd->eh', _leaky_relu(h_src), a_src) + jnp.einsum('ehd,hd->eh', _leaky_relu(h[dst]), a_dst)
        w = jax.nn.softmax(scores, axis=0)
        out = jax.ops.segment_sum(h_src * w[:, :, None], dst, num_segments=n)
        return out.reshape(n, heads * d) + b

    def _L3_gnn_ref(x, edge_index, W, att_src, att_dst, bias):
        import jax, jax.numpy as jnp
        import numpy as np
        N_NODES = 6250
        N_EDGES = 200000
        H_SIZE = 256
        HEADS = 8
        HEAD_DIM = H_SIZE // HEADS
        NEG_SLOPE = 0.2
        'GATConv (concat heads) -> relu -> dropout(eval=identity).\n\n            x: [N, F]; edge_index: [2, E] with (src=row0, dst=row1) meaning message j->i.\n            '
        N = x.shape[0]
        h = jnp.einsum('nf,fhd->nhd', x, W)
        a_src = jnp.sum(h * att_src, axis=-1)
        a_dst = jnp.sum(h * att_dst, axis=-1)
        src = edge_index[0]
        dst = edge_index[1]
        e = jax.nn.leaky_relu(a_src[src] + a_dst[dst], NEG_SLOPE)
        e_max = jax.ops.segment_max(e, dst, num_segments=N)
        e_exp = jnp.exp(e - e_max[dst])
        denom = jax.ops.segment_sum(e_exp, dst, num_segments=N)
        alpha = e_exp / (denom[dst] + 1e-16)
        msg = h[src] * alpha[:, :, None]
        out = jax.ops.segment_sum(msg, dst, num_segments=N)
        out = out.reshape(N, -1) + bias
        return jax.nn.relu(out)
    edge_index = jnp.stack([src, dst])
    h = jnp.maximum(_layernorm(x, axis=-1), 0.0)
    x = x + _L0_gnn_ref(h, L0_gnn_weight, L0_gnn_bias, src, dst, edge_weight)
    h = jnp.maximum(_layernorm(x, axis=-1), 0.0)
    x = x + _L1_gnn_ref(h, edge_weight1, L1_gnn_weight, L1_gnn_gate_weight, src, dst, edge_type_16)
    h = jnp.maximum(_layernorm(x, axis=-1), 0.0)
    x = x + _L2_gnn_ref(h, L2_gnn_W, L2_gnn_att, L2_gnn_b, edge_index)
    h = jnp.maximum(_layernorm(x, axis=-1), 0.0)
    x = x + _L3_gnn_ref(h, edge_index, L3_gnn_W, L3_gnn_att_src, L3_gnn_att_dst, L3_gnn_bias)
    return x

_drawn_inputs = setup_inputs


def setup_inputs(seed=0):
    import zlib

    import numpy as np

    out = dict(_drawn_inputs(seed))
    spreads = {'L0_gnn_bias': (0.0, 0.279), 'L2_gnn_b': (0.0, 0.285), 'L3_gnn_bias': (0.0, 0.44)}
    factors = {'L2_gnn_W': 25.875, 'L2_gnn_att': 27.616, 'L3_gnn_att_src': 33.123, 'L3_gnn_att_dst': 64.0}
    for name, (base, spread) in spreads.items():
        noise = np.random.default_rng([zlib.crc32(name.encode()), seed]).standard_normal(out[name].shape)
        drawn = base * np.exp(spread * noise) if base else spread * noise
        out[name] = jnp.asarray(drawn.astype(out[name].dtype))
    for name, factor in factors.items():
        out[name] = (out[name] * factor).astype(out[name].dtype)
    return out
```

```python
from contextlib import ExitStack, contextmanager

import concourse.bass as bass
from concourse import mybir

F32 = mybir.dt.float32
I32 = mybir.dt.int32
ALU = mybir.AluOpType
ACT = mybir.ActivationFunctionType
AX = mybir.AxisListType
RMAX = bass.bass_isa.ReduceOp.max
RADD = bass.bass_isa.ReduceOp.add

P = 128
N, E, F, R = 6250, 100000, 256, 16
NT = (N + P - 1) // P
NP = NT * P
LAST = N - (NT - 1) * P
NB = 784
BP = 7
SC = 7
NSR = SC * P
G = 8
NBAT = (NB + NT - 1 + G - 1) // G
NBAT += NBAT % 2
K0 = 4
H = 8
C = F // H
W = F + 2 * H
BIG = 1e30
FIELDS = 6
LOC, SRC, IDX1, W0, W1, TAIL = range(FIELDS)


class Chain:

    def __init__(self, eng, sem, n=0):
        self.eng, self.sem, self.n = eng, sem, n

    def __call__(self, ins):
        self.n = self.n + 1
        ins.then_inc(self.sem, 1)
        self.eng.wait_ge(self.sem, self.n)


@contextmanager
def semaphores(nc, prefix):
    held = []

    def sem(name):
        held.append(nc.alloc_semaphore(name=prefix + name))
        return held[-1]

    yield sem
    nc.clear_and_free_semaphores(held)
    nc.all_engine_barrier()


def freed(eng, sem, value):
    if not isinstance(value, int) or value > 0:
        eng.wait_ge(sem, value)


def at(i):
    return slice(i, i + 1) if isinstance(i, int) else bass.ds(i, 1)


def span(start, n):
    return slice(start, start + n) if isinstance(start, int) else bass.ds(start, n)


def batches(eng, body, unroll):
    for u in range(unroll):
        body(0, u)
    with eng.Fori(1, NBAT // unroll - 1) as it:
        for u in range(unroll):
            body(it, u)
    for u in range(unroll):
        body(NBAT // unroll - 1, u)


def exists(b):
    return not isinstance(b, int) or b < NBAT


def tiles(eng, body):
    body(0, 0)
    body(0, 1)
    with eng.Fori(1, NT // 2) as it:
        body(it, 0)
        body(it, 1)
    body(NT // 2, 0)


def flat(ap):
    return ap.rearrange("a b -> (a b)")


def prepare(nc, t, ins):
    ctx = ExitStack()
    with ctx:
        def sb(name, shape, dt=F32):
            return ctx.enter_context(nc.sbuf_tensor("prep_" + name, shape, dt))

        sem = ctx.enter_context(semaphores(nc, "prep_"))

        blocks = sb("blocks", [NB // BP, BP, P], I32)
        pad_dst, pad_zero = sb("pad_dst", [1, NB * P - E], I32), sb("pad_zero", [1, NB * P - E], I32)
        lastf = sb("lastf", [NB // BP, BP])
        limit = sb("limit", [P, NT - 1])
        tile_no = sb("tile_no", [P, NT - 1])
        below = sb("below", [P, NT - 1, BP])
        count = sb("count", [P, NT - 1])
        leave = sb("leave", [P, NT - 1])
        step_no = sb("step_no", [P, SC])
        passed = sb("passed", [P, SC, NT - 1])
        tile_of, tile_base = sb("tile_of", [P, SC]), sb("tile_base", [P, SC])
        blockf, block_of = sb("blockf", [P, SC]), sb("block_of", [P, SC], I32)
        tile_i = sb("tile_i", [SC, P], I32)
        raw = [sb(f"raw{k}", [P, SC, P], I32) for k in range(3)]
        rows = [sb(f"rows{k}", [P, SC, P]) for k in range(FIELDS)]
        dstf = sb("dstf", [P, SC, P])
        here, before = sb("here", [P, NSR]), sb("before", [P, NSR])
        edge_pad = sb("edge_pad", [1, 2])
        ps = [ctx.enter_context(nc.psum_tensor(f"prep_ps{i}", [P, 1024], F32)) for i in range(2)]
        pc = ctx.enter_context(nc.psum_tensor("prep_pc", [P, 512], F32))
        names = ["copied", "padded", "pads", "blocks", "consts", "zeroed", "counted", "dve", "steps_ready",
                 "rows_in", "by_step_out", "by_step", "shifted", "flags_out", "flags", "tails", "ready_t", "tps", "turned", "taken",
                 "tile_t", "tile_c", "tile_out", "tile_in", "x_in", "xz", "pool", "flag_set"]
        s = {n: sem(n) for n in names}
        scr = [t["dst_blk"], t["src_blk"], t["type_blk"], t["w0_blk"], t["w1_blk"]]
        src_in = [ins["dst"], ins["src"], ins["edge_type_16"], ins["edge_weight"], flat(ins["edge_weight1"])]
        with nc.Block() as block:
            @block.sync
            def _(sp):
                for a, b in zip(scr, src_in):
                    sp.dma_start(flat(a)[0:E].rearrange("(a b) -> a b", a=16), b.rearrange("(a b) -> a b", a=16)).then_inc(s["copied"], 16)
                sp.wait_ge(s["pads"], 2)
                for k, a in enumerate(scr):
                    pad = pad_dst if k == 0 else pad_zero
                    pad = pad[:, :] if k < 3 else pad[:, :].bitcast(F32)
                    sp.dma_start(flat(a)[E:NB * P].unsqueeze(0), pad).then_inc(s["padded"], 16)
                sp.wait_ge(s["copied"], 5 * 16)
                sp.wait_ge(s["padded"], 5 * 16)
                sp.dma_start(blocks[:, :, :], t["dst_blk"].rearrange("(p j) e -> p j e", j=BP)).then_inc(s["blocks"], 16)
                sp.wait_ge(s["xz"], 1)
                xin = ins["x"]
                sp.dma_start(t["x"][:, 0:NT - 1, :], xin[0:(NT - 1) * P, :].rearrange("(t p) f -> p t f", p=P)).then_inc(s["x_in"], 16)
                sp.dma_start(t["x"][0:LAST, NT - 1, :], xin[(NT - 1) * P:N, :]).then_inc(s["x_in"], 16)
                sp.wait_ge(s["tile_c"], 1)
                sp.dma_start(t["tile_dram"].rearrange("(c p) -> c p", p=P), tile_i[:, :]).then_inc(s["tile_out"], 16)
                sp.wait_ge(s["tile_out"], 16)
                sp.dma_start(t["tile_row"][:, :], t["tile_dram"].unsqueeze(0)).then_inc(s["tile_in"], 16)
                sp.wait_ge(s["by_step"], 1)
                d = t["dst_step"]
                sp.dma_start(d[1:1 + NSR * P].rearrange("(c p e) -> p c e", p=P, e=P), dstf[:, :, :]).then_inc(s["by_step_out"], 16)
                sp.dma_start(d[0:1].unsqueeze(0), edge_pad[:, 0:1]).then_inc(s["by_step_out"], 16)
                for k, name in ((LOC, "loc_step"), (SRC, "src_step")):
                    sp.dma_start(t[name].rearrange("(c p) e -> p c e", p=P), rows[k][:, :, :]).then_inc(s["by_step_out"], 16)
                sp.wait_ge(s["by_step_out"], 4 * 16)
                sp.dma_start(here[:, :], d[1:1 + NSR * P].rearrange("(p j) -> p j", p=P)).then_inc(s["shifted"], 16)
                sp.dma_start(before[:, :], d[0:NSR * P].rearrange("(p j) -> p j", p=P)).then_inc(s["shifted"], 16)
                sp.wait_ge(s["flag_set"], 1)
                f = t["flag_step"]
                sp.dma_start(f[0:NSR * P].rearrange("(p j) -> p j", p=P), here[:, :]).then_inc(s["flags_out"], 16)
                sp.dma_start(f[NSR * P:NSR * P + 1].unsqueeze(0), edge_pad[:, 1:2]).then_inc(s["flags_out"], 16)
                sp.wait_ge(s["flags_out"], 2 * 16)
                sp.dma_start(rows[TAIL][:, :, :], f[1:1 + NSR * P].rearrange("(c p e) -> p c e", p=P, e=P)).then_inc(s["tails"], 16)
                sp.wait_ge(s["tails"], 16)
                sp.wait_ge(s["tile_in"], 16)
                sp.wait_ge(s["x_in"], 32)

            @block.gpsimd
            def _(pool):
                nc.gpsimd.memset(pad_dst[:, :], 8191).then_inc(s["pads"], 1)
                nc.gpsimd.memset(pad_zero[:, :], 0).then_inc(s["pads"], 1)
                nc.gpsimd.memset(edge_pad[:, 0:1], -1.0).then_inc(s["zeroed"], 1)
                nc.gpsimd.memset(edge_pad[:, 1:2], -BIG).then_inc(s["zeroed"], 1)
                nc.gpsimd.memset(t["ones"][:, :], 1.0).then_inc(s["zeroed"], 1)
                nc.gpsimd.memset(t["ident"][:, :], 0.0).then_inc(s["zeroed"], 1)
                nc.gpsimd.memset(t["valid"][:, :], 0.0).then_inc(s["zeroed"], 1)
                kw = dict(allow_small_or_imprecise_dtypes=True)
                nc.gpsimd.iota(limit[:, :], [[P, NT - 1]], base=P, channel_multiplier=0, **kw).then_inc(s["consts"], 1)
                nc.gpsimd.iota(tile_no[:, :], [[1, NT - 1]], base=0, channel_multiplier=0, **kw).then_inc(s["consts"], 1)
                nc.gpsimd.iota(step_no[:, :], [[P, SC]], base=0, channel_multiplier=1, **kw).then_inc(s["consts"], 1)
                nc.gpsimd.iota(t["col_no"][:, :], [[1, P]], base=0, channel_multiplier=0, **kw).then_inc(s["consts"], 1)
                nc.gpsimd.iota(t["row_no"][:, :], [[0, G]], base=0, channel_multiplier=1, **kw).then_inc(s["consts"], 1)
                nc.gpsimd.iota(t["spare_row"][:, :], [[0, G]], base=NP, channel_multiplier=1, **kw).then_inc(s["consts"], 1)
                pool.wait_ge(s["zeroed"], 5)
                nc.gpsimd.affine_select(out=t["ident"][:, :], in_=t["ident"][:, :], compare_op=ALU.not_equal, fill=1.0,
                                        base=0, pattern=[[-1, P]], channel_multiplier=1).then_inc(s["consts"], 1)
                nc.gpsimd.affine_select(out=t["earlier"][:, :], in_=t["ones"][:, :], compare_op=ALU.is_gt, fill=0.0,
                                        base=0, pattern=[[-1, P]], channel_multiplier=1).then_inc(s["consts"], 1)
                v = t["valid"][:, (NT - 1) * H:NT * H]
                nc.gpsimd.affine_select(out=v, in_=v, compare_op=ALU.is_ge, fill=-BIG,
                                        base=LAST - 1, pattern=[[0, H]], channel_multiplier=-1).then_inc(s["consts"], 1)
                pool.wait_ge(s["steps_ready"], 1)
                pool.wait_ge(s["padded"], 5 * 16)
                dest = [raw[0], raw[1], raw[2], rows[W0], rows[W1]]
                for c in range(SC):
                    for a, d in zip(scr, dest):
                        nc.gpsimd.indirect_dma_start(d[:, c, :], None, a[:, :], bass.IndirectOffsetOnAxis(ap=block_of[:, c:c + 1], axis=0)).then_inc(s["rows_in"], 16)
                pool.wait_ge(s["rows_in"], 5 * SC * 16)

            @block.vector
            def _(dve):
                link = Chain(dve, s["dve"])
                nc.vector.memset(t["x"][:, NT - 1, :], 0.0).then_inc(s["xz"], 1)
                dve.wait_ge(s["blocks"], 16)
                dve.wait_ge(s["consts"], 9)
                link(nc.vector.tensor_copy(lastf[:, :], blocks[:, :, P - 1]))
                nb = NB // BP
                link(nc.vector.tensor_tensor(below[0:nb], lastf[:, :].unsqueeze(1).to_broadcast([nb, NT - 1, BP]),
                                             limit[0:nb, :].unsqueeze(2).to_broadcast([nb, NT - 1, BP]), ALU.is_lt))
                link(nc.vector.reduce_sum(count[0:nb, :], below[0:nb], AX.X))
                nc.vector.tensor_copy(count[0:nb, 0:1], count[0:nb, 0:1]).then_inc(s["ready_t"], 1)
                dve.wait_ge(s["counted"], 1)
                link(nc.vector.tensor_tensor(leave[:, :], pc[:, 0:NT - 1], tile_no[:, :], ALU.add))
                link(nc.vector.tensor_tensor(passed[:, :, :], leave[:, :].unsqueeze(1).to_broadcast([P, SC, NT - 1]),
                                             step_no[:, :].unsqueeze(2).to_broadcast([P, SC, NT - 1]), ALU.is_lt))
                link(nc.vector.reduce_sum(tile_of[:, :], passed[:, :, :], AX.X))
                link(nc.vector.tensor_tensor(blockf[:, :], step_no[:, :], tile_of[:, :], ALU.subtract))
                nc.vector.tensor_scalar_min(block_of[:, :], blockf[:, :], float(NB - 1)).then_inc(s["steps_ready"], 1)
                link(nc.vector.tensor_scalar_mul(tile_base[:, :], tile_of[:, :], float(P)))
                dve.wait_ge(s["tile_t"], 1)
                nc.vector.tensor_copy(tile_i[:, :], pc[0:SC, 256:256 + P]).then_inc(s["tile_c"], 1)
                dve.wait_ge(s["rows_in"], 5 * SC * 16)
                link(nc.vector.tensor_copy(dstf[:, :, :], raw[0][:, :, :]))
                link(nc.vector.tensor_copy(rows[SRC][:, :, :], raw[1][:, :, :]))
                link(nc.vector.tensor_tensor(rows[LOC][:, :, :], dstf[:, :, :], tile_base[:, :].unsqueeze(2).to_broadcast([P, SC, P]), ALU.subtract))
                nc.vector.scalar_tensor_tensor(rows[IDX1][:, :, :], raw[2][:, :, :], float(NP), rows[SRC][:, :, :], ALU.mult, ALU.add).then_inc(s["by_step"], 1)
                dve.wait_ge(s["shifted"], 32)
                link(nc.vector.tensor_tensor(here[:, :], here[:, :], before[:, :], ALU.not_equal))
                nc.vector.tensor_scalar_mul(here[:, :], here[:, :], -BIG).then_inc(s["flag_set"], 1)
                dve.wait_ge(s["tails"], 16)
                nc.vector.tensor_scalar_mul(rows[TAIL][:, :, :], rows[TAIL][:, :, :], -1.0 / BIG).then_inc(s["ready_t"], 1)
                for k in range(FIELDS):
                    dve.wait_ge(s["turned"], k + 1)
                    v = t["edges"][:, :, k]
                    nc.vector.tensor_copy(v[:, 0:512], ps[k % 2][:, 0:512]).then_inc(s["taken"], 1)
                    nc.vector.tensor_copy(v[:, 512:NSR], ps[k % 2][:, 512:NSR]).then_inc(s["taken"], 1)

            @block.tensor
            def _(pe):
                pe.wait_ge(s["ready_t"], 1)
                nb = NB // BP
                nc.tensor.matmul(pc[:, 0:NT - 1], t["ones"][0:nb, :], count[0:nb, :], start=True, stop=True).then_inc(s["counted"], 1)
                pe.wait_ge(s["steps_ready"], 1)
                nc.tensor.transpose(pc[0:SC, 256:256 + P], tile_of[:, :], t["ident"][:, :]).then_inc(s["tile_t"], 1)
                pe.wait_ge(s["ready_t"], 2)
                for k in range(FIELDS):
                    if k >= 2:
                        pe.wait_ge(s["taken"], 2 * (k - 1))
                    for c in range(SC):
                        last = nc.tensor.transpose(ps[k % 2][:, c * P:(c + 1) * P], rows[k][:, c, :], t["ident"][:, :])
                    last.then_inc(s["turned"], 1)


def nodes(nc, t, ins, layer):
    name = f"n{layer}_"
    attention = layer >= 2
    pairs = R // 2 if layer == 1 else 0
    ctx = ExitStack()
    with ctx:
        def sb(n, shape, dt=F32):
            return ctx.enter_context(nc.sbuf_tensor(name + n, shape, dt))

        sem = ctx.enter_context(semaphores(nc, name))

        def both(n):
            return [sem(n + "0"), sem(n + "1")]

        weight = {0: "L0_gnn_weight", 1: "L1_gnn_weight", 2: "L2_gnn_W", 3: "L3_gnn_W"}[layer]
        wide = R if layer == 1 else 1
        w = sb("w", [P, 2, wide * F])
        stats = sb("stats", [P, NT, 6])
        mean, diff, var, std = (sb(n, [P, NT]) for n in ("mean", "diff", "var", "std"))
        rstd, shift = sb("rstd", [P, NT]), sb("shift", [P, NT])
        eps = sb("eps", [P, 1])
        h = sb("h", [P, 2, F])
        hT = sb("hT", [P, 2, 2, P])
        pT = [ctx.enter_context(nc.psum_tensor(name + f"pT{i}", [P, 512], F32)) for i in range(2)]
        if layer == 1:
            gate_w, gate, msg = sb("gate_w", [P, 2, R]), sb("gate", [P, 2, R]), sb("msg", [P, 2, R, F])
            pm = [ctx.enter_context(nc.psum_tensor(name + f"pm{i}", [P, 512], F32)) for i in range(4)]
            pg = [ctx.enter_context(nc.psum_tensor(name + f"pg{i}", [P, 512], F32)) for i in range(2)]
        else:
            pm = [ctx.enter_context(nc.psum_tensor(name + f"pm{i}", [P, 512], F32)) for i in range(2)]
        if layer == 0:
            zero, zero_set = sb("zero", [P, F]), sem("zero_set")
        if attention:
            heads = 4 if layer == 2 else H
            att = sb("att", [P, 2, F])
            row = sb("row", [P, 2, W])
            act_h, weighed, score = sb("act_h", [P, F]), sb("weighed", [P, 2, F]), sb("score", [P, 2, H])
        weights_in, eps_set, chain, stat_done = sem("weights_in"), sem("eps_set"), sem("chain"), sem("stat_done")
        var_ready, std_ready, scale_ready = sem("var_ready"), sem("std_ready"), sem("scale_ready")
        normed, turned, copied, prod, taken, written = (both(n) for n in ("normed", "turned", "copied", "prod", "taken", "written"))
        gate_prod, scored = both("gate_prod"), both("scored")
        filled = [sem(f"filled{i}") for i in range(4)]
        emptied = [sem(f"emptied{i}") for i in range(4)]
        n_weights = {0: 1, 1: 2, 2: 3, 3: 3}[layer]

        def pipeline(eng, first, second):
            def pair(it):
                first(it, 1)
                second(it, 0)
                first(it + 1, 0)
                second(it, 1)

            first(0, 0)
            pair(0)
            with eng.Fori(1, NT // 2) as it:
                pair(it)
            second(NT // 2, 0)

        with nc.Block() as block:
            @block.sync
            def _(sp):
                if layer == 1:
                    for c in range(2):
                        sp.dma_start(w[:, c, :].rearrange("p (r o) -> p r o", r=R),
                                     ins[weight][:, c * P:(c + 1) * P, :].rearrange("r p o -> p r o")).then_inc(weights_in, 16)
                    with nc.allow_non_contiguous_dma(reason="small gate weights"):
                        for c in range(2):
                            sp.dma_start(gate_w[:, c, :], ins["L1_gnn_gate_weight"][:, c * P:(c + 1) * P, 0].rearrange("r p -> p r")).then_inc(weights_in, 16)
                else:
                    src = ins[weight] if layer != 3 else ins[weight].rearrange("f h d -> f (h d)")
                    sp.dma_start(w[:, :, :], src.rearrange("(c p) o -> p c o", p=P)).then_inc(weights_in, 16)
                if layer == 2:
                    a = ins["L2_gnn_att"]
                    for k in range(2):
                        sp.dma_start(att[:, k, :].rearrange("p (h d) -> p h d", h=4),
                                     a[0, :, k * 64:(k + 1) * 64].partition_broadcast(P)).then_inc(weights_in, 16)
                if layer == 3:
                    for k, n in enumerate(("L3_gnn_att_src", "L3_gnn_att_dst")):
                        sp.dma_start(att[:, k, :], flat(ins[n]).partition_broadcast(P)).then_inc(weights_in, 16)

                def store(it, par):
                    i = it * 2 + par
                    if layer == 1:
                        for slot in range(4):
                            sp.wait_ge(emptied[slot], it * 4 + (2 * par + 2))
                        sp.dma_start(t["msg_table"].rearrange("(r t p) f -> t p r f", r=R, p=P)[at(i)].rearrange("a p r f -> (a p) r f"),
                                     msg[:, par, :, :]).then_inc(written[par], 16)
                    if attention:
                        sp.wait_ge(scored[par], it + 1)
                        sp.dma_start(t["head_table"].rearrange("(t p) f -> t p f", p=P)[at(i)].rearrange("a p f -> (a p) f"),
                                     row[:, par, 0:F + H]).then_inc(written[par], 16)

                if layer == 0:
                    sp.wait_ge(zero_set, 1)
                    for a in t["sums"]:
                        sp.dma_start(a.rearrange("(t p) f -> p t f", p=P), zero[:, :].unsqueeze(1).to_broadcast([P, NT + 1, F])).then_inc(written[0], 16)
                    sp.wait_ge(written[0], 16 * K0)
                if layer:
                    store(0, 0)
                    store(0, 1)
                    with sp.Fori(1, NT // 2) as it:
                        store(it, 0)
                        store(it, 1)
                    store(NT // 2, 0)
                    sp.wait_ge(written[0], 16 * (NT // 2 + 1))
                    sp.wait_ge(written[1], 16 * (NT // 2))

            @block.scalar
            def _(act):
                act.wait_ge(eps_set, 1)
                act.wait_ge(var_ready, 1)
                nc.scalar.activation(std[:, :], var[:, :], ACT.Sqrt, bias=eps[:, 0:1]).then_inc(std_ready, 1)
                act.wait_ge(scale_ready, 1)

                def norm(it, par):
                    i = it * 2 + par
                    freed(act, turned[par], it)
                    nc.scalar.activation(h[:, par, :], t["x"][:, at(i), :].rearrange("p a f -> p (a f)"), ACT.Relu,
                                         bias=shift[:, at(i)], scale=rstd[:, at(i)]).then_inc(normed[par], 1)

                def take(it, par):
                    i = it * 2 + par
                    if layer == 1:
                        act.wait_ge(gate_prod[par], it + 1)
                        freed(act, written[par], it * 16)
                        nc.scalar.activation(gate[:, par, :], pg[par][:, 0:R], ACT.Sigmoid).then_inc(taken[par], 1)
                        act.wait_ge(taken[par], it + 1)
                        for p in range(1, pairs, 2):
                            slot = p % 4
                            act.wait_ge(filled[slot], it * 4 + (2 * par + p // 4 + 1))
                            for r in range(2):
                                last = nc.scalar.activation(msg[:, par, 2 * p + r, :], pm[slot][:, r * F:(r + 1) * F], ACT.Copy,
                                                            scale=gate[:, par, 2 * p + r:2 * p + r + 1])
                            last.then_inc(emptied[slot], 1)
                        return
                    act.wait_ge(prod[par], it + 1)
                    if layer == 0:
                        out = t["agg"][:, at(i), 0:F].rearrange("p a f -> p (a f)")
                    else:
                        freed(act, written[par], it * 16)
                        out = row[:, par, 0:F]
                    nc.scalar.activation(out, pm[par][:, 0:F], ACT.Copy).then_inc(taken[par], 1)

                pipeline(act, norm, take)

            @block.vector
            def _(dve):
                link = Chain(dve, chain)
                nc.vector.memset(eps[:, :], 1e-5).then_inc(eps_set, 1)
                if layer == 0:
                    nc.vector.memset(zero[:, :], 0.0).then_inc(zero_set, 1)
                with dve.Fori(0, NT) as i:
                    nc.vector.bn_stats(stats[:, at(i), :].rearrange("p a s -> p (a s)"),
                                       t["x"][:, at(i), :].rearrange("p a f -> p (a f)")).then_inc(stat_done, 1)
                dve.wait_ge(stat_done, NT)
                link(nc.vector.tensor_tensor(mean[:, :], stats[:, :, 1], stats[:, :, 4], ALU.add))
                link(nc.vector.tensor_tensor(diff[:, :], stats[:, :, 1], stats[:, :, 4], ALU.subtract))
                link(nc.vector.tensor_tensor(var[:, :], stats[:, :, 2], stats[:, :, 5], ALU.add))
                link(nc.vector.tensor_tensor(diff[:, :], diff[:, :], diff[:, :], ALU.mult))
                link(nc.vector.tensor_scalar_mul(diff[:, :], diff[:, :], 0.25))
                nc.vector.scalar_tensor_tensor(var[:, :], var[:, :], 1.0 / F, diff[:, :], ALU.mult, ALU.add).then_inc(var_ready, 1)
                dve.wait_ge(std_ready, 1)
                link(nc.vector.reciprocal(rstd[:, :], std[:, :]))
                nc.vector.scalar_tensor_tensor(shift[:, :], mean[:, :], -0.5, rstd[:, :], ALU.mult, ALU.mult).then_inc(scale_ready, 1)
                dve.wait_ge(weights_in, 16 * (4 if layer == 1 else n_weights))

                def copy(it, par):
                    if layer == 1:
                        freed(dve, written[par], it * 16)
                    else:
                        freed(dve, prod[par], it)
                    dve.wait_ge(turned[par], it + 1)
                    nc.vector.tensor_copy(hT[:, par, :, :].rearrange("p c n -> p (c n)"), pT[par][:, 0:F]).then_inc(copied[par], 1)

                def finish(it, par):
                    i = it * 2 + par
                    if layer == 1:
                        dve.wait_ge(taken[par], it + 1)
                        for p in range(0, pairs, 2):
                            slot = p % 4
                            dve.wait_ge(filled[slot], it * 4 + (2 * par + p // 4 + 1))
                            nc.vector.tensor_tensor(msg[:, par, 2 * p:2 * p + 2, :], pm[slot][:, :].rearrange("p (r f) -> p r f", r=2),
                                                    gate[:, par, 2 * p:2 * p + 2].unsqueeze(2).to_broadcast([P, 2, F]), ALU.mult).then_inc(emptied[slot], 1)
                    if attention:
                        dve.wait_ge(taken[par], it + 1)
                        feats = row[:, par, 0:F]
                        base = 6 if layer == 2 else 4
                        k0 = (it * 2 + par) * base + n_links
                        k = 0

                        def step(ins_):
                            nonlocal k
                            k += 1
                            ins_.then_inc(chain, 1)
                            dve.wait_ge(chain, k0 + k)

                        if layer == 2:
                            step(nc.vector.scalar_tensor_tensor(act_h[:, :], feats, 0.2, feats, ALU.mult, ALU.max))
                            feats = act_h[:, :]
                        step(nc.vector.tensor_tensor(weighed[:, 0, :], feats, att[:, 0, :], ALU.mult))
                        step(nc.vector.tensor_tensor(weighed[:, 1, :], feats, att[:, 1, :], ALU.mult))
                        step(nc.vector.reduce_sum(score[:, :, 0:heads], weighed[:, :, :].rearrange("p k (h d) -> p k h d", h=heads), AX.X))
                        rep = H // heads
                        dup = [score[:, k_, 0:heads].unsqueeze(2).to_broadcast([P, heads, rep]) for k_ in range(2)]
                        here = at(i)
                        step(nc.vector.tensor_copy(t["dst_score"][:, here, :].rearrange("p a (h r) -> p (a h) r", r=rep), dup[1]))
                        if layer == 2:
                            step(nc.vector.tensor_copy(t["src_score"][:, here, :].rearrange("p a (h r) -> p (a h) r", r=rep), dup[0]))
                        nc.vector.tensor_copy(row[:, par, F:F + H].rearrange("p (h r) -> p h r", r=rep), dup[0]).then_inc(scored[par], 1)

                n_links = link.n
                pipeline(dve, copy, finish)

            @block.tensor
            def _(pe):
                pe.wait_ge(weights_in, 16 * (4 if layer == 1 else n_weights))

                def turn(it, par):
                    pe.wait_ge(normed[par], it + 1)
                    freed(pe, copied[par], it)
                    for c in range(2):
                        last = nc.tensor.transpose(pT[par][:, c * P:(c + 1) * P], h[:, par, c * P:(c + 1) * P], t["ident"][:, :])
                    last.then_inc(turned[par], 1)

                def multiply(it, par):
                    pe.wait_ge(copied[par], it + 1)
                    if layer != 1:
                        freed(pe, taken[par], it)
                        for c in range(2):
                            last = nc.tensor.matmul(pm[par][:, 0:F], hT[:, par, c, :], w[:, c, :], start=c == 0, stop=c == 1)
                        last.then_inc(prod[par], 1)
                        return
                    freed(pe, taken[par], it)
                    for c in range(2):
                        last = nc.tensor.matmul(pg[par][:, 0:R], hT[:, par, c, :], gate_w[:, c, :], start=c == 0, stop=c == 1)
                    last.then_inc(gate_prod[par], 1)
                    for p in range(pairs):
                        slot = p % 4
                        freed(pe, emptied[slot], it * 4 + (2 * par + p // 4))
                        for c in range(2):
                            last = nc.tensor.matmul(pm[slot][:, :], hT[:, par, c, :], w[:, c, p * 2 * F:(p + 1) * 2 * F], start=c == 0, stop=c == 1)
                        last.then_inc(filled[slot], 1)

                pipeline(pe, turn, multiply)


def scatter_edges(nc, t, ins):
    name = "e0_"
    ctx = ExitStack()
    with ctx:
        def sb(n, shape, dt=F32):
            return ctx.enter_context(nc.sbuf_tensor(name + n, shape, dt))

        sem = ctx.enter_context(semaphores(nc, name))

        def both(n):
            return [sem(n + "0"), sem(n + "1")]

        srow = sb("srow", [P, 2, G, P])
        stage = sb("stage", [P, 2, G, FIELDS])
        S, M = sb("S", [P, 2, G, P]), sb("M", [P, 2, G, P])
        SM = sb("SM", [P, 2, G, P])
        unused, count, off = sb("unused", [P, G, P]), sb("count", [P, G]), sb("off", [P, G])
        index = sb("index", [P, 2, G], I32)
        sums = sb("sums", [P, 2, G, F])
        part = sb("part", [P, 2, K0, F])
        total = sb("total", [P, 2, F])
        bias = sb("bias", [P, F])
        p_sm = [ctx.enter_context(nc.psum_tensor(name + f"psm{i}", [P, 4, P], F32)) for i in range(2)]
        p_sum = [ctx.enter_context(nc.psum_tensor(name + f"psum{i}", [P, 2, F], F32)) for i in range(4)]
        rows_in, parts_in = both("rows_in"), both("parts_in")
        added = [sem(f"added{k}") for k in range(K0)]
        chain, pace, bias_in, made, indexed, part_used = (sem(n) for n in ("chain", "pace", "bias_in", "made", "indexed", "part_used"))
        sm_done, sm_copied, sum_done, sum_copied = (sem(n) for n in ("sm_done", "sm_copied", "sum_done", "sum_copied"))
        LINKS = 4
        with nc.Block() as block:
            @block.sync
            def _(sp):
                sp.dma_start(bias[:, :], ins["L0_gnn_bias"].partition_broadcast(P)).then_inc(bias_in, 16)

                def load(it, u):
                    b = it * 2 + u
                    freed(sp, made, b - 1)
                    sp.dma_start(srow[:, u, :, :].rearrange("p g e -> p (g e)"),
                                 flat(t["src_step"][span(b * G, G), :]).partition_broadcast(P)).then_inc(rows_in[u], 16)

                batches(sp, load, 2)
                for k in range(K0):
                    sp.wait_ge(added[k], 16 * NBAT * (G // K0))

                def parts(it, u):
                    i = it * 2 + u
                    freed(sp, part_used, i - 1)
                    for k in range(K0):
                        sp.dma_start(part[:, u, k, :], t["sums"][k][span(i * P, P), :]).then_inc(parts_in[u], 16)

                tiles(sp, parts)

            @block.vector
            def _(dve):
                def batch(it, u):
                    b = it * 2 + u
                    link = Chain(dve, chain, b * LINKS)
                    link(nc.vector.tensor_copy(stage[:, u, :, :], t["edges"][:, span(b * G, G), :]))
                    freed(dve, sm_done, (b - 1) * 2)
                    dve.wait_ge(rows_in[u], it * 16 + 16)
                    nc.vector.tensor_tensor(S[:, u, :, :], stage[:, u, :, LOC].unsqueeze(2).to_broadcast([P, G, P]),
                                            t["col_no"][:, :].unsqueeze(1).to_broadcast([P, G, P]), ALU.is_equal)
                    for g in range(G):
                        nc.vector.tensor_scalar(M[:, u, g, :], srow[:, u, g, :], stage[:, u, g, SRC:SRC + 1],
                                                stage[:, u, g, W0:W0 + 1], ALU.is_equal, ALU.mult)
                    for g in range(G):
                        last = nc.vector.scalar_tensor_tensor(unused[:, g, :], srow[:, u, g, :], stage[:, u, g, SRC:SRC + 1],
                                                              t["earlier"][:, :], ALU.is_equal, ALU.mult, accum_out=count[:, g:g + 1])
                    last.then_inc(made, 1)
                    dve.wait_ge(made, b + 1)
                    link(nc.vector.tensor_tensor(off[:, :], t["spare_row"][:, :], stage[:, u, :, SRC], ALU.subtract))
                    link(nc.vector.tensor_scalar(count[:, :], count[:, :], 0.0, None, ALU.is_gt))
                    link(nc.vector.tensor_tensor(off[:, :], off[:, :], count[:, :], ALU.mult))
                    for k in range(K0):
                        freed(dve, added[k], (b - 1) * 16 * (G // K0))
                    nc.vector.tensor_tensor(index[:, u, :], off[:, :], stage[:, u, :, SRC], ALU.add).then_inc(indexed, 1)

                batches(dve, batch, 2)
                link = Chain(dve, chain, NBAT * LINKS)
                dve.wait_ge(bias_in, 16)
                link(nc.vector.tensor_tensor(t["x"][:, :, :], t["x"][:, :, :], bias[:, :].unsqueeze(1).to_broadcast([P, NT, F]), ALU.add))

                def add(it, u):
                    i = it * 2 + u
                    link = Chain(dve, chain, i * 2 + (NBAT * LINKS + 1))
                    dve.wait_ge(parts_in[u], it * 16 * K0 + 16 * K0)
                    link(nc.vector.tensor_tensor(part[:, u, 0:2, :], part[:, u, 0:2, :], part[:, u, 2:4, :], ALU.add))
                    link(nc.vector.tensor_tensor(total[:, u, :], part[:, u, 0, :], part[:, u, 1, :], ALU.add))
                    row = t["x"][:, at(i), :].rearrange("p a f -> p (a f)")
                    nc.vector.tensor_tensor(row, row, total[:, u, :], ALU.add).then_inc(part_used, 1)

                tiles(dve, add)

            @block.tensor
            def _(pe):
                def batch(it, u):
                    b = it * 2 + u
                    pe.wait_ge(made, b + 1)
                    for half in range(2):
                        freed(pe, sm_copied, b * 2 + (half - 1))
                        for g in range(4 * half, 4 * half + 4):
                            last = nc.tensor.matmul(p_sm[half][:, g % 4, :], S[:, u, g, :], M[:, u, g, :], start=True, stop=True)
                        last.then_inc(sm_done, 1)
                    for pair in range(4):
                        pe.wait_ge(sm_copied, b * 2 + (pair // 2 + 1))
                        freed(pe, sum_copied, b * 4 + (pair - 3))
                        for g in range(2 * pair, 2 * pair + 2):
                            tile = pe.value_load(t["tile_row"][0:1, at(b * G + g)], min_val=0, max_val=NT - 1)
                            last = nc.tensor.matmul(p_sum[pair][:, g % 2, :], SM[:, u, g, :],
                                                    t["agg"][:, bass.ds(tile, 1), 0:F].rearrange("p a f -> p (a f)"), start=True, stop=True)
                        last.then_inc(sum_done, 1)

                batches(pe, batch, 2)

            @block.scalar
            def _(act):
                def batch(it, u):
                    b = it * 2 + u
                    for half in range(2):
                        act.wait_ge(sm_done, b * 2 + (half + 1))
                        freed(act, sum_done, (b - 1) * 4)
                        nc.scalar.copy(SM[:, u, 4 * half:4 * half + 4, :], p_sm[half][:, :, :]).then_inc(sm_copied, 1)
                    for pair in range(4):
                        act.wait_ge(sum_done, b * 4 + (pair + 1))
                        for k in ((2 * pair) % K0, (2 * pair + 1) % K0):
                            freed(act, added[k], (b * 2 + (pair // 2 - 3)) * 16)
                        nc.scalar.copy(sums[:, u, 2 * pair:2 * pair + 2, :], p_sum[pair][:, :, :]).then_inc(sum_copied, 1)

                batches(act, batch, 2)

            @block.gpsimd
            def _(pool):
                def batch(it, u):
                    b = it * 2 + u
                    pool.wait_ge(indexed, b + 1)
                    for g in range(G):
                        k = g % K0
                        pool.wait_ge(sum_copied, b * 4 + (g // 2 + 1))
                        freed(pool, added[k], (b * 2 + g // K0) * 16)
                        pool.sem_inc(pace, 1)
                        nc.gpsimd.indirect_dma_start(t["sums"][k][:, :], bass.IndirectOffsetOnAxis(ap=index[:, u, g:g + 1], axis=0),
                                                     sums[:, u, g, :], None, compute_op=ALU.add).then_inc(added[k], 16)

                batches(pool, batch, 2)
                for k in range(K0):
                    pool.wait_ge(added[k], 16 * NBAT * (G // K0))


def relation_edges(nc, t, ins):
    name = "e1_"
    ctx = ExitStack()
    with ctx:
        def sb(n, shape, dt=F32):
            return ctx.enter_context(nc.sbuf_tensor(name + n, shape, dt))

        sem = ctx.enter_context(semaphores(nc, name))

        U = 4
        stage = sb("stage", [P, 2, G, FIELDS])
        S = sb("S", [P, 2, G, P])
        index = sb("index", [P, U, G], I32)
        rows = sb("rows", [P, U, G, F])
        p_sum = [ctx.enter_context(nc.psum_tensor(name + f"psum{i}", [P, 2, F], F32)) for i in range(4)]
        gathered = [[sem(f"gathered{u}_{g}") for g in range(G)] for u in range(U)]
        staged, pace, indexed, made, sum_done, zeroed, added = (
            sem(n) for n in ("staged", "pace", "indexed", "made", "sum_done", "zeroed", "added"))
        with nc.Block() as block:
            @block.gpsimd
            def _(pool):
                def batch(it, u):
                    b = it * U + u
                    pool.wait_ge(indexed, b + 1)
                    freed(pool, sum_done, (b - (U - 1)) * 4)
                    pool.sem_inc(pace, 1)
                    for g in range(G):
                        nc.gpsimd.indirect_dma_start(rows[:, u, g, :], None, t["msg_table"][:, :],
                                                     bass.IndirectOffsetOnAxis(ap=index[:, u, g:g + 1], axis=0)).then_inc(gathered[u][g], 16)

                batches(pool, batch, U)

            @block.vector
            def _(dve):
                nc.vector.memset(t["agg"][:, :, :], 0.0).then_inc(zeroed, 1)

                def look_up(it, u):
                    for g in range(G):
                        freed(dve, gathered[u][g], it * 16)
                    nc.vector.tensor_copy(index[:, u, :], t["edges"][:, span((it * U + u) * G, G), IDX1]).then_inc(indexed, 1)

                def batch(it, u):
                    b = it * U + u
                    if exists(b + 2):
                        look_up(it + (u + 2) // U, (u + 2) % U)
                    nc.vector.tensor_copy(stage[:, u % 2, :, :], t["edges"][:, span(b * G, G), :]).then_inc(staged, 1)
                    dve.wait_ge(staged, b + 1)
                    freed(dve, sum_done, (b - 1) * 4)
                    for g in range(G):
                        last = nc.vector.tensor_scalar(S[:, u % 2, g, :], t["col_no"][:, :], stage[:, u % 2, g, LOC:LOC + 1],
                                                       stage[:, u % 2, g, W1:W1 + 1], ALU.is_equal, ALU.mult)
                    last.then_inc(made, 1)
                    for g in range(G):
                        if g % 2 == 0:
                            dve.wait_ge(sum_done, b * 4 + (g // 2 + 1))
                        tile = dve.value_load(t["tile_row"][0:1, at(b * G + g)], min_val=0, max_val=NT - 1)
                        row = t["agg"][:, bass.ds(tile, 1), 0:F].rearrange("p a f -> p (a f)")
                        nc.vector.tensor_tensor(row, row, p_sum[g // 2][:, g % 2, :], ALU.add).then_inc(added, 1)
                        dve.wait_ge(added, b * G + (g + 1))

                dve.wait_ge(zeroed, 1)
                look_up(0, 0)
                look_up(0, 1)
                batches(dve, batch, U)
                nc.vector.scalar_tensor_tensor(t["x"][:, :, :], t["agg"][:, :, 0:F], 0.0, t["x"][:, :, :], ALU.max, ALU.add).then_inc(zeroed, 1)
                dve.wait_ge(zeroed, 2)

            @block.tensor
            def _(pe):
                def batch(it, u):
                    b = it * U + u
                    pe.wait_ge(made, b + 1)
                    for g in range(G):
                        if g % 2 == 0:
                            freed(pe, added, (b - 1) * G + (g + 2))
                        pe.wait_ge(gathered[u][g], it * 16 + 16)
                        last = nc.tensor.matmul(p_sum[g // 2][:, g % 2, :], S[:, u % 2, g, :], rows[:, u, g, :], start=True, stop=True)
                        if g % 2:
                            last.then_inc(sum_done, 1)

                batches(pe, batch, U)


def attention_edges(nc, t, ins, layer):
    name = f"a{layer}_"
    leaky = layer == 3
    ctx = ExitStack()
    with ctx:
        def sb(n, shape, dt=F32):
            return ctx.enter_context(nc.sbuf_tensor(name + n, shape, dt))

        sem = ctx.enter_context(semaphores(nc, name))

        U = 4
        GP = G * P
        V = slice(F, F + H)
        stage = sb("stage", [P, 2, G, FIELDS])
        S, ST = sb("S", [P, 2, G, P]), sb("ST", [P, GP])
        index = sb("index", [P, U, G], I32)
        rows = sb("rows", [P, U, G, W])
        loc_row = sb("loc_row", [P, 2, GP])
        new_dst = sb("new_dst", [H, GP + 1])
        up, top = sb("up", [H, GP]), sb("top", [H, GP])
        carry = sb("carry", [H, 2])
        a = sb("a", [P, G * H])
        z = sb("z", [P, 2, (G + 1) * H])
        growth = sb("growth", [1, H])
        scale = sb("scale", [P, H])
        p_turn = ctx.enter_context(nc.psum_tensor(name + "pturn", [H, GP], F32))
        bank_a = ctx.enter_context(nc.psum_tensor(name + "bank_a", [P, 512], F32))
        bank_b = ctx.enter_context(nc.psum_tensor(name + "bank_b", [P, 512], F32))
        p_a, p_scale = bank_a[:, 0:G * H], bank_a[:, G * H:G * H + H]
        p_top, p_old = bank_b[:, 0:G * H], bank_b[0:1, G * H:G * H + H]
        p_sum = [ctx.enter_context(nc.psum_tensor(name + f"psum{i}", [P, 512], F32)) for i in range(4)]
        gathered = [sem(f"gathered{u}") for u in range(U)]
        loc_in, new_in = [sem("loc_in0"), sem("loc_in1")], [sem("new_in0"), sem("new_in1")]
        names = ["rows_set", "pace", "turn_pace", "indexed", "staged", "st_made", "made", "turned", "a_done", "scanned_up", "carried", "scanned", "top_done",
                 "c3", "z_ready", "exp_done", "weighed", "scale_done", "sum_done", "c5", "added", "zeroed"]
        s = {n: sem(n) for n in names}
        C3 = 3 if leaky else 1
        with nc.Block() as block:
            @block.sync
            def _(sp):
                def load(it, u):
                    b = it * U + u
                    freed(sp, s["st_made"], b - 1)
                    sp.dma_start(loc_row[:, u % 2, :], flat(t["loc_step"][span(b * G, G), :]).partition_broadcast(P)).then_inc(loc_in[u % 2], 16)
                    freed(sp, s["scanned"], b)
                    sp.dma_start(new_dst[:, :], t["flag_step"][span(b * GP, GP + 1)].partition_broadcast(H)).then_inc(new_in[u % 2], 16)

                batches(sp, load, U)

            @block.gpsimd
            def _(pool):
                nc.gpsimd.memset(rows[:, :, :, F:W], 0.0).then_inc(s["rows_set"], 1)
                pool.wait_ge(s["rows_set"], 1)

                def batch(it, u):
                    b = it * U + u
                    pool.wait_ge(s["indexed"], b + 1)
                    freed(pool, s["sum_done"], (b - (U - 1)) * G)
                    pool.sem_inc(s["pace"], 1)
                    for g in range(G):
                        nc.gpsimd.indirect_dma_start(rows[:, u, g, 0:F + H], None, t["head_table"][:, :],
                                                     bass.IndirectOffsetOnAxis(ap=index[:, u, g:g + 1], axis=0)).then_inc(gathered[u], 16)

                batches(pool, batch, U)

            @block.vector
            def _(dve):
                nc.vector.memset(t["agg"][:, :, :], 0.0).then_inc(s["zeroed"], 1)
                nc.vector.memset(carry[:, :], -BIG).then_inc(s["zeroed"], 1)
                nc.vector.memset(z[:, :, :], 0.0).then_inc(s["zeroed"], 1)
                if not leaky:
                    nc.vector.memset(a[:, :], 0.0).then_inc(s["zeroed"], 1)

                def look_up(it, u):
                    freed(dve, gathered[u], it * 16 * G)
                    nc.vector.tensor_copy(index[:, u, :], t["edges"][:, span((it * U + u) * G, G), SRC]).then_inc(s["indexed"], 1)

                def one_hots(it, u):
                    b = it * U + u
                    nc.vector.tensor_copy(stage[:, u % 2, :, :], t["edges"][:, span(b * G, G), :]).then_inc(s["staged"], 1)
                    dve.wait_ge(s["staged"], b + 1)
                    freed(dve, s["sum_done"], (b - 1) * G)
                    for g in range(G):
                        last = nc.vector.tensor_scalar(S[:, u % 2, g, :], t["col_no"][:, :], stage[:, u % 2, g, LOC:LOC + 1], None, ALU.is_equal)
                    last.then_inc(s["made"], 1)
                    dve.wait_ge(loc_in[u % 2], it * (16 * U // 2) + 16 * (u // 2 + 1))
                    if leaky:
                        freed(dve, s["a_done"], b)
                    nc.vector.tensor_scalar(ST[:, :], loc_row[:, u % 2, :], t["row_no"][:, 0:1], None, ALU.is_equal).then_inc(s["st_made"], 1)
                    dve.wait_ge(s["st_made"], b + 1)

                def scans(it, u):
                    b = it * U + u
                    dve.wait_ge(s["turned"], b + 1)
                    dve.wait_ge(new_in[u % 2], it * (16 * U // 2) + 16 * (u // 2 + 1))
                    freed(dve, s["top_done"], b)
                    nc.vector.tensor_tensor_scan(up[:, :], new_dst[:, 0:GP], p_turn[:, :], carry[:, (u + 1) % 2:(u + 1) % 2 + 1],
                                                 ALU.add, ALU.max).then_inc(s["scanned_up"], 1)
                    dve.wait_ge(s["scanned_up"], b + 1)
                    nc.vector.tensor_copy(carry[:, u % 2:u % 2 + 1], up[:, GP - 1:GP]).then_inc(s["carried"], 1)
                    nc.vector.tensor_tensor_scan(top[:, ::-1], new_dst[:, 1:GP + 1][:, ::-1], up[:, ::-1], -BIG,
                                                 ALU.add, ALU.max).then_inc(s["scanned"], 1)
                    dve.wait_ge(s["carried"], b + 1)

                def differences(it, u):
                    b = it * U + u
                    link = Chain(dve, s["c3"], b * C3)
                    dve.wait_ge(s["top_done"], b + 1)
                    v = rows[:, u, :, V]
                    as_rows = [x.rearrange("p (g h) -> p g h", h=H) for x in (z[:, 0, 0:G * H], z[:, 1, 0:G * H], p_top, a[:, :])]
                    nc.vector.tensor_tensor(rows[:, u, :, F + H:W], as_rows[2],
                                            stage[:, u % 2, :, TAIL].unsqueeze(2).to_broadcast([P, G, H]), ALU.mult)
                    if not leaky:
                        link(nc.vector.tensor_copy(a[0:1, 0:H], p_top[0:1, 0:H]))
                        nc.vector.scalar_tensor_tensor(z[0:1, 0, G * H:], a[0:1, 0:H], 1.0, p_old, ALU.mult, ALU.min)
                        nc.vector.tensor_tensor(as_rows[0], v, as_rows[2], ALU.subtract).then_inc(s["z_ready"], 1)
                        dve.wait_ge(s["z_ready"], b * 2 + 1)
                        nc.vector.tensor_tensor(z[0:1, 0, G * H:], z[0:1, 0, G * H:], a[0:1, 0:H], ALU.subtract).then_inc(s["z_ready"], 1)
                        return
                    link(nc.vector.tensor_copy(a[:, :], p_a))
                    nc.vector.tensor_tensor(z[:, 1, 0:G * H], p_top, a[:, :], ALU.add)
                    nc.vector.tensor_tensor(z[0:1, 1, G * H:], p_top[0:1, 0:H], a[0:1, 0:H], ALU.add)
                    nc.vector.tensor_tensor(z[0:1, 0, G * H:], p_old, a[0:1, 0:H], ALU.add)
                    link(nc.vector.tensor_tensor(as_rows[0], v, as_rows[3], ALU.add))
                    link(nc.vector.scalar_tensor_tensor(z[:, :, :], z[:, :, :], 0.2, z[:, :, :], ALU.mult, ALU.max))
                    nc.vector.tensor_tensor(z[0:1, 0, G * H:], z[0:1, 0, G * H:], z[0:1, 1, G * H:], ALU.min).then_inc(s["z_ready"], 1)
                    dve.wait_ge(s["z_ready"], b * 2 + 1)
                    nc.vector.tensor_tensor(z[:, 0, :], z[:, 0, :], z[:, 1, :], ALU.subtract).then_inc(s["z_ready"], 1)

                def weigh(it, u):
                    b = it * U + u
                    dve.wait_ge(s["exp_done"], b * 2 + 2)
                    nc.vector.tensor_scalar_add(growth[:, :], z[0:1, 1, G * H:], -1.0)
                    feats = rows[:, u, :, 0:F].rearrange("p g (h c) -> p g h c", h=H)
                    nc.vector.tensor_tensor(feats, feats, rows[:, u, :, V].unsqueeze(3).to_broadcast([P, G, H, C]), ALU.mult).then_inc(s["weighed"], 1)

                def add(it, u):
                    b = it * U + u
                    link = Chain(dve, s["c5"], b * 2)
                    dve.wait_ge(s["scale_done"], b + 1)
                    link(nc.vector.tensor_scalar_add(scale[:, :], p_scale, 1.0))
                    for g in range(G):
                        tile = dve.value_load(t["tile_row"][0:1, at(b * G + g)], min_val=0, max_val=NT - 1)
                        here = t["agg"][:, bass.ds(tile, 1), :].rearrange("p a f -> p (a f)")
                        if g == 0:
                            old = here[:, 0:F].rearrange("p (h c) -> p h c", h=H)
                            nc.vector.tensor_tensor(old, old, scale[:, :].unsqueeze(2).to_broadcast([P, H, C]), ALU.mult)
                            link(nc.vector.tensor_tensor(here[:, V], here[:, V], scale[:, :], ALU.mult))
                        dve.wait_ge(s["sum_done"], b * G + (g + 1))
                        nc.vector.tensor_tensor(here, here, p_sum[g % 4][:, 0:W], ALU.add).then_inc(s["added"], 1)
                        dve.wait_ge(s["added"], b * G + (g + 1))

                def ahead(it, u, by):
                    return it + (u + by) // U, (u + by) % U

                def batch(it, u):
                    b = it * U + u
                    if exists(b + 3):
                        look_up(*ahead(it, u, 3))
                    weigh(it, u)
                    if exists(b + 1):
                        scans(*ahead(it, u, 1))
                    add(it, u)
                    if exists(b + 2):
                        one_hots(*ahead(it, u, 2))
                    if exists(b + 1):
                        differences(*ahead(it, u, 1))

                dve.wait_ge(s["zeroed"], 3 if leaky else 4)
                for u in range(3):
                    look_up(0, u)
                one_hots(0, 0)
                scans(0, 0)
                one_hots(0, 1)
                differences(0, 0)
                batches(dve, batch, U)

            @block.scalar
            def _(act):
                def batch(it, u):
                    b = it * U + u
                    act.wait_ge(s["z_ready"], b * 2 + 2)
                    nc.scalar.activation(rows[:, u, :, V], z[:, 0, 0:G * H].rearrange("p (g h) -> p g h", h=H), ACT.Exp).then_inc(s["exp_done"], 1)
                    nc.scalar.activation(z[0:1, 1, G * H:], z[0:1, 0, G * H:], ACT.Exp).then_inc(s["exp_done"], 1)

                batches(act, batch, U)

            @block.tensor
            def _(pe):
                def scores(it, u):
                    b = it * U + u
                    pe.wait_ge(gathered[u], it * 16 * G + 16 * G)
                    freed(pe, s["scanned_up"], b)
                    for g in range(G):
                        last = nc.tensor.transpose(p_turn[:, g * P:(g + 1) * P], rows[:, u, g, V], t["ident"][:, :])
                    last.then_inc(s["turned"], 1)
                    if leaky:
                        pe.wait_ge(s["st_made"], b + 1)
                        if not isinstance(b, int) or b > 0:
                            pe.wait_ge(s["c3"], (b - 1) * C3 + 1)
                        for g in range(G):
                            tile = pe.value_load(t["tile_row"][0:1, at(b * G + g)], min_val=0, max_val=NT - 1)
                            last = nc.tensor.matmul(p_a[:, g * H:(g + 1) * H], ST[:, g * P:(g + 1) * P],
                                                    t["dst_score"][:, bass.ds(tile, 1), :].rearrange("p a h -> p (a h)"), start=True, stop=True)
                        last.then_inc(s["a_done"], 1)

                def maxima(it, u):
                    b = it * U + u
                    pe.wait_ge(s["scanned"], b + 1)
                    freed(pe, s["z_ready"], b * 2)
                    pe.sem_inc(s["turn_pace"], 1)
                    for g in range(G):
                        nc.tensor.transpose(p_top[:, g * H:(g + 1) * H], top[:, g * P:(g + 1) * P], t["ident"][0:H, 0:H])
                    nc.tensor.transpose(p_old, carry[:, (u + 1) % 2:(u + 1) % 2 + 1], t["ident"][0:H, 0:H]).then_inc(s["top_done"], 1)

                def sums(it, u):
                    b = it * U + u
                    pe.wait_ge(s["made"], b + 1)
                    pe.wait_ge(s["weighed"], b + 1)
                    nc.tensor.matmul(p_scale, S[0:1, u % 2, 0, :], growth[:, :], start=True, stop=True).then_inc(s["scale_done"], 1)
                    for g in range(G):
                        freed(pe, s["added"], b * G + (g - 3))
                        nc.tensor.matmul(p_sum[g % 4][:, 0:W], S[:, u % 2, g, :], rows[:, u, g, :], start=True, stop=True).then_inc(s["sum_done"], 1)

                def batch(it, u):
                    b = it * U + u
                    sums(it, u)
                    if exists(b + 1):
                        maxima(it + (u + 1) // U, (u + 1) % U)
                    if exists(b + 2):
                        scores(it + (u + 2) // U, (u + 2) % U)

                scores(0, 0)
                maxima(0, 0)
                scores(0, 1)
                batches(pe, batch, U)


def finish_global(nc, t, ins):
    ctx = ExitStack()
    with ctx:
        def sb(n, shape, dt=F32):
            return ctx.enter_context(nc.sbuf_tensor("f2_" + n, shape, dt))

        sem = ctx.enter_context(semaphores(nc, "f2_"))

        h = sb("h", [P, NT, F])
        bias = sb("bias", [P, F])
        m, own, q, top, low = (sb(n, [P, NT, H]) for n in ("m", "own", "q", "top", "low"))
        best, best_all, part, inv = (sb(n, [P, H]) for n in ("best", "best_all", "part", "inv"))
        pz = ctx.enter_context(nc.psum_tensor("f2_pz", [P, 512], F32))
        h_in, bias_in, chain, best_ready, all_ready, exp_in, exp_out, part_ready, z_ready = (
            sem(n) for n in ("h_in", "bias_in", "chain", "best_ready", "all_ready", "exp_in", "exp_out", "part_ready", "z_ready"))
        everywhere = [P, NT, H]
        with nc.Block() as block:
            @block.sync
            def _(sp):
                sp.dma_start(h[:, :, :], t["head_table"].rearrange("(t p) f -> p t f", p=P)[:, :, 0:F]).then_inc(h_in, 16)
                sp.dma_start(bias[:, :], ins["L2_gnn_b"].partition_broadcast(P)).then_inc(bias_in, 16)

            @block.vector
            def _(dve):
                link = Chain(dve, chain)
                agg, x = t["agg"], t["x"]
                den, tail = agg[:, :, F:F + H], agg[:, :, F + H:W]
                link(nc.vector.tensor_scalar(m[:, :, :], den, 0.0, -BIG, ALU.is_equal, ALU.mult))
                link(nc.vector.tensor_tensor(m[:, :, :], m[:, :, :], tail, ALU.add))
                link(nc.vector.tensor_tensor(top[:, :, :], m[:, :, :], t["src_score"][:, :, :], ALU.max))
                link(nc.vector.tensor_tensor(m[:, :, :], m[:, :, :], top[:, :, :], ALU.subtract))
                nc.vector.tensor_tensor(own[:, :, :], t["src_score"][:, :, :], top[:, :, :], ALU.subtract).then_inc(exp_in, 1)
                link(nc.vector.tensor_tensor(q[:, :, :], top[:, :, :], t["dst_score"][:, :, :], ALU.add))
                link(nc.vector.tensor_tensor(q[:, :, :], q[:, :, :], t["valid"][:, :].rearrange("p (t h) -> p t h", h=H), ALU.add))
                nc.vector.tensor_reduce(best[:, :], q[:, :, :].rearrange("p t h -> p h t"), AX.X, ALU.max).then_inc(best_ready, 1)
                dve.wait_ge(all_ready, 1)
                nc.vector.tensor_tensor(q[:, :, :], q[:, :, :], best_all[:, :].unsqueeze(1).to_broadcast(everywhere), ALU.subtract).then_inc(exp_in, 1)
                dve.wait_ge(exp_out, 3)
                link(nc.vector.tensor_tensor(low[:, :, :], den, m[:, :, :], ALU.mult))
                link(nc.vector.tensor_tensor(low[:, :, :], low[:, :, :], own[:, :, :], ALU.add))
                link(nc.vector.tensor_tensor(low[:, :, :], low[:, :, :], q[:, :, :], ALU.mult))
                nc.vector.reduce_sum(part[:, :], low[:, :, :].rearrange("p t h -> p h t"), AX.X).then_inc(part_ready, 1)
                dve.wait_ge(z_ready, 1)
                link(nc.vector.reciprocal(inv[:, :], pz[:, 0:H]))
                link(nc.vector.tensor_tensor(q[:, :, :], q[:, :, :], inv[:, :].unsqueeze(1).to_broadcast(everywhere), ALU.mult))
                link(nc.vector.tensor_tensor(m[:, :, :], m[:, :, :], q[:, :, :], ALU.mult))
                link(nc.vector.tensor_tensor(own[:, :, :], own[:, :, :], q[:, :, :], ALU.mult))

                def by_head(x_):
                    return x_.rearrange("p t (h c) -> p t h c", h=H)

                heads = [P, NT, H, C]
                feats = agg[:, :, 0:F]
                dve.wait_ge(h_in, 16)
                dve.wait_ge(bias_in, 16)
                link(nc.vector.tensor_tensor(by_head(feats), by_head(feats), m[:, :, :].unsqueeze(3).to_broadcast(heads), ALU.mult))
                link(nc.vector.tensor_tensor(by_head(h[:, :, :]), by_head(h[:, :, :]), own[:, :, :].unsqueeze(3).to_broadcast(heads), ALU.mult))
                link(nc.vector.tensor_tensor(h[:, :, :], h[:, :, :], feats, ALU.add))
                link(nc.vector.tensor_tensor(h[:, :, :], h[:, :, :], bias[:, :].unsqueeze(1).to_broadcast([P, NT, F]), ALU.add))
                link(nc.vector.tensor_tensor(x[:, :, :], x[:, :, :], h[:, :, :], ALU.add))

            @block.gpsimd
            def _(pool):
                pool.wait_ge(best_ready, 1)
                nc.gpsimd.partition_all_reduce(best_all[:, :], best[:, :], P, RMAX).then_inc(all_ready, 1)

            @block.scalar
            def _(act):
                act.wait_ge(exp_in, 1)
                nc.scalar.activation(m[:, :, :], m[:, :, :], ACT.Exp).then_inc(exp_out, 1)
                nc.scalar.activation(own[:, :, :], own[:, :, :], ACT.Exp).then_inc(exp_out, 1)
                act.wait_ge(exp_in, 2)
                nc.scalar.activation(q[:, :, :], q[:, :, :], ACT.Exp).then_inc(exp_out, 1)

            @block.tensor
            def _(pe):
                pe.wait_ge(part_ready, 1)
                nc.tensor.matmul(pz[:, 0:H], t["ones"][:, :], part[:, :], start=True, stop=True).then_inc(z_ready, 1)


def finish_local(nc, t, ins):
    ctx = ExitStack()
    with ctx:
        bias = ctx.enter_context(nc.sbuf_tensor("f3_bias", [P, F], F32))
        inv = ctx.enter_context(nc.sbuf_tensor("f3_inv", [P, NT, H], F32))
        sem = ctx.enter_context(semaphores(nc, "f3_"))
        bias_in, chain = sem("bias_in"), sem("chain")
        with nc.Block() as block:
            @block.sync
            def _(sp):
                sp.dma_start(bias[:, :], ins["L3_gnn_bias"].partition_broadcast(P)).then_inc(bias_in, 16)

            @block.vector
            def _(dve):
                link = Chain(dve, chain)
                agg, x = t["agg"], t["x"]
                feats = agg[:, :, 0:F]
                by_head = feats.rearrange("p t (h c) -> p t h c", h=H)
                link(nc.vector.tensor_scalar_add(inv[:, :, :], agg[:, :, F:F + H], 1e-16))
                link(nc.vector.reciprocal(inv[:, :, :], inv[:, :, :]))
                link(nc.vector.tensor_tensor(by_head, by_head, inv[:, :, :].unsqueeze(3).to_broadcast([P, NT, H, C]), ALU.mult))
                dve.wait_ge(bias_in, 16)
                link(nc.vector.tensor_tensor(feats, feats, bias[:, :].unsqueeze(1).to_broadcast([P, NT, F]), ALU.add))
                link(nc.vector.scalar_tensor_tensor(x[:, :, :], feats, 0.0, x[:, :, :], ALU.max, ALU.add))


def program(nc, ins, out):
    ctx = ExitStack()
    with ctx:
        def sb(name, shape, dt=F32):
            return ctx.enter_context(nc.sbuf_tensor(name, shape, dt))

        def dram(name, shape, dt=F32):
            return nc.dram_tensor(name, shape, dt, kind="Internal").ap()

        t = {
            "x": sb("x", [P, NT, F]),
            "edges": sb("edges", [P, NSR, FIELDS]),
            "tile_row": sb("tile_row", [1, NSR], I32),
            "ones": sb("ones", [P, P]), "ident": sb("ident", [P, P]), "earlier": sb("earlier", [P, P]),
            "col_no": sb("col_no", [P, P]), "row_no": sb("row_no", [P, G]), "spare_row": sb("spare_row", [P, G]),
            "valid": sb("valid", [P, NT * H]),
            "dst_blk": dram("dst_blk", (NB, P), I32), "src_blk": dram("src_blk", (NB, P), I32),
            "type_blk": dram("type_blk", (NB, P), I32),
            "w0_blk": dram("w0_blk", (NB, P)), "w1_blk": dram("w1_blk", (NB, P)),
            "tile_dram": dram("tile_dram", (NSR,), I32),
            "dst_step": dram("dst_step", (NSR * P + 1,)), "flag_step": dram("flag_step", (NSR * P + 1,)),
            "loc_step": dram("loc_step", (NSR, P)), "src_step": dram("src_step", (NSR, P)),
        }
        t["agg"] = sb("agg", [P, NT, W])
        t["dst_score"], t["src_score"] = sb("dst_score", [P, NT, H]), sb("src_score", [P, NT, H])
        t["msg_table"] = dram("msg_table", (R * NP, F))
        t["sums"] = [dram(f"sums{k}", (NP + P, F)) for k in range(K0)]
        t["head_table"] = dram("head_table", (NP, F + H))
        prepare(nc, t, ins)
        nodes(nc, t, ins, 0)
        scatter_edges(nc, t, ins)
        nodes(nc, t, ins, 1)
        relation_edges(nc, t, ins)
        nodes(nc, t, ins, 2)
        attention_edges(nc, t, ins, 2)
        finish_global(nc, t, ins)
        nodes(nc, t, ins, 3)
        attention_edges(nc, t, ins, 3)
        finish_local(nc, t, ins)
        with nc.semaphore("stored") as stored, nc.Block() as block:
            @block.sync
            def _(sp):
                sp.dma_start(out[0:(NT - 1) * P, :].rearrange("(t p) f -> p t f", p=P), t["x"][:, 0:NT - 1, :]).then_inc(stored, 16)
                sp.dma_start(out[(NT - 1) * P:N, :], t["x"][0:LAST, NT - 1, :]).then_inc(stored, 16)
                sp.wait_ge(stored, 32)


INPUTS = ["x", "src", "dst", "edge_type_16", "edge_weight", "edge_weight1", "L0_gnn_weight", "L0_gnn_bias",
          "L1_gnn_weight", "L1_gnn_gate_weight", "L2_gnn_W", "L2_gnn_att", "L2_gnn_b", "L3_gnn_W",
          "L3_gnn_att_src", "L3_gnn_att_dst", "L3_gnn_bias"]


def kernel(**inputs):
    import numpy as np
    import concourse.bacc as bacc
    from concourse.bass_utils import run_bass_kernel_spmd

    nc = bacc.Bacc("TRN2", target_bir_lowering=False, num_devices=1)
    arrays, ins = {}, {}
    for name in INPUTS:
        a = np.ascontiguousarray(inputs[name])
        arrays[f"in_{name}"] = a
        ins[name] = nc.dram_tensor(f"in_{name}", a.shape, mybir.dt.from_np(a.dtype), kind="ExternalInput").ap()
    out = nc.dram_tensor("result", (N, F), F32, kind="ExternalOutput").ap()
    program(nc, ins, out)
    return run_bass_kernel_spmd(nc, [arrays], core_ids=[0]).results[0]["result"]
```

```python
from contextlib import ExitStack, contextmanager

import concourse.bass as bass
from concourse import mybir

F32 = mybir.dt.float32
I32 = mybir.dt.int32
ALU = mybir.AluOpType
ACT = mybir.ActivationFunctionType
AX = mybir.AxisListType
RMAX = bass.bass_isa.ReduceOp.max
RADD = bass.bass_isa.ReduceOp.add

P = 128
N, E, F, R = 6250, 100000, 256, 16
NT = (N + P - 1) // P
NP = NT * P
LAST = N - (NT - 1) * P
NB = 784
BP = 7
SC = 7
NSR = SC * P
G = 8
NBAT = (NB + NT - 1 + G - 1) // G
NBAT += NBAT % 2
K0 = 4
H = 8
C = F // H
W = F + 2 * H
BIG = 1e30
FIELDS = 6
LOC, SRC, IDX1, W0, W1, TAIL = range(FIELDS)


class Chain:

    def __init__(self, eng, sem, n=0):
        self.eng, self.sem, self.n = eng, sem, n

    def __call__(self, ins):
        self.n = self.n + 1
        ins.then_inc(self.sem, 1)
        self.eng.wait_ge(self.sem, self.n)


@contextmanager
def semaphores(nc, prefix):
    held = []

    def sem(name):
        held.append(nc.alloc_semaphore(name=prefix + name))
        return held[-1]

    yield sem
    nc.clear_and_free_semaphores(held)
    nc.all_engine_barrier()


def freed(eng, sem, value):
    if not isinstance(value, int) or value > 0:
        eng.wait_ge(sem, value)


def at(i):
    return slice(i, i + 1) if isinstance(i, int) else bass.ds(i, 1)


def span(start, n):
    return slice(start, start + n) if isinstance(start, int) else bass.ds(start, n)


def batches(eng, body, unroll):
    for u in range(unroll):
        body(0, u)
    with eng.Fori(1, NBAT // unroll - 1) as it:
        for u in range(unroll):
            body(it, u)
    for u in range(unroll):
        body(NBAT // unroll - 1, u)


def exists(b):
    return not isinstance(b, int) or b < NBAT


def tiles_of(nc, eng, t, b):
    _, values = nc.values_load_multi_w_load_instructions(
        t["tile_row"][0:1, span(b * G, G)], engines=(eng.engine,), min_val=0, max_val=NT - 1,
        skip_runtime_bounds_check_because="a step's tile counts at most NT - 1 tile ends")
    return values


def tiles(eng, body):
    body(0, 0)
    body(0, 1)
    with eng.Fori(1, NT // 2) as it:
        body(it, 0)
        body(it, 1)
    body(NT // 2, 0)


def flat(ap):
    return ap.rearrange("a b -> (a b)")


def prepare(nc, t, ins):
    ctx = ExitStack()
    with ctx:
        def sb(name, shape, dt=F32):
            return ctx.enter_context(nc.sbuf_tensor("prep_" + name, shape, dt))

        sem = ctx.enter_context(semaphores(nc, "prep_"))

        blocks = sb("blocks", [NB // BP, BP, P], I32)
        pad_dst, pad_zero = sb("pad_dst", [1, NB * P - E], I32), sb("pad_zero", [1, NB * P - E], I32)
        lastf = sb("lastf", [NB // BP, BP])
        limit = sb("limit", [P, NT - 1])
        tile_no = sb("tile_no", [P, NT - 1])
        below = sb("below", [P, NT - 1, BP])
        count = sb("count", [P, NT - 1])
        leave = sb("leave", [P, NT - 1])
        step_no = sb("step_no", [P, SC])
        passed = sb("passed", [P, SC, NT - 1])
        tile_of, tile_base = sb("tile_of", [P, SC]), sb("tile_base", [P, SC])
        blockf, block_of = sb("blockf", [P, SC]), sb("block_of", [P, SC], I32)
        tile_i = sb("tile_i", [SC, P], I32)
        raw = [sb(f"raw{k}", [P, SC, P], I32) for k in range(3)]
        rows = [sb(f"rows{k}", [P, SC, P]) for k in range(FIELDS)]
        dstf = sb("dstf", [P, SC, P])
        here, before = sb("here", [P, NSR]), sb("before", [P, NSR])
        flags = sb("flags", [P, SC, P])
        split, split_c = sb("split", [P, 2, SC]), sb("split_c", [SC, 2, P])
        edge_pad = sb("edge_pad", [1, 2])
        ps = [ctx.enter_context(nc.psum_tensor(f"prep_ps{i}", [P, 1024], F32)) for i in range(2)]
        pc = ctx.enter_context(nc.psum_tensor("prep_pc", [P, 512], F32))
        names = ["copied", "padded", "pads", "blocks", "consts", "zeroed", "counted", "dve", "steps_ready",
                 "rows_in", "by_step_out", "by_step", "shifted", "flags_out", "flags", "tails", "ready_t", "tps", "turned", "taken",
                 "tile_t", "tile_c", "tile_out", "tile_in", "x_in", "xz", "pool", "flag_set",
                 "rep", "split_t", "split_out", "split_min", "split_p"]
        s = {n: sem(n) for n in names}
        scr = [t["dst_blk"], t["src_blk"], t["type_blk"], t["w0_blk"], t["w1_blk"]]
        src_in = [ins["dst"], ins["src"], ins["edge_type_16"], ins["edge_weight"], flat(ins["edge_weight1"])]
        with nc.Block() as block:
            @block.sync
            def _(sp):
                for a, b in zip(scr, src_in):
                    sp.dma_start(flat(a)[0:E].rearrange("(a b) -> a b", a=16), b.rearrange("(a b) -> a b", a=16)).then_inc(s["copied"], 16)
                sp.wait_ge(s["pads"], 2)
                for k, a in enumerate(scr):
                    pad = pad_dst if k == 0 else pad_zero
                    pad = pad[:, :] if k < 3 else pad[:, :].bitcast(F32)
                    sp.dma_start(flat(a)[E:NB * P].unsqueeze(0), pad).then_inc(s["padded"], 16)
                sp.wait_ge(s["copied"], 5 * 16)
                sp.wait_ge(s["padded"], 5 * 16)
                sp.dma_start(blocks[:, :, :], t["dst_blk"].rearrange("(p j) e -> p j e", j=BP)).then_inc(s["blocks"], 16)
                sp.wait_ge(s["xz"], 1)
                xin = ins["x"]
                sp.dma_start(t["x"][:, 0:NT - 1, :], xin[0:(NT - 1) * P, :].rearrange("(t p) f -> p t f", p=P)).then_inc(s["x_in"], 16)
                sp.dma_start(t["x"][0:LAST, NT - 1, :], xin[(NT - 1) * P:N, :]).then_inc(s["x_in"], 16)
                sp.wait_ge(s["tile_c"], 1)
                sp.dma_start(t["tile_dram"].rearrange("(c p) -> c p", p=P), tile_i[:, :]).then_inc(s["tile_out"], 16)
                sp.wait_ge(s["tile_out"], 16)
                sp.dma_start(t["tile_row"][:, :], t["tile_dram"].unsqueeze(0)).then_inc(s["tile_in"], 16)
                sp.wait_ge(s["by_step"], 1)
                d = t["dst_step"]
                sp.dma_start(d[1:1 + NSR * P].rearrange("(c p e) -> p c e", p=P, e=P), dstf[:, :, :]).then_inc(s["by_step_out"], 16)
                sp.dma_start(d[0:1].unsqueeze(0), edge_pad[:, 0:1]).then_inc(s["by_step_out"], 16)
                for k, name in ((LOC, "loc_step"), (SRC, "src_step")):
                    sp.dma_start(t[name].rearrange("(c p) e -> p c e", p=P), rows[k][:, :, :]).then_inc(s["by_step_out"], 16)
                sp.wait_ge(s["by_step_out"], 4 * 16)
                sp.dma_start(here[:, :], d[1:1 + NSR * P].rearrange("(p j) -> p j", p=P)).then_inc(s["shifted"], 16)
                sp.dma_start(before[:, :], d[0:NSR * P].rearrange("(p j) -> p j", p=P)).then_inc(s["shifted"], 16)
                sp.wait_ge(s["flag_set"], 1)
                f = t["flag_step"]
                sp.dma_start(f[0:NSR * P].rearrange("(p j) -> p j", p=P), here[:, :]).then_inc(s["flags_out"], 16)
                sp.dma_start(f[NSR * P:NSR * P + 1].unsqueeze(0), edge_pad[:, 1:2]).then_inc(s["flags_out"], 16)
                sp.wait_ge(s["flags_out"], 2 * 16)
                sp.dma_start(rows[TAIL][:, :, :], f[1:1 + NSR * P].rearrange("(c p e) -> p c e", p=P, e=P)).then_inc(s["tails"], 16)
                rep = t["flag_rows"]
                nf = NBAT * G * P
                sp.dma_start(rep[:, 0, 0:G, 0:P], f[0:nf].rearrange("(b g e) -> b g e", g=G, e=P)).then_inc(s["rep"], 16)
                sp.dma_start(rep[:, 0, 0:G, P:P + 1], f[1:1 + nf].rearrange("(b g e) -> b g e", g=G, e=P)[:, :, P - 1:P],
                             allow_slow_non_contiguous=True).then_inc(s["rep"], 16)
                sp.dma_start(rep[:, 0, G, :], f[0:nf].rearrange("(b e) -> b e", e=G * P)[:, 0:P + 1]).then_inc(s["rep"], 16)
                sp.wait_ge(s["rep"], 48)
                for h in range(1, H):
                    sp.dma_start(rep[:, h, :, :], rep[:, 0, :, :]).then_inc(s["rep"], 16)
                sp.dma_start(flags[:, :, :], f[0:NSR * P].rearrange("(c p e) -> p c e", p=P, e=P)).then_inc(s["flags"], 16)
                for k in range(2):
                    sp.wait_ge(s["split_t"], k + 1)
                    sp.dma_start(t["split_dram"][k].rearrange("(c p) -> c p", p=P), split_c[:, k, :]).then_inc(s["split_out"], 16)
                sp.wait_ge(s["split_out"], 32)
                sp.dma_start(t["split_row"][0:1, :, :].rearrange("a k s -> a (k s)"), t["split_dram"].rearrange("k s -> (k s)").unsqueeze(0)).then_inc(s["split_out"], 16)
                sp.wait_ge(s["split_out"], 48)
                sp.wait_ge(s["rep"], (H + 2) * 16)
                sp.wait_ge(s["tails"], 16)
                sp.wait_ge(s["tile_in"], 16)
                sp.wait_ge(s["x_in"], 32)

            @block.gpsimd
            def _(pool):
                nc.gpsimd.memset(pad_dst[:, :], 8191).then_inc(s["pads"], 1)
                nc.gpsimd.memset(pad_zero[:, :], 0).then_inc(s["pads"], 1)
                nc.gpsimd.memset(edge_pad[:, 0:1], -1.0).then_inc(s["zeroed"], 1)
                nc.gpsimd.memset(edge_pad[:, 1:2], -BIG).then_inc(s["zeroed"], 1)
                nc.gpsimd.memset(t["ones"][:, :], 1.0).then_inc(s["zeroed"], 1)
                nc.gpsimd.memset(t["ident"][:, :], 0.0).then_inc(s["zeroed"], 1)
                nc.gpsimd.memset(t["valid"][:, :], 0.0).then_inc(s["zeroed"], 1)
                kw = dict(allow_small_or_imprecise_dtypes=True)
                nc.gpsimd.iota(limit[:, :], [[P, NT - 1]], base=P, channel_multiplier=0, **kw).then_inc(s["consts"], 1)
                nc.gpsimd.iota(tile_no[:, :], [[1, NT - 1]], base=0, channel_multiplier=0, **kw).then_inc(s["consts"], 1)
                nc.gpsimd.iota(step_no[:, :], [[P, SC]], base=0, channel_multiplier=1, **kw).then_inc(s["consts"], 1)
                nc.gpsimd.iota(t["col_no"][:, :], [[1, P]], base=0, channel_multiplier=0, **kw).then_inc(s["consts"], 1)
                nc.gpsimd.iota(t["row_no"][:, :], [[0, G]], base=0, channel_multiplier=1, **kw).then_inc(s["consts"], 1)
                nc.gpsimd.iota(t["spare_row"][:, :], [[0, G]], base=NP, channel_multiplier=1, **kw).then_inc(s["consts"], 1)
                pool.wait_ge(s["zeroed"], 5)
                nc.gpsimd.affine_select(out=t["ident"][:, :], in_=t["ident"][:, :], compare_op=ALU.not_equal, fill=1.0,
                                        base=0, pattern=[[-1, P]], channel_multiplier=1).then_inc(s["consts"], 1)
                nc.gpsimd.affine_select(out=t["earlier"][:, :], in_=t["ones"][:, :], compare_op=ALU.is_gt, fill=0.0,
                                        base=0, pattern=[[-1, P]], channel_multiplier=1).then_inc(s["consts"], 1)
                v = t["valid"][:, (NT - 1) * H:NT * H]
                nc.gpsimd.affine_select(out=v, in_=v, compare_op=ALU.is_ge, fill=-BIG,
                                        base=LAST - 1, pattern=[[0, H]], channel_multiplier=-1).then_inc(s["consts"], 1)
                pool.wait_ge(s["steps_ready"], 1)
                pool.wait_ge(s["padded"], 5 * 16)
                dest = [raw[0], raw[1], raw[2], rows[W0], rows[W1]]
                for c in range(SC):
                    for a, d in zip(scr, dest):
                        nc.gpsimd.indirect_dma_start(d[:, c, :], None, a[:, :], bass.IndirectOffsetOnAxis(ap=block_of[:, c:c + 1], axis=0)).then_inc(s["rows_in"], 16)
                pool.wait_ge(s["rows_in"], 5 * SC * 16)

            @block.vector
            def _(dve):
                link = Chain(dve, s["dve"])
                nc.vector.memset(t["x"][:, NT - 1, :], 0.0).then_inc(s["xz"], 1)
                dve.wait_ge(s["blocks"], 16)
                dve.wait_ge(s["consts"], 9)
                link(nc.vector.tensor_copy(lastf[:, :], blocks[:, :, P - 1]))
                nb = NB // BP
                link(nc.vector.tensor_tensor(below[0:nb], lastf[:, :].unsqueeze(1).to_broadcast([nb, NT - 1, BP]),
                                             limit[0:nb, :].unsqueeze(2).to_broadcast([nb, NT - 1, BP]), ALU.is_lt))
                link(nc.vector.reduce_sum(count[0:nb, :], below[0:nb], AX.X))
                nc.vector.tensor_copy(count[0:nb, 0:1], count[0:nb, 0:1]).then_inc(s["ready_t"], 1)
                dve.wait_ge(s["counted"], 1)
                link(nc.vector.tensor_tensor(leave[:, :], pc[:, 0:NT - 1], tile_no[:, :], ALU.add))
                link(nc.vector.tensor_tensor(passed[:, :, :], leave[:, :].unsqueeze(1).to_broadcast([P, SC, NT - 1]),
                                             step_no[:, :].unsqueeze(2).to_broadcast([P, SC, NT - 1]), ALU.is_lt))
                link(nc.vector.reduce_sum(tile_of[:, :], passed[:, :, :], AX.X))
                link(nc.vector.tensor_tensor(blockf[:, :], step_no[:, :], tile_of[:, :], ALU.subtract))
                nc.vector.tensor_scalar_min(block_of[:, :], blockf[:, :], float(NB - 1)).then_inc(s["steps_ready"], 1)
                link(nc.vector.tensor_scalar_mul(tile_base[:, :], tile_of[:, :], float(P)))
                dve.wait_ge(s["tile_t"], 1)
                nc.vector.tensor_copy(tile_i[:, :], pc[0:SC, 256:256 + P]).then_inc(s["tile_c"], 1)
                dve.wait_ge(s["rows_in"], 5 * SC * 16)
                link(nc.vector.tensor_copy(dstf[:, :, :], raw[0][:, :, :]))
                link(nc.vector.tensor_copy(rows[SRC][:, :, :], raw[1][:, :, :]))
                link(nc.vector.tensor_tensor(rows[LOC][:, :, :], dstf[:, :, :], tile_base[:, :].unsqueeze(2).to_broadcast([P, SC, P]), ALU.subtract))
                nc.vector.scalar_tensor_tensor(rows[IDX1][:, :, :], raw[2][:, :, :], float(NP), rows[SRC][:, :, :], ALU.mult, ALU.add).then_inc(s["by_step"], 1)
                dve.wait_ge(s["shifted"], 32)
                link(nc.vector.tensor_tensor(here[:, :], here[:, :], before[:, :], ALU.not_equal))
                nc.vector.tensor_scalar_mul(here[:, :], here[:, :], -BIG).then_inc(s["flag_set"], 1)
                dve.wait_ge(s["tails"], 16)
                dve.wait_ge(s["flags"], 16)
                nc.vector.tensor_reduce(split[:, 0, :], flags[:, :, :], AX.X, ALU.min).then_inc(s["split_min"], 1)
                nc.vector.tensor_reduce(split[:, 1, :], rows[TAIL][:, :, :], AX.X, ALU.min).then_inc(s["split_min"], 1)
                dve.wait_ge(s["split_min"], 2)
                for k in range(2):
                    dve.wait_ge(s["split_p"], k + 1)
                    nc.vector.tensor_copy(split_c[:, k, :], pc[0:SC, 384:384 + P]).then_inc(s["split_t"], 1)
                nc.vector.tensor_scalar_mul(rows[TAIL][:, :, :], rows[TAIL][:, :, :], -1.0 / BIG).then_inc(s["ready_t"], 1)
                for k in range(FIELDS):
                    dve.wait_ge(s["turned"], k + 1)
                    v = t["edges"][:, :, k]
                    nc.vector.tensor_copy(v[:, 0:512], ps[k % 2][:, 0:512]).then_inc(s["taken"], 1)
                    nc.vector.tensor_copy(v[:, 512:NSR], ps[k % 2][:, 512:NSR]).then_inc(s["taken"], 1)

            @block.tensor
            def _(pe):
                pe.wait_ge(s["ready_t"], 1)
                nb = NB // BP
                nc.tensor.matmul(pc[:, 0:NT - 1], t["ones"][0:nb, :], count[0:nb, :], start=True, stop=True).then_inc(s["counted"], 1)
                pe.wait_ge(s["steps_ready"], 1)
                nc.tensor.transpose(pc[0:SC, 256:256 + P], tile_of[:, :], t["ident"][:, :]).then_inc(s["tile_t"], 1)
                pe.wait_ge(s["split_min"], 2)
                pe.wait_ge(s["tile_c"], 1)
                for k in range(2):
                    freed(pe, s["split_t"], k)
                    nc.tensor.transpose(pc[0:SC, 384:384 + P], split[:, k, :], t["ident"][:, :]).then_inc(s["split_p"], 1)
                pe.wait_ge(s["ready_t"], 2)
                for k in range(FIELDS):
                    if k >= 2:
                        pe.wait_ge(s["taken"], 2 * (k - 1))
                    for c in range(SC):
                        last = nc.tensor.transpose(ps[k % 2][:, c * P:(c + 1) * P], rows[k][:, c, :], t["ident"][:, :])
                    last.then_inc(s["turned"], 1)


def nodes(nc, t, ins, layer):
    name = f"n{layer}_"
    attention = layer >= 2
    pairs = R // 2 if layer == 1 else 0
    ctx = ExitStack()
    with ctx:
        def sb(n, shape, dt=F32):
            return ctx.enter_context(nc.sbuf_tensor(name + n, shape, dt))

        sem = ctx.enter_context(semaphores(nc, name))

        def both(n):
            return [sem(n + "0"), sem(n + "1")]

        weight = {0: "L0_gnn_weight", 1: "L1_gnn_weight", 2: "L2_gnn_W", 3: "L3_gnn_W"}[layer]
        if layer == 1:
            w = t["agg"][:, :, :].rearrange("p t f -> p (t f)")[:, 0:2 * R * F].rearrange("p (c o) -> p c o", c=2)
        else:
            w = sb("w", [P, 2, F])
        stats = sb("stats", [P, NT, 6])
        mean, diff, var, std = (sb(n, [P, NT]) for n in ("mean", "diff", "var", "std"))
        rstd, shift = sb("rstd", [P, NT]), sb("shift", [P, NT])
        eps = sb("eps", [P, 1])
        h = sb("h", [P, 2, F])
        hT = sb("hT", [P, 2, 2, P])
        pT = [ctx.enter_context(nc.psum_tensor(name + f"pT{i}", [P, 512], F32)) for i in range(2)]
        if layer == 1:
            gate_w, gate, msg = sb("gate_w", [P, 2, R]), sb("gate", [P, 2, R]), sb("msg", [P, 2, R, F])
            pm = [ctx.enter_context(nc.psum_tensor(name + f"pm{i}", [P, 512], F32)) for i in range(4)]
            pg = [ctx.enter_context(nc.psum_tensor(name + f"pg{i}", [P, 512], F32)) for i in range(2)]
        else:
            pm = [ctx.enter_context(nc.psum_tensor(name + f"pm{i}", [P, 512], F32)) for i in range(2)]
        if layer == 0:
            zero, zero_set = sb("zero", [P, F]), sem("zero_set")
        if attention:
            heads = 4 if layer == 2 else H
            att = sb("att", [P, 2, F])
            row = sb("row", [P, 2, W])
            act_h, weighed, score = sb("act_h", [P, F]), sb("weighed", [P, 2, F]), sb("score", [P, 2, H])
        weights_in, eps_set, chain, stat_done = sem("weights_in"), sem("eps_set"), sem("chain"), sem("stat_done")
        var_ready, std_ready, scale_ready = sem("var_ready"), sem("std_ready"), sem("scale_ready")
        normed, turned, copied, prod, taken, written = (both(n) for n in ("normed", "turned", "copied", "prod", "taken", "written"))
        gate_prod, scored = both("gate_prod"), both("scored")
        filled = [sem(f"filled{i}") for i in range(4)]
        emptied = [sem(f"emptied{i}") for i in range(4)]
        n_weights = {0: 1, 1: 2, 2: 3, 3: 3}[layer]

        def pipeline(eng, first, second):
            def pair(it):
                first(it, 1)
                second(it, 0)
                first(it + 1, 0)
                second(it, 1)

            first(0, 0)
            pair(0)
            with eng.Fori(1, NT // 2) as it:
                pair(it)
            second(NT // 2, 0)

        with nc.Block() as block:
            @block.sync
            def _(sp):
                if layer == 1:
                    for c in range(2):
                        sp.dma_start(w[:, c, :].rearrange("p (r o) -> p r o", r=R),
                                     ins[weight][:, c * P:(c + 1) * P, :].rearrange("r p o -> p r o")).then_inc(weights_in, 16)
                    with nc.allow_non_contiguous_dma(reason="small gate weights"):
                        for c in range(2):
                            sp.dma_start(gate_w[:, c, :], ins["L1_gnn_gate_weight"][:, c * P:(c + 1) * P, 0].rearrange("r p -> p r")).then_inc(weights_in, 16)
                else:
                    src = ins[weight] if layer != 3 else ins[weight].rearrange("f h d -> f (h d)")
                    sp.dma_start(w[:, :, :], src.rearrange("(c p) o -> p c o", p=P)).then_inc(weights_in, 16)
                if layer == 2:
                    a = ins["L2_gnn_att"]
                    for k in range(2):
                        sp.dma_start(att[:, k, :].rearrange("p (h d) -> p h d", h=4),
                                     a[0, :, k * 64:(k + 1) * 64].partition_broadcast(P)).then_inc(weights_in, 16)
                if layer == 3:
                    for k, n in enumerate(("L3_gnn_att_src", "L3_gnn_att_dst")):
                        sp.dma_start(att[:, k, :], flat(ins[n]).partition_broadcast(P)).then_inc(weights_in, 16)

                def store(it, par):
                    i = it * 2 + par
                    if layer == 1:
                        for slot in range(4):
                            sp.wait_ge(emptied[slot], it * 4 + (2 * par + 2))
                        sp.dma_start(t["msg_table"].rearrange("(r t p) f -> t p r f", r=R, p=P)[at(i)].rearrange("a p r f -> (a p) r f"),
                                     msg[:, par, :, :]).then_inc(written[par], 16)
                    if attention:
                        sp.wait_ge(scored[par], it + 1)
                        sp.dma_start(t["head_table"].rearrange("(t p) f -> t p f", p=P)[at(i)].rearrange("a p f -> (a p) f"),
                                     row[:, par, 0:F + H]).then_inc(written[par], 16)

                if layer == 0:
                    sp.wait_ge(zero_set, 1)
                    for a in t["sums"]:
                        sp.dma_start(a.rearrange("(t p) f -> p t f", p=P), zero[:, :].unsqueeze(1).to_broadcast([P, NT + 1, F])).then_inc(written[0], 16)
                    sp.wait_ge(written[0], 16 * K0)
                if layer:
                    store(0, 0)
                    store(0, 1)
                    with sp.Fori(1, NT // 2) as it:
                        store(it, 0)
                        store(it, 1)
                    store(NT // 2, 0)
                    sp.wait_ge(written[0], 16 * (NT // 2 + 1))
                    sp.wait_ge(written[1], 16 * (NT // 2))

            @block.scalar
            def _(act):
                act.wait_ge(eps_set, 1)
                act.wait_ge(var_ready, 1)
                nc.scalar.activation(std[:, :], var[:, :], ACT.Sqrt, bias=eps[:, 0:1]).then_inc(std_ready, 1)
                act.wait_ge(scale_ready, 1)

                def norm(it, par):
                    i = it * 2 + par
                    freed(act, turned[par], it)
                    nc.scalar.activation(h[:, par, :], t["x"][:, at(i), :].rearrange("p a f -> p (a f)"), ACT.Relu,
                                         bias=shift[:, at(i)], scale=rstd[:, at(i)]).then_inc(normed[par], 1)

                def take(it, par):
                    i = it * 2 + par
                    if layer == 1:
                        act.wait_ge(gate_prod[par], it + 1)
                        freed(act, written[par], it * 16)
                        nc.scalar.activation(gate[:, par, :], pg[par][:, 0:R], ACT.Sigmoid).then_inc(taken[par], 1)
                        act.wait_ge(taken[par], it + 1)
                        for p in range(1, pairs, 2):
                            slot = p % 4
                            act.wait_ge(filled[slot], it * 4 + (2 * par + p // 4 + 1))
                            for r in range(2):
                                last = nc.scalar.activation(msg[:, par, 2 * p + r, :], pm[slot][:, r * F:(r + 1) * F], ACT.Copy,
                                                            scale=gate[:, par, 2 * p + r:2 * p + r + 1])
                            last.then_inc(emptied[slot], 1)
                        return
                    act.wait_ge(prod[par], it + 1)
                    if layer == 0:
                        out = t["agg"][:, at(i), 0:F].rearrange("p a f -> p (a f)")
                    else:
                        freed(act, written[par], it * 16)
                        out = row[:, par, 0:F]
                    nc.scalar.activation(out, pm[par][:, 0:F], ACT.Copy).then_inc(taken[par], 1)

                pipeline(act, norm, take)

            @block.vector
            def _(dve):
                link = Chain(dve, chain)
                nc.vector.memset(eps[:, :], 1e-5).then_inc(eps_set, 1)
                if layer == 0:
                    nc.vector.memset(zero[:, :], 0.0).then_inc(zero_set, 1)
                with dve.Fori(0, NT) as i:
                    nc.vector.bn_stats(stats[:, at(i), :].rearrange("p a s -> p (a s)"),
                                       t["x"][:, at(i), :].rearrange("p a f -> p (a f)")).then_inc(stat_done, 1)
                dve.wait_ge(stat_done, NT)
                link(nc.vector.tensor_tensor(mean[:, :], stats[:, :, 1], stats[:, :, 4], ALU.add))
                link(nc.vector.tensor_tensor(diff[:, :], stats[:, :, 1], stats[:, :, 4], ALU.subtract))
                link(nc.vector.tensor_tensor(var[:, :], stats[:, :, 2], stats[:, :, 5], ALU.add))
                link(nc.vector.tensor_tensor(diff[:, :], diff[:, :], diff[:, :], ALU.mult))
                link(nc.vector.tensor_scalar_mul(diff[:, :], diff[:, :], 0.25))
                nc.vector.scalar_tensor_tensor(var[:, :], var[:, :], 1.0 / F, diff[:, :], ALU.mult, ALU.add).then_inc(var_ready, 1)
                dve.wait_ge(std_ready, 1)
                link(nc.vector.reciprocal(rstd[:, :], std[:, :]))
                nc.vector.scalar_tensor_tensor(shift[:, :], mean[:, :], -0.5, rstd[:, :], ALU.mult, ALU.mult).then_inc(scale_ready, 1)
                dve.wait_ge(weights_in, 16 * (4 if layer == 1 else n_weights))

                def copy(it, par):
                    if layer == 1:
                        freed(dve, written[par], it * 16)
                    else:
                        freed(dve, prod[par], it)
                    dve.wait_ge(turned[par], it + 1)
                    nc.vector.tensor_copy(hT[:, par, :, :].rearrange("p c n -> p (c n)"), pT[par][:, 0:F]).then_inc(copied[par], 1)

                def finish(it, par):
                    i = it * 2 + par
                    if layer == 1:
                        dve.wait_ge(taken[par], it + 1)
                        for p in range(0, pairs, 2):
                            slot = p % 4
                            dve.wait_ge(filled[slot], it * 4 + (2 * par + p // 4 + 1))
                            nc.vector.tensor_tensor(msg[:, par, 2 * p:2 * p + 2, :], pm[slot][:, :].rearrange("p (r f) -> p r f", r=2),
                                                    gate[:, par, 2 * p:2 * p + 2].unsqueeze(2).to_broadcast([P, 2, F]), ALU.mult).then_inc(emptied[slot], 1)
                    if attention:
                        dve.wait_ge(taken[par], it + 1)
                        feats = row[:, par, 0:F]
                        base = 6 if layer == 2 else 4
                        k0 = (it * 2 + par) * base + n_links
                        k = 0

                        def step(ins_):
                            nonlocal k
                            k += 1
                            ins_.then_inc(chain, 1)
                            dve.wait_ge(chain, k0 + k)

                        if layer == 2:
                            step(nc.vector.scalar_tensor_tensor(act_h[:, :], feats, 0.2, feats, ALU.mult, ALU.max))
                            feats = act_h[:, :]
                        step(nc.vector.tensor_tensor(weighed[:, 0, :], feats, att[:, 0, :], ALU.mult))
                        step(nc.vector.tensor_tensor(weighed[:, 1, :], feats, att[:, 1, :], ALU.mult))
                        step(nc.vector.reduce_sum(score[:, :, 0:heads], weighed[:, :, :].rearrange("p k (h d) -> p k h d", h=heads), AX.X))
                        rep = H // heads
                        dup = [score[:, k_, 0:heads].unsqueeze(2).to_broadcast([P, heads, rep]) for k_ in range(2)]
                        here = at(i)
                        step(nc.vector.tensor_copy(t["dst_score"][:, here, :].rearrange("p a (h r) -> p (a h) r", r=rep), dup[1]))
                        if layer == 2:
                            step(nc.vector.tensor_copy(t["src_score"][:, here, :].rearrange("p a (h r) -> p (a h) r", r=rep), dup[0]))
                        nc.vector.tensor_copy(row[:, par, F:F + H].rearrange("p (h r) -> p h r", r=rep), dup[0]).then_inc(scored[par], 1)

                n_links = link.n
                pipeline(dve, copy, finish)

            @block.tensor
            def _(pe):
                pe.wait_ge(weights_in, 16 * (4 if layer == 1 else n_weights))

                def turn(it, par):
                    pe.wait_ge(normed[par], it + 1)
                    freed(pe, copied[par], it)
                    for c in range(2):
                        last = nc.tensor.transpose(pT[par][:, c * P:(c + 1) * P], h[:, par, c * P:(c + 1) * P], t["ident"][:, :])
                    last.then_inc(turned[par], 1)

                def multiply(it, par):
                    pe.wait_ge(copied[par], it + 1)
                    if layer != 1:
                        freed(pe, taken[par], it)
                        for c in range(2):
                            last = nc.tensor.matmul(pm[par][:, 0:F], hT[:, par, c, :], w[:, c, :], start=c == 0, stop=c == 1)
                        last.then_inc(prod[par], 1)
                        return
                    freed(pe, taken[par], it)
                    for c in range(2):
                        last = nc.tensor.matmul(pg[par][:, 0:R], hT[:, par, c, :], gate_w[:, c, :], start=c == 0, stop=c == 1)
                    last.then_inc(gate_prod[par], 1)
                    for p in range(pairs):
                        slot = p % 4
                        freed(pe, emptied[slot], it * 4 + (2 * par + p // 4))
                        for c in range(2):
                            last = nc.tensor.matmul(pm[slot][:, :], hT[:, par, c, :], w[:, c, p * 2 * F:(p + 1) * 2 * F], start=c == 0, stop=c == 1)
                        last.then_inc(filled[slot], 1)

                pipeline(pe, turn, multiply)


def scatter_edges(nc, t, ins):
    name = "e0_"
    ctx = ExitStack()
    with ctx:
        def sb(n, shape, dt=F32):
            return ctx.enter_context(nc.sbuf_tensor(name + n, shape, dt))

        sem = ctx.enter_context(semaphores(nc, name))

        def both(n):
            return [sem(n + "0"), sem(n + "1")]

        srow = sb("srow", [P, 2, G, P])
        stage = sb("stage", [P, 2, G, FIELDS])
        S, M = sb("S", [P, 2, G, P]), sb("M", [P, 2, G, P])
        SM = sb("SM", [P, 2, G, P])
        unused, count, off = sb("unused", [P, G, P]), sb("count", [P, G]), sb("off", [P, G])
        index = sb("index", [P, 2, G], I32)
        sums = sb("sums", [P, 2, G, F])
        part = sb("part", [P, 2, K0, F])
        total = sb("total", [P, 2, F])
        bias = sb("bias", [P, F])
        p_sm = [ctx.enter_context(nc.psum_tensor(name + f"psm{i}", [P, 4, P], F32)) for i in range(2)]
        p_sum = [ctx.enter_context(nc.psum_tensor(name + f"psum{i}", [P, 2, F], F32)) for i in range(4)]
        rows_in, parts_in = both("rows_in"), both("parts_in")
        added = [sem(f"added{k}") for k in range(K0)]
        chain, pace, bias_in, made, indexed, part_used = (sem(n) for n in ("chain", "pace", "bias_in", "made", "indexed", "part_used"))
        sm_done, sm_copied, sum_done, sum_copied = (sem(n) for n in ("sm_done", "sm_copied", "sum_done", "sum_copied"))
        LINKS = 4
        with nc.Block() as block:
            @block.sync
            def _(sp):
                sp.dma_start(bias[:, :], ins["L0_gnn_bias"].partition_broadcast(P)).then_inc(bias_in, 16)

                def load(it, u):
                    b = it * 2 + u
                    freed(sp, made, b - 1)
                    sp.dma_start(srow[:, u, :, :].rearrange("p g e -> p (g e)"),
                                 flat(t["src_step"][span(b * G, G), :]).partition_broadcast(P)).then_inc(rows_in[u], 16)

                batches(sp, load, 2)
                for k in range(K0):
                    sp.wait_ge(added[k], 16 * NBAT * (G // K0))

                def parts(it, u):
                    i = it * 2 + u
                    freed(sp, part_used, i - 1)
                    for k in range(K0):
                        sp.dma_start(part[:, u, k, :], t["sums"][k][span(i * P, P), :]).then_inc(parts_in[u], 16)

                tiles(sp, parts)

            @block.vector
            def _(dve):
                def batch(it, u):
                    b = it * 2 + u
                    link = Chain(dve, chain, b * LINKS)
                    link(nc.vector.tensor_copy(stage[:, u, :, :], t["edges"][:, span(b * G, G), :]))
                    freed(dve, sm_done, (b - 1) * 2)
                    dve.wait_ge(rows_in[u], it * 16 + 16)
                    nc.vector.tensor_tensor(S[:, u, :, :], stage[:, u, :, LOC].unsqueeze(2).to_broadcast([P, G, P]),
                                            t["col_no"][:, :].unsqueeze(1).to_broadcast([P, G, P]), ALU.is_equal)
                    for g in range(G):
                        nc.vector.tensor_scalar(M[:, u, g, :], srow[:, u, g, :], stage[:, u, g, SRC:SRC + 1],
                                                stage[:, u, g, W0:W0 + 1], ALU.is_equal, ALU.mult)
                    for g in range(G):
                        last = nc.vector.scalar_tensor_tensor(unused[:, g, :], srow[:, u, g, :], stage[:, u, g, SRC:SRC + 1],
                                                              t["earlier"][:, :], ALU.is_equal, ALU.mult, accum_out=count[:, g:g + 1])
                    last.then_inc(made, 1)
                    dve.wait_ge(made, b + 1)
                    link(nc.vector.tensor_tensor(off[:, :], t["spare_row"][:, :], stage[:, u, :, SRC], ALU.subtract))
                    link(nc.vector.tensor_scalar(count[:, :], count[:, :], 0.0, None, ALU.is_gt))
                    link(nc.vector.tensor_tensor(off[:, :], off[:, :], count[:, :], ALU.mult))
                    for k in range(K0):
                        freed(dve, added[k], (b - 1) * 16 * (G // K0))
                    nc.vector.tensor_tensor(index[:, u, :], off[:, :], stage[:, u, :, SRC], ALU.add).then_inc(indexed, 1)

                batches(dve, batch, 2)
                link = Chain(dve, chain, NBAT * LINKS)
                dve.wait_ge(bias_in, 16)
                link(nc.vector.tensor_tensor(t["x"][:, :, :], t["x"][:, :, :], bias[:, :].unsqueeze(1).to_broadcast([P, NT, F]), ALU.add))

                def add(it, u):
                    i = it * 2 + u
                    link = Chain(dve, chain, i * 2 + (NBAT * LINKS + 1))
                    dve.wait_ge(parts_in[u], it * 16 * K0 + 16 * K0)
                    link(nc.vector.tensor_tensor(part[:, u, 0:2, :], part[:, u, 0:2, :], part[:, u, 2:4, :], ALU.add))
                    link(nc.vector.tensor_tensor(total[:, u, :], part[:, u, 0, :], part[:, u, 1, :], ALU.add))
                    row = t["x"][:, at(i), :].rearrange("p a f -> p (a f)")
                    nc.vector.tensor_tensor(row, row, total[:, u, :], ALU.add).then_inc(part_used, 1)

                tiles(dve, add)

            @block.tensor
            def _(pe):
                def batch(it, u):
                    b = it * 2 + u
                    tile = tiles_of(nc, pe, t, b)
                    pe.wait_ge(made, b + 1)
                    for half in range(2):
                        freed(pe, sm_copied, b * 2 + (half - 1))
                        for g in range(4 * half, 4 * half + 4):
                            last = nc.tensor.matmul(p_sm[half][:, g % 4, :], S[:, u, g, :], M[:, u, g, :], start=True, stop=True)
                        last.then_inc(sm_done, 1)
                    for pair in range(4):
                        pe.wait_ge(sm_copied, b * 2 + (pair // 2 + 1))
                        freed(pe, sum_copied, b * 4 + (pair - 3))
                        for g in range(2 * pair, 2 * pair + 2):
                            last = nc.tensor.matmul(p_sum[pair][:, g % 2, :], SM[:, u, g, :],
                                                    t["agg"][:, bass.ds(tile[g], 1), 0:F].rearrange("p a f -> p (a f)"), start=True, stop=True)
                        last.then_inc(sum_done, 1)

                batches(pe, batch, 2)

            @block.scalar
            def _(act):
                def batch(it, u):
                    b = it * 2 + u
                    for half in range(2):
                        act.wait_ge(sm_done, b * 2 + (half + 1))
                        freed(act, sum_done, (b - 1) * 4)
                        nc.scalar.copy(SM[:, u, 4 * half:4 * half + 4, :], p_sm[half][:, :, :]).then_inc(sm_copied, 1)
                    for pair in range(4):
                        act.wait_ge(sum_done, b * 4 + (pair + 1))
                        for k in ((2 * pair) % K0, (2 * pair + 1) % K0):
                            freed(act, added[k], (b * 2 + (pair // 2 - 3)) * 16)
                        nc.scalar.copy(sums[:, u, 2 * pair:2 * pair + 2, :], p_sum[pair][:, :, :]).then_inc(sum_copied, 1)

                batches(act, batch, 2)

            @block.gpsimd
            def _(pool):
                def batch(it, u):
                    b = it * 2 + u
                    pool.wait_ge(indexed, b + 1)
                    for g in range(G):
                        k = g % K0
                        pool.wait_ge(sum_copied, b * 4 + (g // 2 + 1))
                        freed(pool, added[k], (b * 2 + g // K0) * 16)
                        pool.sem_inc(pace, 1)
                        nc.gpsimd.indirect_dma_start(t["sums"][k][:, :], bass.IndirectOffsetOnAxis(ap=index[:, u, g:g + 1], axis=0),
                                                     sums[:, u, g, :], None, compute_op=ALU.add).then_inc(added[k], 16)

                batches(pool, batch, 2)
                for k in range(K0):
                    pool.wait_ge(added[k], 16 * NBAT * (G // K0))


def relation_edges(nc, t, ins):
    name = "e1_"
    ctx = ExitStack()
    with ctx:
        def sb(n, shape, dt=F32):
            return ctx.enter_context(nc.sbuf_tensor(name + n, shape, dt))

        sem = ctx.enter_context(semaphores(nc, name))

        U = 4
        stage = sb("stage", [P, 2, G, FIELDS])
        S = sb("S", [P, 2, G, P])
        index = sb("index", [P, U, G], I32)
        rows = sb("rows", [P, U, G, F])
        p_sum = [ctx.enter_context(nc.psum_tensor(name + f"psum{i}", [P, 2, F], F32)) for i in range(4)]
        gathered = [[sem(f"gathered{u}_{g}") for g in range(G)] for u in range(U)]
        staged, pace, indexed, made, sum_done, zeroed, added = (
            sem(n) for n in ("staged", "pace", "indexed", "made", "sum_done", "zeroed", "added"))
        with nc.Block() as block:
            @block.gpsimd
            def _(pool):
                def batch(it, u):
                    b = it * U + u
                    pool.wait_ge(indexed, b + 1)
                    freed(pool, sum_done, (b - (U - 1)) * 4)
                    pool.sem_inc(pace, 1)
                    for g in range(G):
                        nc.gpsimd.indirect_dma_start(rows[:, u, g, :], None, t["msg_table"][:, :],
                                                     bass.IndirectOffsetOnAxis(ap=index[:, u, g:g + 1], axis=0)).then_inc(gathered[u][g], 16)

                batches(pool, batch, U)

            @block.vector
            def _(dve):
                nc.vector.memset(t["agg"][:, :, :], 0.0).then_inc(zeroed, 1)

                def look_up(it, u):
                    for g in range(G):
                        freed(dve, gathered[u][g], it * 16)
                    nc.vector.tensor_copy(index[:, u, :], t["edges"][:, span((it * U + u) * G, G), IDX1]).then_inc(indexed, 1)

                def one_hot(it, u):
                    b = it * U + u
                    nc.vector.tensor_copy(stage[:, u % 2, :, :], t["edges"][:, span(b * G, G), :]).then_inc(staged, 1)
                    dve.wait_ge(staged, b * 2 + 1)
                    freed(dve, sum_done, (b - 1) * 4)
                    wide = [P, G, P]
                    nc.vector.tensor_tensor(S[:, u % 2, :, :], stage[:, u % 2, :, LOC].unsqueeze(2).to_broadcast(wide),
                                            t["col_no"][:, :].unsqueeze(1).to_broadcast(wide), ALU.is_equal).then_inc(staged, 1)
                    dve.wait_ge(staged, b * 2 + 2)
                    nc.vector.tensor_tensor(S[:, u % 2, :, :], S[:, u % 2, :, :], stage[:, u % 2, :, W1].unsqueeze(2).to_broadcast(wide),
                                            ALU.mult).then_inc(made, 1)

                def batch(it, u):
                    b = it * U + u
                    tile = tiles_of(nc, dve, t, b)
                    if exists(b + 2):
                        look_up(it + (u + 2) // U, (u + 2) % U)
                    if exists(b + 1):
                        one_hot(it + (u + 1) // U, (u + 1) % U)
                    for g in range(G):
                        if g % 2 == 0:
                            dve.wait_ge(sum_done, b * 4 + (g // 2 + 1))
                        row = t["agg"][:, bass.ds(tile[g], 1), 0:F].rearrange("p a f -> p (a f)")
                        nc.vector.tensor_tensor(row, row, p_sum[g // 2][:, g % 2, :], ALU.add).then_inc(added, 1)
                        dve.wait_ge(added, b * G + (g + 1))

                dve.wait_ge(zeroed, 1)
                look_up(0, 0)
                look_up(0, 1)
                one_hot(0, 0)
                batches(dve, batch, U)
                nc.vector.scalar_tensor_tensor(t["x"][:, :, :], t["agg"][:, :, 0:F], 0.0, t["x"][:, :, :], ALU.max, ALU.add).then_inc(zeroed, 1)
                dve.wait_ge(zeroed, 2)

            @block.tensor
            def _(pe):
                def batch(it, u):
                    b = it * U + u
                    pe.wait_ge(made, b + 1)
                    for g in range(G):
                        if g % 2 == 0:
                            freed(pe, added, (b - 1) * G + (g + 2))
                        pe.wait_ge(gathered[u][g], it * 16 + 16)
                        last = nc.tensor.matmul(p_sum[g // 2][:, g % 2, :], S[:, u % 2, g, :], rows[:, u, g, :], start=True, stop=True)
                        if g % 2:
                            last.then_inc(sum_done, 1)

                batches(pe, batch, U)


def attention_edges(nc, t, ins, layer):
    name = f"a{layer}_"
    leaky = layer == 3
    ctx = ExitStack()
    with ctx:
        def sb(n, shape, dt=F32):
            return ctx.enter_context(nc.sbuf_tensor(name + n, shape, dt))

        def bank(n):
            return ctx.enter_context(nc.psum_tensor(name + n, [P, 512], F32))

        sem = ctx.enter_context(semaphores(nc, name))
        U = 4
        HG = H * G
        J = G + 1
        HJ = H * J
        V = slice(F, F + H)
        stage = sb("stage", [P, U, G, FIELDS])
        S, ST = sb("S", [P, U, G, P]), sb("ST", [P, G * P])
        index = sb("index", [P, U, G], I32)
        rows = sb("rows", [P, U, G, W])
        loc_row = sb("loc_row", [P, G * P])
        new_dst = sb("new_dst", [HJ, 2, P + 1])
        turned = sb("turned", [P, 2, H, J])
        up, top = sb("up", [HJ, P]), sb("top", [HJ, P])
        carried = sb("carried", [HJ, 2])
        split_up, split_down = sb("split_up", [1, 2, H, J]), sb("split_down", [1, 2, H, J])
        last_up, first_down = sb("last_up", [1, H, J]), sb("first_down", [1, H, J])
        join_up, join_down = sb("join_up", [1, 2, H, J]), sb("join_down", [1, HJ + 1])
        a = sb("a", [P, HG])
        z = sb("z", [P, 2, HG + H])
        growth = sb("growth", [1, H])
        scale = sb("scale", [P, H])
        bank_a, bank_top, bank_turn, bank_join = bank("bank_a"), bank("bank_top"), bank("bank_turn"), bank("bank_join")
        p_a, p_scale = bank_a[:, 0:HG], bank_a[:, HG:HG + H]
        p_top, p_turn = bank_top[:, 0:HJ], bank_turn[0:HJ, 0:P]
        p_last, p_first, p_carried = bank_join[0:1, 0:HJ], bank_join[0:1, HJ:2 * HJ], bank_join[0:HJ, 2 * HJ:2 * HJ + 2]
        p_sum = [bank(f"psum{i}") for i in range(4)]
        gathered = [sem(f"gathered{u}") for u in range(U)]
        loc_in, new_in = sem("loc_in"), [sem("new_in0"), sem("new_in1")]
        names = ["rows_set", "packed", "pace", "turn_pace", "indexed", "staged", "splits", "st_made", "st_half", "s_half", "made", "turned", "a_done",
                 "first_scans", "joined_in", "joined", "ends_turned", "carried_done", "carried_in", "up_done", "scanned", "top_done",
                 "c3", "z_ready", "exp_done", "weighed", "scale_done", "sum_done", "c5", "added", "zeroed"]
        s = {n: sem(n) for n in names}
        C3 = 3 if leaky else 1

        def flat1(ap):
            return ap.rearrange("p h j -> p (h j)")

        with nc.Block() as block:
            @block.sync
            def _(sp):
                def load(it, u):
                    b = it * U + u
                    freed(sp, s["scanned"], b - 1)
                    sp.dma_start(new_dst[:, u % 2, :], t["flag_rows"][span(b, 1)].rearrange("a h g e -> (a h g) e")).then_inc(new_in[u % 2], 16)
                    if leaky:
                        freed(sp, s["st_half"], b)
                        sp.dma_start(loc_row[:, :], flat(t["loc_step"][span(b * G, G), :]).partition_broadcast(P)).then_inc(loc_in, 16)

                batches(sp, load, U)

            @block.gpsimd
            def _(pool):
                nc.gpsimd.memset(rows[:, :, :, F:W], 0.0).then_inc(s["rows_set"], 1)
                pool.wait_ge(s["rows_set"], 1)

                def batch(it, u):
                    b = it * U + u
                    pool.wait_ge(s["indexed"], b + 1)
                    freed(pool, s["sum_done"], (b - (U - 1)) * G)
                    pool.sem_inc(s["pace"], 1)
                    for g in range(G):
                        nc.gpsimd.indirect_dma_start(rows[:, u, g, 0:F + H], None, t["head_table"][:, :],
                                                     bass.IndirectOffsetOnAxis(ap=index[:, u, g:g + 1], axis=0)).then_inc(gathered[u], 16)

                batches(pool, batch, U)

            @block.scalar
            def _(act):
                act.wait_ge(s["zeroed"], 7)

                def one_hots(it, u):
                    b = it * U + u
                    freed(act, s["z_ready"], (b - (U - 1)) * 2)
                    nc.scalar.copy(stage[:, u, :, :], t["edges"][:, span(b * G, G), :]).then_inc(s["staged"], 1)
                    freed(act, s["joined"], b - 1)
                    for k, (split, lo) in enumerate(((split_up, 1), (split_down, 0))):
                        last = nc.scalar.copy(split[:, u % 2, :, lo:lo + G], t["split_row"][0:1, k, span(b * G, G)].unsqueeze(1).to_broadcast([1, H, G]))
                    last.then_inc(s["splits"], 1)
                    act.wait_ge(s["staged"], b + 1)
                    freed(act, s["sum_done"], (b - (U - 1)) * G)
                    for g in range(G):
                        last = nc.scalar.activation(S[:, u, g, :], t["col_no"][:, :], ACT.Abs, bias=stage[:, u, g, LOC:LOC + 1], scale=-1.0)
                    last.then_inc(s["s_half"], 1)
                    if leaky:
                        act.wait_ge(loc_in, b * 16 + 16)
                        freed(act, s["a_done"], b)
                        nc.scalar.activation(ST[:, :], loc_row[:, :], ACT.Abs, bias=t["row_no"][:, 0:1], scale=-1.0).then_inc(s["st_half"], 1)
                    act.wait_ge(s["s_half"], b + 1)
                    nc.scalar.activation(S[:, u, :, :], S[:, u, :, :], ACT.Relu, bias=t["ones"][:, 0:1], scale=-1.0).then_inc(s["made"], 1)
                    if leaky:
                        act.wait_ge(s["st_half"], b + 1)
                        nc.scalar.activation(ST[:, :], ST[:, :], ACT.Relu, bias=t["ones"][:, 0:1], scale=-1.0).then_inc(s["st_made"], 1)

                def pack(it, u):
                    b = it * U + u
                    act.wait_ge(gathered[u], it * 16 * G + 16 * G)
                    freed(act, s["turned"], b - 1)
                    nc.scalar.copy(turned[:, u % 2, :, 0:G], rows[:, u, :, V].rearrange("p g h -> p h g")).then_inc(s["packed"], 1)

                def exponentials(it, u):
                    b = it * U + u
                    act.wait_ge(s["z_ready"], b * 2 + 2)
                    nc.scalar.activation(rows[:, u, :, V], z[:, 0, 0:HG].rearrange("p (g h) -> p g h", h=H), ACT.Exp).then_inc(s["exp_done"], 1)
                    nc.scalar.activation(z[0:1, 1, HG:], z[0:1, 0, HG:], ACT.Exp).then_inc(s["exp_done"], 1)

                def batch(it, u):
                    b = it * U + u
                    if exists(b + 2):
                        one_hots(it + (u + 2) // U, (u + 2) % U)
                        pack(it + (u + 2) // U, (u + 2) % U)
                    if exists(b + 1):
                        exponentials(it + (u + 1) // U, (u + 1) % U)

                one_hots(0, 0)
                pack(0, 0)
                one_hots(0, 1)
                pack(0, 1)
                exponentials(0, 0)
                batches(act, batch, U)

            @block.vector
            def _(dve):
                nc.vector.memset(t["agg"][:, :, :], 0.0).then_inc(s["zeroed"], 1)
                nc.vector.memset(z[:, :, :], 0.0).then_inc(s["zeroed"], 1)
                nc.vector.memset(join_up[:, :, :, :], -BIG).then_inc(s["zeroed"], 1)
                nc.vector.memset(turned[:, :, :, :], -BIG).then_inc(s["zeroed"], 1)
                nc.vector.memset(split_up[:, :, :, :], -BIG).then_inc(s["zeroed"], 1)
                nc.vector.memset(split_down[:, :, :, :], -BIG).then_inc(s["zeroed"], 1)
                nc.vector.memset(join_down[:, :], -BIG).then_inc(s["zeroed"], 1)

                def look_up(it, u):
                    freed(dve, gathered[u], it * 16 * G)
                    nc.vector.tensor_copy(index[:, u, :], t["edges"][:, span((it * U + u) * G, G), SRC]).then_inc(s["indexed"], 1)

                def scan_steps(it, u):
                    b = it * U + u
                    new = new_dst[:, u % 2, :]
                    dve.wait_ge(s["turned"], b + 1)
                    dve.wait_ge(new_in[u % 2], it * (16 * U // 2) + 16 * (u // 2 + 1))
                    nc.vector.tensor_tensor_scan(up[:, :], new[:, 0:P], p_turn, -BIG, ALU.add, ALU.max).then_inc(s["first_scans"], 1)
                    freed(dve, s["top_done"], b)
                    nc.vector.tensor_tensor_scan(top[:, ::-1], new[:, 1:P + 1][:, ::-1], p_turn[:, ::-1], -BIG, ALU.add, ALU.max).then_inc(s["first_scans"], 1)

                def join_steps(it, u):
                    b = it * U + u
                    dve.wait_ge(s["ends_turned"], b + 1)
                    dve.wait_ge(s["splits"], b + 1)
                    freed(dve, s["carried_done"], b)
                    nc.vector.tensor_copy(flat1(last_up[:, :, :])[:, 1:HJ], p_last[:, 0:HJ - 1]).then_inc(s["joined_in"], 1)
                    nc.vector.tensor_copy(flat1(first_down[:, :, :]), p_first).then_inc(s["joined_in"], 1)
                    dve.wait_ge(s["joined_in"], b * 5 + 2)
                    nc.vector.tensor_copy(last_up[:, :, 0], join_up[:, (u + 1) % 2, :, G]).then_inc(s["joined_in"], 1)
                    dve.wait_ge(s["joined_in"], b * 5 + 3)
                    nc.vector.tensor_tensor_scan(flat1(join_up[:, u % 2, :, :]), flat1(split_up[:, u % 2, :, :]), flat1(last_up[:, :, :]),
                                                 -BIG, ALU.add, ALU.max).then_inc(s["joined_in"], 1)
                    nc.vector.tensor_tensor_scan(join_down[:, 0:HJ][:, ::-1], flat1(split_down[:, u % 2, :, :])[:, ::-1],
                                                 flat1(first_down[:, :, :])[:, ::-1], -BIG, ALU.add, ALU.max).then_inc(s["joined_in"], 1)
                    dve.wait_ge(s["joined_in"], b * 5 + 5)
                    dve.sem_inc(s["joined"], 1)

                def scan_again(it, u):
                    b = it * U + u
                    new = new_dst[:, u % 2, :]
                    dve.wait_ge(s["carried_done"], b + 1)
                    nc.vector.tensor_copy(carried[:, :], p_carried).then_inc(s["carried_in"], 1)
                    dve.wait_ge(s["carried_in"], b + 1)
                    nc.vector.tensor_tensor_scan(up[:, :], new[:, 0:P], p_turn, carried[:, 0:1], ALU.add, ALU.max).then_inc(s["up_done"], 1)
                    dve.wait_ge(s["up_done"], b + 1)
                    nc.vector.tensor_tensor_scan(top[:, ::-1], new[:, 1:P + 1][:, ::-1], up[:, ::-1], carried[:, 1:2],
                                                 ALU.add, ALU.max).then_inc(s["scanned"], 1)
                    dve.wait_ge(s["scanned"], b + 1)

                def differences(it, u):
                    b = it * U + u
                    link = Chain(dve, s["c3"], b * C3)
                    dve.wait_ge(s["top_done"], b + 1)
                    dve.wait_ge(s["staged"], b + 1)
                    v = rows[:, u, :, V]
                    here, tops = z[:, 0, 0:HG].rearrange("p (g h) -> p g h", h=H), p_top.rearrange("p (h g) -> p g h", h=H)[:, 0:G, :]
                    top0, old = p_top[0:1, :].rearrange("p (h g) -> p h g", h=H)[:, :, 0], join_up[:, u % 2, :, 0]
                    nc.vector.tensor_tensor(rows[:, u, :, F + H:W], tops, stage[:, u, :, TAIL].unsqueeze(2).to_broadcast([P, G, H]), ALU.mult)
                    if not leaky:
                        link(nc.vector.tensor_tensor(z[0:1, 0, HG:], old, top0, ALU.min))
                        nc.vector.tensor_tensor(here, v, tops, ALU.subtract).then_inc(s["z_ready"], 1)
                        nc.vector.tensor_tensor(z[0:1, 0, HG:], z[0:1, 0, HG:], top0, ALU.subtract).then_inc(s["z_ready"], 1)
                        dve.wait_ge(s["z_ready"], b * 2 + 2)
                        return
                    link(nc.vector.tensor_copy(a[:, :], p_a))
                    by_step = a[:, :].rearrange("p (g h) -> p g h", h=H)
                    nc.vector.tensor_tensor(z[:, 1, 0:HG].rearrange("p (g h) -> p g h", h=H), tops, by_step, ALU.add)
                    nc.vector.tensor_tensor(z[0:1, 1, HG:], top0, a[0:1, 0:H], ALU.add)
                    nc.vector.tensor_tensor(z[0:1, 0, HG:], old, a[0:1, 0:H], ALU.add)
                    link(nc.vector.tensor_tensor(here, v, by_step, ALU.add))
                    link(nc.vector.scalar_tensor_tensor(z[:, :, :], z[:, :, :], 0.2, z[:, :, :], ALU.mult, ALU.max))
                    nc.vector.tensor_tensor(z[0:1, 0, HG:], z[0:1, 0, HG:], z[0:1, 1, HG:], ALU.min).then_inc(s["z_ready"], 1)
                    dve.wait_ge(s["z_ready"], b * 2 + 1)
                    nc.vector.tensor_tensor(z[:, 0, :], z[:, 0, :], z[:, 1, :], ALU.subtract).then_inc(s["z_ready"], 1)
                    dve.wait_ge(s["z_ready"], b * 2 + 2)

                def weigh(it, u):
                    b = it * U + u
                    dve.wait_ge(s["exp_done"], b * 2 + 2)
                    nc.vector.tensor_scalar_add(growth[:, :], z[0:1, 1, HG:], -1.0)
                    feats = rows[:, u, :, 0:F].rearrange("p g (h c) -> p g h c", h=H)
                    nc.vector.tensor_tensor(feats, feats, rows[:, u, :, V].unsqueeze(3).to_broadcast([P, G, H, C]), ALU.mult).then_inc(s["weighed"], 1)

                def add(it, u, tile, some):
                    b = it * U + u
                    link = Chain(dve, s["c5"], b * 2)
                    for g in some:
                        here = t["agg"][:, bass.ds(tile[g], 1), :].rearrange("p a f -> p (a f)")
                        if g == 0:
                            dve.wait_ge(s["scale_done"], b + 1)
                            link(nc.vector.tensor_scalar_add(scale[:, :], p_scale, 1.0))
                            old = here[:, 0:F].rearrange("p (h c) -> p h c", h=H)
                            nc.vector.tensor_tensor(old, old, scale[:, :].unsqueeze(2).to_broadcast([P, H, C]), ALU.mult)
                            link(nc.vector.tensor_tensor(here[:, V], here[:, V], scale[:, :], ALU.mult))
                        dve.wait_ge(s["sum_done"], b * G + (g + 1))
                        nc.vector.tensor_tensor(here, here, p_sum[g % 4][:, 0:W], ALU.add).then_inc(s["added"], 1)
                        dve.wait_ge(s["added"], b * G + (g + 1))

                def ahead(it, u, by):
                    return it + (u + by) // U, (u + by) % U

                def batch(it, u):
                    b = it * U + u
                    tile = tiles_of(nc, dve, t, b)
                    if exists(b + 3):
                        look_up(*ahead(it, u, 3))
                    weigh(it, u)
                    if exists(b + 1):
                        join_steps(*ahead(it, u, 1))
                    add(it, u, tile, range(0, G // 2))
                    if exists(b + 1):
                        scan_again(*ahead(it, u, 1))
                    add(it, u, tile, range(G // 2, G))
                    if exists(b + 1):
                        differences(*ahead(it, u, 1))
                    if exists(b + 2):
                        scan_steps(*ahead(it, u, 2))

                dve.wait_ge(s["zeroed"], 7)
                for u in range(3):
                    look_up(0, u)
                scan_steps(0, 0)
                join_steps(0, 0)
                scan_again(0, 0)
                differences(0, 0)
                scan_steps(0, 1)
                batches(dve, batch, U)

            @block.tensor
            def _(pe):
                def turn(it, u):
                    pe.wait_ge(s["packed"], it * U + u + 1)
                    pe.sem_inc(s["turn_pace"], 1)
                    nc.tensor.transpose(p_turn, turned[:, u % 2, :, :].rearrange("p h g -> p (h g)"), t["ident"][:, :]).then_inc(s["turned"], 1)

                def dst_scores(it, u):
                    b = it * U + u
                    tile = tiles_of(nc, pe, t, b)
                    pe.wait_ge(s["st_made"], b + 1)
                    freed(pe, s["c3"], (b - 1) * C3 + 1 if not isinstance(b, int) or b else 0)
                    for g in range(G):
                        last = nc.tensor.matmul(p_a[:, g * H:(g + 1) * H], ST[:, g * P:(g + 1) * P],
                                                t["dst_score"][:, bass.ds(tile[g], 1), :].rearrange("p a h -> p (a h)"), start=True, stop=True)
                    last.then_inc(s["a_done"], 1)

                def turn_ends(it, u):
                    b = it * U + u
                    pe.wait_ge(s["first_scans"], b * 2 + 2)
                    pe.sem_inc(s["turn_pace"], 1)
                    nc.tensor.transpose(p_last, up[:, P - 1:P], t["ident"][0:HJ, 0:HJ])
                    nc.tensor.transpose(p_first, top[:, 0:1], t["ident"][0:HJ, 0:HJ]).then_inc(s["ends_turned"], 1)

                def turn_joined(it, u):
                    b = it * U + u
                    pe.wait_ge(s["joined"], b + 1)
                    pe.sem_inc(s["turn_pace"], 1)
                    nc.tensor.transpose(p_carried[:, 0:1], flat1(join_up[:, u % 2, :, :]), t["ident"][0:1, 0:1])
                    nc.tensor.transpose(p_carried[:, 1:2], join_down[:, 1:HJ + 1], t["ident"][0:1, 0:1]).then_inc(s["carried_done"], 1)

                def turn_maxima(it, u):
                    b = it * U + u
                    pe.wait_ge(s["scanned"], b + 1)
                    pe.sem_inc(s["turn_pace"], 1)
                    nc.tensor.transpose(p_top, top[:, :], t["ident"][0:HJ, 0:HJ]).then_inc(s["top_done"], 1)

                def sums(it, u, some):
                    b = it * U + u
                    for g in some:
                        if g == 0:
                            pe.wait_ge(s["made"], b + 1)
                            pe.wait_ge(s["weighed"], b + 1)
                            nc.tensor.matmul(p_scale, S[0:1, u, 0, :], growth[:, :], start=True, stop=True).then_inc(s["scale_done"], 1)
                        freed(pe, s["added"], b * G + (g - 3))
                        nc.tensor.matmul(p_sum[g % 4][:, 0:W], S[:, u, g, :], rows[:, u, g, :], start=True, stop=True).then_inc(s["sum_done"], 1)

                def batch(it, u):
                    b = it * U + u
                    one, two = (it + (u + 1) // U, (u + 1) % U), (it + (u + 2) // U, (u + 2) % U)
                    if exists(b + 1):
                        turn_ends(*one)
                        if leaky:
                            dst_scores(*one)
                    sums(it, u, range(0, G // 2))
                    if exists(b + 1):
                        turn_joined(*one)
                    sums(it, u, range(G // 2, G))
                    if exists(b + 1):
                        turn_maxima(*one)
                    if exists(b + 2):
                        turn(*two)

                turn(0, 0)
                turn_ends(0, 0)
                if leaky:
                    dst_scores(0, 0)
                turn_joined(0, 0)
                turn_maxima(0, 0)
                turn(0, 1)
                batches(pe, batch, U)


def finish_global(nc, t, ins):
    ctx = ExitStack()
    with ctx:
        def sb(n, shape, dt=F32):
            return ctx.enter_context(nc.sbuf_tensor("f2_" + n, shape, dt))

        sem = ctx.enter_context(semaphores(nc, "f2_"))

        h = sb("h", [P, NT, F])
        bias = sb("bias", [P, F])
        m, own, q, top, low = (sb(n, [P, NT, H]) for n in ("m", "own", "q", "top", "low"))
        best, best_all, part, inv = (sb(n, [P, H]) for n in ("best", "best_all", "part", "inv"))
        pz = ctx.enter_context(nc.psum_tensor("f2_pz", [P, 512], F32))
        h_in, bias_in, chain, best_ready, all_ready, exp_in, exp_out, part_ready, z_ready = (
            sem(n) for n in ("h_in", "bias_in", "chain", "best_ready", "all_ready", "exp_in", "exp_out", "part_ready", "z_ready"))
        everywhere = [P, NT, H]
        with nc.Block() as block:
            @block.sync
            def _(sp):
                sp.dma_start(h[:, :, :], t["head_table"].rearrange("(t p) f -> p t f", p=P)[:, :, 0:F]).then_inc(h_in, 16)
                sp.dma_start(bias[:, :], ins["L2_gnn_b"].partition_broadcast(P)).then_inc(bias_in, 16)

            @block.vector
            def _(dve):
                link = Chain(dve, chain)
                agg, x = t["agg"], t["x"]
                den, tail = agg[:, :, F:F + H], agg[:, :, F + H:W]
                link(nc.vector.tensor_scalar(m[:, :, :], den, 0.0, -BIG, ALU.is_equal, ALU.mult))
                link(nc.vector.tensor_tensor(m[:, :, :], m[:, :, :], tail, ALU.add))
                link(nc.vector.tensor_tensor(top[:, :, :], m[:, :, :], t["src_score"][:, :, :], ALU.max))
                link(nc.vector.tensor_tensor(m[:, :, :], m[:, :, :], top[:, :, :], ALU.subtract))
                nc.vector.tensor_tensor(own[:, :, :], t["src_score"][:, :, :], top[:, :, :], ALU.subtract).then_inc(exp_in, 1)
                link(nc.vector.tensor_tensor(q[:, :, :], top[:, :, :], t["dst_score"][:, :, :], ALU.add))
                link(nc.vector.tensor_tensor(q[:, :, :], q[:, :, :], t["valid"][:, :].rearrange("p (t h) -> p t h", h=H), ALU.add))
                nc.vector.tensor_reduce(best[:, :], q[:, :, :].rearrange("p t h -> p h t"), AX.X, ALU.max).then_inc(best_ready, 1)
                dve.wait_ge(all_ready, 1)
                nc.vector.tensor_tensor(q[:, :, :], q[:, :, :], best_all[:, :].unsqueeze(1).to_broadcast(everywhere), ALU.subtract).then_inc(exp_in, 1)
                dve.wait_ge(exp_out, 3)
                link(nc.vector.tensor_tensor(low[:, :, :], den, m[:, :, :], ALU.mult))
                link(nc.vector.tensor_tensor(low[:, :, :], low[:, :, :], own[:, :, :], ALU.add))
                link(nc.vector.tensor_tensor(low[:, :, :], low[:, :, :], q[:, :, :], ALU.mult))
                nc.vector.reduce_sum(part[:, :], low[:, :, :].rearrange("p t h -> p h t"), AX.X).then_inc(part_ready, 1)
                dve.wait_ge(z_ready, 1)
                link(nc.vector.reciprocal(inv[:, :], pz[:, 0:H]))
                link(nc.vector.tensor_tensor(q[:, :, :], q[:, :, :], inv[:, :].unsqueeze(1).to_broadcast(everywhere), ALU.mult))
                link(nc.vector.tensor_tensor(m[:, :, :], m[:, :, :], q[:, :, :], ALU.mult))
                link(nc.vector.tensor_tensor(own[:, :, :], own[:, :, :], q[:, :, :], ALU.mult))

                def by_head(x_):
                    return x_.rearrange("p t (h c) -> p t h c", h=H)

                heads = [P, NT, H, C]
                feats = agg[:, :, 0:F]
                dve.wait_ge(h_in, 16)
                dve.wait_ge(bias_in, 16)
                link(nc.vector.tensor_tensor(by_head(feats), by_head(feats), m[:, :, :].unsqueeze(3).to_broadcast(heads), ALU.mult))
                link(nc.vector.tensor_tensor(by_head(h[:, :, :]), by_head(h[:, :, :]), own[:, :, :].unsqueeze(3).to_broadcast(heads), ALU.mult))
                link(nc.vector.tensor_tensor(h[:, :, :], h[:, :, :], feats, ALU.add))
                link(nc.vector.tensor_tensor(h[:, :, :], h[:, :, :], bias[:, :].unsqueeze(1).to_broadcast([P, NT, F]), ALU.add))
                link(nc.vector.tensor_tensor(x[:, :, :], x[:, :, :], h[:, :, :], ALU.add))

            @block.gpsimd
            def _(pool):
                pool.wait_ge(best_ready, 1)
                nc.gpsimd.partition_all_reduce(best_all[:, :], best[:, :], P, RMAX).then_inc(all_ready, 1)

            @block.scalar
            def _(act):
                act.wait_ge(exp_in, 1)
                nc.scalar.activation(m[:, :, :], m[:, :, :], ACT.Exp).then_inc(exp_out, 1)
                nc.scalar.activation(own[:, :, :], own[:, :, :], ACT.Exp).then_inc(exp_out, 1)
                act.wait_ge(exp_in, 2)
                nc.scalar.activation(q[:, :, :], q[:, :, :], ACT.Exp).then_inc(exp_out, 1)

            @block.tensor
            def _(pe):
                pe.wait_ge(part_ready, 1)
                nc.tensor.matmul(pz[:, 0:H], t["ones"][:, :], part[:, :], start=True, stop=True).then_inc(z_ready, 1)


def finish_local(nc, t, ins):
    ctx = ExitStack()
    with ctx:
        bias = ctx.enter_context(nc.sbuf_tensor("f3_bias", [P, F], F32))
        inv = ctx.enter_context(nc.sbuf_tensor("f3_inv", [P, NT, H], F32))
        sem = ctx.enter_context(semaphores(nc, "f3_"))
        bias_in, chain = sem("bias_in"), sem("chain")
        with nc.Block() as block:
            @block.sync
            def _(sp):
                sp.dma_start(bias[:, :], ins["L3_gnn_bias"].partition_broadcast(P)).then_inc(bias_in, 16)

            @block.vector
            def _(dve):
                link = Chain(dve, chain)
                agg, x = t["agg"], t["x"]
                feats = agg[:, :, 0:F]
                by_head = feats.rearrange("p t (h c) -> p t h c", h=H)
                link(nc.vector.tensor_scalar_add(inv[:, :, :], agg[:, :, F:F + H], 1e-16))
                link(nc.vector.reciprocal(inv[:, :, :], inv[:, :, :]))
                link(nc.vector.tensor_tensor(by_head, by_head, inv[:, :, :].unsqueeze(3).to_broadcast([P, NT, H, C]), ALU.mult))
                dve.wait_ge(bias_in, 16)
                link(nc.vector.tensor_tensor(feats, feats, bias[:, :].unsqueeze(1).to_broadcast([P, NT, F]), ALU.add))
                link(nc.vector.scalar_tensor_tensor(x[:, :, :], feats, 0.0, x[:, :, :], ALU.max, ALU.add))


def program(nc, ins, out):
    ctx = ExitStack()
    with ctx:
        def sb(name, shape, dt=F32):
            return ctx.enter_context(nc.sbuf_tensor(name, shape, dt))

        def dram(name, shape, dt=F32):
            return nc.dram_tensor(name, shape, dt, kind="Internal").ap()

        t = {
            "x": sb("x", [P, NT, F]),
            "edges": sb("edges", [P, NSR, FIELDS]),
            "split_row": sb("split_row", [1, 2, NSR]),
            "split_dram": dram("split_dram", (2, NSR)), "flag_rows": dram("flag_rows", (NBAT, H, G + 1, P + 1)),
            "tile_row": sb("tile_row", [1, NSR], I32),
            "ones": sb("ones", [P, P]), "ident": sb("ident", [P, P]), "earlier": sb("earlier", [P, P]),
            "col_no": sb("col_no", [P, P]), "row_no": sb("row_no", [P, G]), "spare_row": sb("spare_row", [P, G]),
            "valid": sb("valid", [P, NT * H]),
            "dst_blk": dram("dst_blk", (NB, P), I32), "src_blk": dram("src_blk", (NB, P), I32),
            "type_blk": dram("type_blk", (NB, P), I32),
            "w0_blk": dram("w0_blk", (NB, P)), "w1_blk": dram("w1_blk", (NB, P)),
            "tile_dram": dram("tile_dram", (NSR,), I32),
            "dst_step": dram("dst_step", (NSR * P + 1,)), "flag_step": dram("flag_step", (NSR * P + 1,)),
            "loc_step": dram("loc_step", (NSR, P)), "src_step": dram("src_step", (NSR, P)),
        }
        t["agg"] = sb("agg", [P, NT, W])
        t["dst_score"], t["src_score"] = sb("dst_score", [P, NT, H]), sb("src_score", [P, NT, H])
        t["msg_table"] = dram("msg_table", (R * NP, F))
        t["sums"] = [dram(f"sums{k}", (NP + P, F)) for k in range(K0)]
        t["head_table"] = dram("head_table", (NP, F + H))
        prepare(nc, t, ins)
        nodes(nc, t, ins, 0)
        scatter_edges(nc, t, ins)
        nodes(nc, t, ins, 1)
        relation_edges(nc, t, ins)
        nodes(nc, t, ins, 2)
        attention_edges(nc, t, ins, 2)
        finish_global(nc, t, ins)
        nodes(nc, t, ins, 3)
        attention_edges(nc, t, ins, 3)
        finish_local(nc, t, ins)
        with nc.semaphore("stored") as stored, nc.Block() as block:
            @block.sync
            def _(sp):
                sp.dma_start(out[0:(NT - 1) * P, :].rearrange("(t p) f -> p t f", p=P), t["x"][:, 0:NT - 1, :]).then_inc(stored, 16)
                sp.dma_start(out[(NT - 1) * P:N, :], t["x"][0:LAST, NT - 1, :]).then_inc(stored, 16)
                sp.wait_ge(stored, 32)


INPUTS = ["x", "src", "dst", "edge_type_16", "edge_weight", "edge_weight1", "L0_gnn_weight", "L0_gnn_bias",
          "L1_gnn_weight", "L1_gnn_gate_weight", "L2_gnn_W", "L2_gnn_att", "L2_gnn_b", "L3_gnn_W",
          "L3_gnn_att_src", "L3_gnn_att_dst", "L3_gnn_bias"]


def kernel(**inputs):
    import numpy as np
    import concourse.bacc as bacc
    from concourse.bass_utils import run_bass_kernel_spmd

    nc = bacc.Bacc("TRN2", target_bir_lowering=False, num_devices=1)
    arrays, ins = {}, {}
    for name in INPUTS:
        a = np.ascontiguousarray(inputs[name])
        arrays[f"in_{name}"] = a
        ins[name] = nc.dram_tensor(f"in_{name}", a.shape, mybir.dt.from_np(a.dtype), kind="ExternalInput").ap()
    out = nc.dram_tensor("result", (N, F), F32, kind="ExternalOutput").ap()
    program(nc, ins, out)
    return run_bass_kernel_spmd(nc, [arrays], core_ids=[0]).results[0]["result"]
```

```python
from contextlib import ExitStack, contextmanager

import concourse.bass as bass
from concourse import mybir

F32 = mybir.dt.float32
I32 = mybir.dt.int32
BF16 = mybir.dt.bfloat16
ALU = mybir.AluOpType
ACT = mybir.ActivationFunctionType
AX = mybir.AxisListType
RMAX = bass.bass_isa.ReduceOp.max

P = 128
N, E, F, R = 6250, 100000, 256, 16
NT = (N + P - 1) // P
NP = NT * P
LAST = N - (NT - 1) * P
NB = 784
BP = 7
SC = 7
NSR = SC * P
G = 8
NBAT = (NB + NT - 1 + G - 1) // G
NBAT += -NBAT % 4
K0 = 4
H = 8
C = F // H
W = F + 2 * H
BIG = 1e30
FIELDS = 6
LOC, SRC, IDX1, W0, W1, TAIL = range(FIELDS)


class Chain:

    def __init__(self, eng, sem, n=0):
        self.eng, self.sem, self.n = eng, sem, n

    def __call__(self, ins):
        self.n = self.n + 1
        ins.then_inc(self.sem, 1)
        self.eng.wait_ge(self.sem, self.n)


@contextmanager
def semaphores(nc, prefix):
    held = []

    def sem(name):
        held.append(nc.alloc_semaphore(name=prefix + name))
        return held[-1]

    yield sem
    nc.clear_and_free_semaphores(held)
    nc.all_engine_barrier()


def freed(eng, sem, value):
    if not isinstance(value, int) or value > 0:
        eng.wait_ge(sem, value)


def at(i):
    return slice(i, i + 1) if isinstance(i, int) else bass.ds(i, 1)


def span(start, n):
    return slice(start, start + n) if isinstance(start, int) else bass.ds(start, n)


def batches(eng, body, unroll):
    for u in range(unroll):
        body(0, u)
    with eng.Fori(1, NBAT // unroll - 1) as it:
        for u in range(unroll):
            body(it, u)
    for u in range(unroll):
        body(NBAT // unroll - 1, u)


def exists(b):
    return not isinstance(b, int) or b < NBAT


def tiles_of(nc, eng, t, b):
    _, values = nc.values_load_multi_w_load_instructions(
        t["tile_row"][0:1, span(b * G, G)], engines=(eng.engine,), min_val=0, max_val=NT - 1,
        skip_runtime_bounds_check_because="a step's tile counts at most NT - 1 tile ends")
    return values


def tiles(eng, body):
    body(0, 0)
    body(0, 1)
    with eng.Fori(1, NT // 2) as it:
        body(it, 0)
        body(it, 1)
    body(NT // 2, 0)


def flat(ap):
    return ap.rearrange("a b -> (a b)")


def prepare(nc, t, ins):
    ctx = ExitStack()
    with ctx:
        def sb(name, shape, dt=F32):
            return ctx.enter_context(nc.sbuf_tensor("prep_" + name, shape, dt))

        sem = ctx.enter_context(semaphores(nc, "prep_"))

        blocks = sb("blocks", [NB // BP, BP, P], I32)
        pad_dst, pad_zero = sb("pad_dst", [1, NB * P - E], I32), sb("pad_zero", [1, NB * P - E], I32)
        lastf = sb("lastf", [NB // BP, BP])
        limit = sb("limit", [P, NT - 1])
        tile_no = sb("tile_no", [P, NT - 1])
        below = sb("below", [P, NT - 1, BP])
        count = sb("count", [P, NT - 1])
        leave = sb("leave", [P, NT - 1])
        step_no = sb("step_no", [P, SC])
        passed = sb("passed", [P, SC, NT - 1])
        tile_of, tile_base = sb("tile_of", [P, SC]), sb("tile_base", [P, SC])
        blockf, block_of = sb("blockf", [P, SC]), sb("block_of", [P, SC], I32)
        tile_i = sb("tile_i", [SC, P], I32)
        raw = [sb(f"raw{k}", [P, SC, P], I32) for k in range(3)]
        rows = [sb(f"rows{k}", [P, SC, P]) for k in range(FIELDS)]
        dstf = sb("dstf", [P, SC, P])
        here, before = sb("here", [P, NSR]), sb("before", [P, NSR])
        flags = sb("flags", [P, SC, P])
        split, split_c = sb("split", [P, 2, SC]), sb("split_c", [SC, 2, P])
        edge_pad = sb("edge_pad", [1, 2])
        ps = [ctx.enter_context(nc.psum_tensor(f"prep_ps{i}", [P, 1024], F32)) for i in range(2)]
        pc = ctx.enter_context(nc.psum_tensor("prep_pc", [P, 512], F32))
        names = ["copied", "padded", "pads", "blocks", "consts", "zeroed", "counted", "dve", "steps_ready",
                 "rows_in", "by_step_out", "by_step", "shifted", "flags_out", "flags", "tails", "ready_t", "tps", "turned", "taken",
                 "tile_t", "tile_c", "tile_out", "tile_in", "x_in", "xz", "pool", "flag_set",
                 "rep", "split_t", "split_out", "split_min", "split_p"]
        s = {n: sem(n) for n in names}
        scr = [t["dst_blk"], t["src_blk"], t["type_blk"], t["w0_blk"], t["w1_blk"]]
        src_in = [ins["dst"], ins["src"], ins["edge_type_16"], ins["edge_weight"], flat(ins["edge_weight1"])]
        with nc.Block() as block:
            @block.sync
            def _(sp):
                for a, b in zip(scr, src_in):
                    sp.dma_start(flat(a)[0:E].rearrange("(a b) -> a b", a=16), b.rearrange("(a b) -> a b", a=16)).then_inc(s["copied"], 16)
                sp.wait_ge(s["pads"], 2)
                for k, a in enumerate(scr):
                    pad = pad_dst if k == 0 else pad_zero
                    pad = pad[:, :] if k < 3 else pad[:, :].bitcast(F32)
                    sp.dma_start(flat(a)[E:NB * P].unsqueeze(0), pad).then_inc(s["padded"], 16)
                sp.wait_ge(s["copied"], 5 * 16)
                sp.wait_ge(s["padded"], 5 * 16)
                sp.dma_start(blocks[:, :, :], t["dst_blk"].rearrange("(p j) e -> p j e", j=BP)).then_inc(s["blocks"], 16)
                sp.wait_ge(s["xz"], 1)
                xin = ins["x"]
                sp.dma_start(t["x"][:, 0:NT - 1, :], xin[0:(NT - 1) * P, :].rearrange("(t p) f -> p t f", p=P)).then_inc(s["x_in"], 16)
                sp.dma_start(t["x"][0:LAST, NT - 1, :], xin[(NT - 1) * P:N, :]).then_inc(s["x_in"], 16)
                sp.wait_ge(s["tile_c"], 1)
                sp.dma_start(t["tile_dram"].rearrange("(c p) -> c p", p=P), tile_i[:, :]).then_inc(s["tile_out"], 16)
                sp.wait_ge(s["tile_out"], 16)
                sp.dma_start(t["tile_row"][:, :], t["tile_dram"].unsqueeze(0)).then_inc(s["tile_in"], 16)
                sp.wait_ge(s["by_step"], 1)
                d = t["dst_step"]
                sp.dma_start(d[1:1 + NSR * P].rearrange("(c p e) -> p c e", p=P, e=P), dstf[:, :, :]).then_inc(s["by_step_out"], 16)
                sp.dma_start(d[0:1].unsqueeze(0), edge_pad[:, 0:1]).then_inc(s["by_step_out"], 16)
                for k, name in ((LOC, "loc_step"), (SRC, "src_step")):
                    sp.dma_start(t[name].rearrange("(c p) e -> p c e", p=P), rows[k][:, :, :]).then_inc(s["by_step_out"], 16)
                sp.wait_ge(s["by_step_out"], 4 * 16)
                sp.dma_start(here[:, :], d[1:1 + NSR * P].rearrange("(p j) -> p j", p=P)).then_inc(s["shifted"], 16)
                sp.dma_start(before[:, :], d[0:NSR * P].rearrange("(p j) -> p j", p=P)).then_inc(s["shifted"], 16)
                sp.wait_ge(s["flag_set"], 1)
                f = t["flag_step"]
                sp.dma_start(f[0:NSR * P].rearrange("(p j) -> p j", p=P), here[:, :]).then_inc(s["flags_out"], 16)
                sp.dma_start(f[NSR * P:NSR * P + 1].unsqueeze(0), edge_pad[:, 1:2]).then_inc(s["flags_out"], 16)
                sp.wait_ge(s["flags_out"], 2 * 16)
                sp.dma_start(rows[TAIL][:, :, :], f[1:1 + NSR * P].rearrange("(c p e) -> p c e", p=P, e=P)).then_inc(s["tails"], 16)
                rep = t["flag_rows"]
                nf = NBAT * G * P
                sp.dma_start(rep[:, 0, 0:G, 0:P], f[0:nf].rearrange("(b g e) -> b g e", g=G, e=P)).then_inc(s["rep"], 16)
                sp.dma_start(rep[:, 0, 0:G, P:P + 1], f[1:1 + nf].rearrange("(b g e) -> b g e", g=G, e=P)[:, :, P - 1:P],
                             allow_slow_non_contiguous=True).then_inc(s["rep"], 16)
                sp.dma_start(rep[:, 0, G, :], f[0:nf].rearrange("(b e) -> b e", e=G * P)[:, 0:P + 1]).then_inc(s["rep"], 16)
                sp.wait_ge(s["rep"], 48)
                for h in range(1, H):
                    sp.dma_start(rep[:, h, :, :], rep[:, 0, :, :]).then_inc(s["rep"], 16)
                sp.dma_start(flags[:, :, :], f[0:NSR * P].rearrange("(c p e) -> p c e", p=P, e=P)).then_inc(s["flags"], 16)
                for k in range(2):
                    sp.wait_ge(s["split_t"], k + 1)
                    sp.dma_start(t["split_dram"][k].rearrange("(c p) -> c p", p=P), split_c[:, k, :]).then_inc(s["split_out"], 16)
                sp.wait_ge(s["split_out"], 32)
                sp.dma_start(t["split_row"][0:1, :, :].rearrange("a k s -> a (k s)"), t["split_dram"].rearrange("k s -> (k s)").unsqueeze(0)).then_inc(s["split_out"], 16)
                sp.wait_ge(s["split_out"], 48)
                sp.wait_ge(s["rep"], (H + 2) * 16)
                sp.wait_ge(s["tails"], 16)
                sp.wait_ge(s["tile_in"], 16)
                sp.wait_ge(s["x_in"], 32)

            @block.gpsimd
            def _(pool):
                nc.gpsimd.memset(pad_dst[:, :], 8191).then_inc(s["pads"], 1)
                nc.gpsimd.memset(pad_zero[:, :], 0).then_inc(s["pads"], 1)
                nc.gpsimd.memset(edge_pad[:, 0:1], -1.0).then_inc(s["zeroed"], 1)
                nc.gpsimd.memset(edge_pad[:, 1:2], -BIG).then_inc(s["zeroed"], 1)
                nc.gpsimd.memset(t["ones"][:, :], 1.0).then_inc(s["zeroed"], 1)
                nc.gpsimd.memset(t["ident"][:, :], 0.0).then_inc(s["zeroed"], 1)
                nc.gpsimd.memset(t["valid"][:, :], 0.0).then_inc(s["zeroed"], 1)
                kw = dict(allow_small_or_imprecise_dtypes=True)
                nc.gpsimd.iota(limit[:, :], [[P, NT - 1]], base=P, channel_multiplier=0, **kw).then_inc(s["consts"], 1)
                nc.gpsimd.iota(tile_no[:, :], [[1, NT - 1]], base=0, channel_multiplier=0, **kw).then_inc(s["consts"], 1)
                nc.gpsimd.iota(step_no[:, :], [[P, SC]], base=0, channel_multiplier=1, **kw).then_inc(s["consts"], 1)
                nc.gpsimd.iota(t["col_no"][:, :], [[1, P]], base=0, channel_multiplier=0, **kw).then_inc(s["consts"], 1)
                nc.gpsimd.iota(t["row_no"][:, :], [[0, G]], base=0, channel_multiplier=1, **kw).then_inc(s["consts"], 1)
                nc.gpsimd.iota(t["spare_row"][:, :], [[0, G]], base=NP, channel_multiplier=1, **kw).then_inc(s["consts"], 1)
                pool.wait_ge(s["zeroed"], 5)
                nc.gpsimd.affine_select(out=t["ident"][:, :], in_=t["ident"][:, :], compare_op=ALU.not_equal, fill=1.0,
                                        base=0, pattern=[[-1, P]], channel_multiplier=1).then_inc(s["consts"], 1)
                nc.gpsimd.affine_select(out=t["earlier"][:, :], in_=t["ones"][:, :], compare_op=ALU.is_gt, fill=0.0,
                                        base=0, pattern=[[-1, P]], channel_multiplier=1).then_inc(s["consts"], 1)
                v = t["valid"][:, (NT - 1) * H:NT * H]
                nc.gpsimd.affine_select(out=v, in_=v, compare_op=ALU.is_ge, fill=-BIG,
                                        base=LAST - 1, pattern=[[0, H]], channel_multiplier=-1).then_inc(s["consts"], 1)
                pool.wait_ge(s["steps_ready"], 1)
                pool.wait_ge(s["padded"], 5 * 16)
                dest = [raw[0], raw[1], raw[2], rows[W0], rows[W1]]
                for c in range(SC):
                    for a, d in zip(scr, dest):
                        nc.gpsimd.indirect_dma_start(d[:, c, :], None, a[:, :], bass.IndirectOffsetOnAxis(ap=block_of[:, c:c + 1], axis=0)).then_inc(s["rows_in"], 16)
                pool.wait_ge(s["rows_in"], 5 * SC * 16)

            @block.vector
            def _(dve):
                link = Chain(dve, s["dve"])
                nc.vector.memset(t["x"][:, NT - 1, :], 0.0).then_inc(s["xz"], 1)
                dve.wait_ge(s["blocks"], 16)
                dve.wait_ge(s["consts"], 9)
                link(nc.vector.tensor_copy(lastf[:, :], blocks[:, :, P - 1]))
                nb = NB // BP
                link(nc.vector.tensor_tensor(below[0:nb], lastf[:, :].unsqueeze(1).to_broadcast([nb, NT - 1, BP]),
                                             limit[0:nb, :].unsqueeze(2).to_broadcast([nb, NT - 1, BP]), ALU.is_lt))
                link(nc.vector.reduce_sum(count[0:nb, :], below[0:nb], AX.X))
                nc.vector.tensor_copy(count[0:nb, 0:1], count[0:nb, 0:1]).then_inc(s["ready_t"], 1)
                dve.wait_ge(s["counted"], 1)
                link(nc.vector.tensor_tensor(leave[:, :], pc[:, 0:NT - 1], tile_no[:, :], ALU.add))
                link(nc.vector.tensor_tensor(passed[:, :, :], leave[:, :].unsqueeze(1).to_broadcast([P, SC, NT - 1]),
                                             step_no[:, :].unsqueeze(2).to_broadcast([P, SC, NT - 1]), ALU.is_lt))
                link(nc.vector.reduce_sum(tile_of[:, :], passed[:, :, :], AX.X))
                link(nc.vector.tensor_tensor(blockf[:, :], step_no[:, :], tile_of[:, :], ALU.subtract))
                nc.vector.tensor_scalar_min(block_of[:, :], blockf[:, :], float(NB - 1)).then_inc(s["steps_ready"], 1)
                link(nc.vector.tensor_scalar_mul(tile_base[:, :], tile_of[:, :], float(P)))
                dve.wait_ge(s["tile_t"], 1)
                nc.vector.tensor_copy(tile_i[:, :], pc[0:SC, 256:256 + P]).then_inc(s["tile_c"], 1)
                dve.wait_ge(s["rows_in"], 5 * SC * 16)
                link(nc.vector.tensor_copy(dstf[:, :, :], raw[0][:, :, :]))
                link(nc.vector.tensor_copy(rows[SRC][:, :, :], raw[1][:, :, :]))
                link(nc.vector.tensor_tensor(rows[LOC][:, :, :], dstf[:, :, :], tile_base[:, :].unsqueeze(2).to_broadcast([P, SC, P]), ALU.subtract))
                nc.vector.scalar_tensor_tensor(rows[IDX1][:, :, :], raw[2][:, :, :], float(NP), rows[SRC][:, :, :], ALU.mult, ALU.add).then_inc(s["by_step"], 1)
                dve.wait_ge(s["shifted"], 32)
                link(nc.vector.tensor_tensor(here[:, :], here[:, :], before[:, :], ALU.not_equal))
                nc.vector.tensor_scalar_mul(here[:, :], here[:, :], -BIG).then_inc(s["flag_set"], 1)
                dve.wait_ge(s["tails"], 16)
                dve.wait_ge(s["flags"], 16)
                nc.vector.tensor_reduce(split[:, 0, :], flags[:, :, :], AX.X, ALU.min).then_inc(s["split_min"], 1)
                nc.vector.tensor_reduce(split[:, 1, :], rows[TAIL][:, :, :], AX.X, ALU.min).then_inc(s["split_min"], 1)
                dve.wait_ge(s["split_min"], 2)
                for k in range(2):
                    dve.wait_ge(s["split_p"], k + 1)
                    nc.vector.tensor_copy(split_c[:, k, :], pc[0:SC, 384:384 + P]).then_inc(s["split_t"], 1)
                nc.vector.tensor_scalar_mul(rows[TAIL][:, :, :], rows[TAIL][:, :, :], -1.0 / BIG).then_inc(s["ready_t"], 1)
                for k in range(FIELDS):
                    dve.wait_ge(s["turned"], k + 1)
                    v = t["edges"][:, :, k]
                    nc.vector.tensor_copy(v[:, 0:512], ps[k % 2][:, 0:512]).then_inc(s["taken"], 1)
                    nc.vector.tensor_copy(v[:, 512:NSR], ps[k % 2][:, 512:NSR]).then_inc(s["taken"], 1)

            @block.tensor
            def _(pe):
                pe.wait_ge(s["ready_t"], 1)
                nb = NB // BP
                nc.tensor.matmul(pc[:, 0:NT - 1], t["ones"][0:nb, :], count[0:nb, :], start=True, stop=True).then_inc(s["counted"], 1)
                pe.wait_ge(s["steps_ready"], 1)
                nc.tensor.transpose(pc[0:SC, 256:256 + P], tile_of[:, :], t["ident"][:, :]).then_inc(s["tile_t"], 1)
                pe.wait_ge(s["split_min"], 2)
                pe.wait_ge(s["tile_c"], 1)
                for k in range(2):
                    freed(pe, s["split_t"], k)
                    nc.tensor.transpose(pc[0:SC, 384:384 + P], split[:, k, :], t["ident"][:, :]).then_inc(s["split_p"], 1)
                pe.wait_ge(s["ready_t"], 2)
                for k in range(FIELDS):
                    if k >= 2:
                        pe.wait_ge(s["taken"], 2 * (k - 1))
                    for c in range(SC):
                        last = nc.tensor.transpose(ps[k % 2][:, c * P:(c + 1) * P], rows[k][:, c, :], t["ident"][:, :])
                    last.then_inc(s["turned"], 1)


def nodes(nc, t, ins, layer):
    name = f"n{layer}_"
    attention = layer >= 2
    pairs = R // 2 if layer == 1 else 0
    ctx = ExitStack()
    with ctx:
        def sb(n, shape, dt=F32):
            return ctx.enter_context(nc.sbuf_tensor(name + n, shape, dt))

        sem = ctx.enter_context(semaphores(nc, name))

        def both(n):
            return [sem(n + "0"), sem(n + "1")]

        weight = {0: "L0_gnn_weight", 1: "L1_gnn_weight", 2: "L2_gnn_W", 3: "L3_gnn_W"}[layer]
        if layer == 1:
            w = t["agg"][:, :, :].rearrange("p t f -> p (t f)")[:, 0:2 * R * F].rearrange("p (c o) -> p c o", c=2)
        else:
            w = sb("w", [P, 2, F])
        stats = sb("stats", [P, NT, 6])
        mean, diff, var, std = (sb(n, [P, NT]) for n in ("mean", "diff", "var", "std"))
        rstd, shift = sb("rstd", [P, NT]), sb("shift", [P, NT])
        eps = sb("eps", [P, 1])
        h = sb("h", [P, 2, F])
        hT = sb("hT", [P, 2, 2, P])
        pT = [ctx.enter_context(nc.psum_tensor(name + f"pT{i}", [P, 512], F32)) for i in range(2)]
        if layer == 1:
            gate_w, gate, msg = sb("gate_w", [P, 2, R]), sb("gate", [P, 2, R]), sb("msg", [P, 2, R, F])
            pm = [ctx.enter_context(nc.psum_tensor(name + f"pm{i}", [P, 512], F32)) for i in range(4)]
            pg = [ctx.enter_context(nc.psum_tensor(name + f"pg{i}", [P, 512], F32)) for i in range(2)]
        else:
            pm = [ctx.enter_context(nc.psum_tensor(name + f"pm{i}", [P, 512], F32)) for i in range(2)]
        if layer == 0:
            zero, zero_set = sb("zero", [P, F]), sem("zero_set")
        if attention:
            heads = 4 if layer == 2 else H
            att = sb("att", [P, 2, F])
            row = sb("row", [P, 2, W])
            act_h, weighed, score = sb("act_h", [P, F]), sb("weighed", [P, 2, F]), sb("score", [P, 2, H])
        weights_in, eps_set, chain, stat_done = sem("weights_in"), sem("eps_set"), sem("chain"), sem("stat_done")
        var_ready, std_ready, scale_ready = sem("var_ready"), sem("std_ready"), sem("scale_ready")
        normed, turned, copied, prod, taken, written = (both(n) for n in ("normed", "turned", "copied", "prod", "taken", "written"))
        gate_prod, scored = both("gate_prod"), both("scored")
        filled = [sem(f"filled{i}") for i in range(4)]
        emptied = [sem(f"emptied{i}") for i in range(4)]
        n_weights = {0: 1, 1: 2, 2: 3, 3: 3}[layer]

        def pipeline(eng, first, second):
            def pair(it):
                first(it, 1)
                second(it, 0)
                first(it + 1, 0)
                second(it, 1)

            first(0, 0)
            pair(0)
            with eng.Fori(1, NT // 2) as it:
                pair(it)
            second(NT // 2, 0)

        def pipeline_two(eng, first, between, second):
            def pair(it, last=False):
                first(it + 1, 0)
                between(it, 1)
                second(it, 0)
                if not last:
                    first(it + 1, 1)
                between(it + 1, 0)
                second(it, 1)

            first(0, 0)
            first(0, 1)
            between(0, 0)
            pair(0)
            with eng.Fori(1, NT // 2 - 1) as it:
                pair(it)
            pair(NT // 2 - 1, last=True)
            second(NT // 2, 0)

        with nc.Block() as block:
            @block.sync
            def _(sp):
                if layer == 1:
                    for c in range(2):
                        sp.dma_start(w[:, c, :].rearrange("p (r o) -> p r o", r=R),
                                     ins[weight][:, c * P:(c + 1) * P, :].rearrange("r p o -> p r o")).then_inc(weights_in, 16)
                    with nc.allow_non_contiguous_dma(reason="small gate weights"):
                        for c in range(2):
                            sp.dma_start(gate_w[:, c, :], ins["L1_gnn_gate_weight"][:, c * P:(c + 1) * P, 0].rearrange("r p -> p r")).then_inc(weights_in, 16)
                else:
                    src = ins[weight] if layer != 3 else ins[weight].rearrange("f h d -> f (h d)")
                    sp.dma_start(w[:, :, :], src.rearrange("(c p) o -> p c o", p=P)).then_inc(weights_in, 16)
                if layer == 2:
                    a = ins["L2_gnn_att"]
                    for k in range(2):
                        sp.dma_start(att[:, k, :].rearrange("p (h d) -> p h d", h=4),
                                     a[0, :, k * 64:(k + 1) * 64].partition_broadcast(P)).then_inc(weights_in, 16)
                if layer == 3:
                    for k, n in enumerate(("L3_gnn_att_src", "L3_gnn_att_dst")):
                        sp.dma_start(att[:, k, :], flat(ins[n]).partition_broadcast(P)).then_inc(weights_in, 16)

                def store(it, par):
                    i = it * 2 + par
                    if layer == 1:
                        for slot in range(4):
                            sp.wait_ge(emptied[slot], it * 4 + (2 * par + 2))
                        sp.dma_start(t["msg_table"].rearrange("(r t p) f -> t p r f", r=R, p=P)[at(i)].rearrange("a p r f -> (a p) r f"),
                                     msg[:, par, :, :]).then_inc(written[par], 16)
                    if attention:
                        sp.wait_ge(scored[par], it + 1)
                        sp.dma_start(t["head_table"].rearrange("(t p) f -> t p f", p=P)[at(i)].rearrange("a p f -> (a p) f"),
                                     row[:, par, 0:F + H]).then_inc(written[par], 16)

                if layer == 0:
                    sp.wait_ge(zero_set, 1)
                    for a in t["sums"]:
                        sp.dma_start(a.rearrange("(t p) f -> p t f", p=P), zero[:, :].unsqueeze(1).to_broadcast([P, NT + 1, F])).then_inc(written[0], 16)
                    sp.wait_ge(written[0], 16 * K0)
                if layer:
                    store(0, 0)
                    store(0, 1)
                    with sp.Fori(1, NT // 2) as it:
                        store(it, 0)
                        store(it, 1)
                    store(NT // 2, 0)
                    sp.wait_ge(written[0], 16 * (NT // 2 + 1))
                    sp.wait_ge(written[1], 16 * (NT // 2))

            @block.scalar
            def _(act):
                act.wait_ge(eps_set, 1)
                act.wait_ge(var_ready, 1)
                nc.scalar.activation(std[:, :], var[:, :], ACT.Sqrt, bias=eps[:, 0:1]).then_inc(std_ready, 1)
                act.wait_ge(scale_ready, 1)

                def norm(it, par):
                    i = it * 2 + par
                    freed(act, turned[par], it)
                    nc.scalar.activation(h[:, par, :], t["x"][:, at(i), :].rearrange("p a f -> p (a f)"), ACT.Relu,
                                         bias=shift[:, at(i)], scale=rstd[:, at(i)]).then_inc(normed[par], 1)

                def copy(it, par):
                    freed(act, prod[par], it)
                    act.wait_ge(turned[par], it + 1)
                    nc.scalar.copy(hT[:, par, :, :].rearrange("p c n -> p (c n)"), pT[par][:, 0:F]).then_inc(copied[par], 1)

                def take(it, par):
                    i = it * 2 + par
                    if layer == 1:
                        act.wait_ge(gate_prod[par], it + 1)
                        freed(act, written[par], it * 16)
                        nc.scalar.activation(gate[:, par, :], pg[par][:, 0:R], ACT.Sigmoid).then_inc(taken[par], 1)
                        act.wait_ge(taken[par], it + 1)
                        for p in range(1, pairs, 2):
                            slot = p % 4
                            act.wait_ge(filled[slot], it * 4 + (2 * par + p // 4 + 1))
                            for r in range(2):
                                last = nc.scalar.activation(msg[:, par, 2 * p + r, :], pm[slot][:, r * F:(r + 1) * F], ACT.Copy,
                                                            scale=gate[:, par, 2 * p + r:2 * p + r + 1])
                            last.then_inc(emptied[slot], 1)
                        return
                    act.wait_ge(prod[par], it + 1)
                    if layer == 0:
                        out = t["agg"][:, at(i), 0:F].rearrange("p a f -> p (a f)")
                    else:
                        freed(act, written[par], it * 16)
                        out = row[:, par, 0:F]
                    nc.scalar.activation(out, pm[par][:, 0:F], ACT.Copy).then_inc(taken[par], 1)

                pipeline_two(act, norm, copy if attention else lambda it, par: None, take)

            @block.vector
            def _(dve):
                link = Chain(dve, chain)
                nc.vector.memset(eps[:, :], 1e-5).then_inc(eps_set, 1)
                if layer == 0:
                    nc.vector.memset(zero[:, :], 0.0).then_inc(zero_set, 1)
                with dve.Fori(0, NT // 7) as c:
                    for k in range(7):
                        i = c * 7 + k
                        nc.vector.bn_stats(stats[:, at(i), :].rearrange("p a s -> p (a s)"),
                                           t["x"][:, at(i), :].rearrange("p a f -> p (a f)")).then_inc(stat_done, 1)
                dve.wait_ge(stat_done, NT)
                link(nc.vector.tensor_tensor(mean[:, :], stats[:, :, 1], stats[:, :, 4], ALU.add))
                link(nc.vector.tensor_tensor(diff[:, :], stats[:, :, 1], stats[:, :, 4], ALU.subtract))
                link(nc.vector.tensor_tensor(var[:, :], stats[:, :, 2], stats[:, :, 5], ALU.add))
                link(nc.vector.tensor_tensor(diff[:, :], diff[:, :], diff[:, :], ALU.mult))
                link(nc.vector.tensor_scalar_mul(diff[:, :], diff[:, :], 0.25))
                nc.vector.scalar_tensor_tensor(var[:, :], var[:, :], 1.0 / F, diff[:, :], ALU.mult, ALU.add).then_inc(var_ready, 1)
                dve.wait_ge(std_ready, 1)
                link(nc.vector.reciprocal(rstd[:, :], std[:, :]))
                nc.vector.scalar_tensor_tensor(shift[:, :], mean[:, :], -0.5, rstd[:, :], ALU.mult, ALU.mult).then_inc(scale_ready, 1)
                dve.wait_ge(weights_in, 16 * (4 if layer == 1 else n_weights))

                def copy(it, par):
                    if layer == 1:
                        freed(dve, filled[3], it * 4 + (2 * par - 2))
                    else:
                        freed(dve, prod[par], it)
                    dve.wait_ge(turned[par], it + 1)
                    nc.vector.tensor_copy(hT[:, par, :, :].rearrange("p c n -> p (c n)"), pT[par][:, 0:F]).then_inc(copied[par], 1)

                def finish(it, par):
                    i = it * 2 + par
                    if layer == 1:
                        dve.wait_ge(taken[par], it + 1)
                        for p in range(0, pairs, 2):
                            slot = p % 4
                            dve.wait_ge(filled[slot], it * 4 + (2 * par + p // 4 + 1))
                            nc.vector.tensor_tensor(msg[:, par, 2 * p:2 * p + 2, :], pm[slot][:, :].rearrange("p (r f) -> p r f", r=2),
                                                    gate[:, par, 2 * p:2 * p + 2].unsqueeze(2).to_broadcast([P, 2, F]), ALU.mult).then_inc(emptied[slot], 1)
                    if attention:
                        dve.wait_ge(taken[par], it + 1)
                        feats = row[:, par, 0:F]
                        base = 5 if layer == 2 else 3
                        k0 = (it * 2 + par) * base + n_links
                        k = 0

                        def step(ins_):
                            nonlocal k
                            k += 1
                            ins_.then_inc(chain, 1)
                            dve.wait_ge(chain, k0 + k)

                        if layer == 2:
                            step(nc.vector.scalar_tensor_tensor(act_h[:, :], feats, 0.2, feats, ALU.mult, ALU.max))
                            feats = act_h[:, :]
                        step(nc.vector.tensor_tensor(weighed[:, :, :], feats.unsqueeze(1).to_broadcast([P, 2, F]), att[:, :, :], ALU.mult))
                        step(nc.vector.reduce_sum(score[:, :, 0:heads], weighed[:, :, :].rearrange("p k (h d) -> p k h d", h=heads), AX.X))
                        rep = H // heads
                        dup = [score[:, k_, 0:heads].unsqueeze(2).to_broadcast([P, heads, rep]) for k_ in range(2)]
                        here = at(i)
                        nc.vector.tensor_copy(t["dst_score"][:, here, :].rearrange("p a (h r) -> p (a h) r", r=rep), dup[1]).then_inc(chain, 1)
                        if layer == 2:
                            nc.vector.tensor_copy(t["src_score"][:, here, :].rearrange("p a (h r) -> p (a h) r", r=rep), dup[0]).then_inc(chain, 1)
                        nc.vector.tensor_copy(row[:, par, F:F + H].rearrange("p (h r) -> p h r", r=rep), dup[0]).then_inc(scored[par], 1)

                n_links = link.n
                pipeline(dve, (lambda it, par: None) if attention else copy, finish)
                if attention:
                    dve.wait_ge(chain, n_links + NT * (5 if layer == 2 else 3))

            @block.tensor
            def _(pe):
                pe.wait_ge(weights_in, 16 * (4 if layer == 1 else n_weights))

                def turn(it, par):
                    pe.wait_ge(normed[par], it + 1)
                    freed(pe, copied[par], it)
                    for c in range(2):
                        last = nc.tensor.transpose(pT[par][:, c * P:(c + 1) * P], h[:, par, c * P:(c + 1) * P], t["ident"][:, :])
                    last.then_inc(turned[par], 1)

                def multiply(it, par):
                    pe.wait_ge(copied[par], it + 1)
                    if layer != 1:
                        freed(pe, taken[par], it)
                        for c in range(2):
                            last = nc.tensor.matmul(pm[par][:, 0:F], hT[:, par, c, :], w[:, c, :], start=c == 0, stop=c == 1)
                        last.then_inc(prod[par], 1)
                        return
                    freed(pe, taken[par], it)
                    for c in range(2):
                        last = nc.tensor.matmul(pg[par][:, 0:R], hT[:, par, c, :], gate_w[:, c, :], start=c == 0, stop=c == 1)
                    last.then_inc(gate_prod[par], 1)
                    for p in range(pairs):
                        slot = p % 4
                        freed(pe, emptied[slot], it * 4 + (2 * par + p // 4))
                        for c in range(2):
                            last = nc.tensor.matmul(pm[slot][:, :], hT[:, par, c, :], w[:, c, p * 2 * F:(p + 1) * 2 * F], start=c == 0, stop=c == 1)
                        last.then_inc(filled[slot], 1)

                pipeline(pe, turn, multiply)


def scatter_edges(nc, t, ins):
    name = "e0_"
    ctx = ExitStack()
    with ctx:
        def sb(n, shape, dt=F32):
            return ctx.enter_context(nc.sbuf_tensor(name + n, shape, dt))

        sem = ctx.enter_context(semaphores(nc, name))

        def both(n):
            return [sem(n + "0"), sem(n + "1")]

        srow = sb("srow", [P, 2, G, P])
        stage = sb("stage", [P, 2, G, FIELDS])
        S, M = sb("S", [P, 2, G, P]), sb("M", [P, 2, G, P])
        SM = sb("SM", [P, 2, G, P])
        unused, count, off = sb("unused", [P, G, P]), sb("count", [P, G]), sb("off", [P, G])
        index = sb("index", [P, 2, G], I32)
        sums = sb("sums", [P, 2, G, F])
        p_sm = [ctx.enter_context(nc.psum_tensor(name + f"psm{i}", [P, 4, P], F32)) for i in range(2)]
        p_sum = [ctx.enter_context(nc.psum_tensor(name + f"psum{i}", [P, 2, F], F32)) for i in range(4)]
        rows_in = both("rows_in")
        added = [sem(f"added{k}") for k in range(K0)]
        chain, pace, made, indexed = (sem(n) for n in ("chain", "pace", "made", "indexed"))
        sm_done, sm_copied, sum_done, sum_copied = (sem(n) for n in ("sm_done", "sm_copied", "sum_done", "sum_copied"))
        LINKS = 4
        with nc.Block() as block:
            @block.sync
            def _(sp):
                def load(it, u):
                    b = it * 2 + u
                    freed(sp, made, b - 1)
                    sp.dma_start(srow[:, u, :, :].rearrange("p g e -> p (g e)"),
                                 flat(t["src_step"][span(b * G, G), :]).partition_broadcast(P)).then_inc(rows_in[u], 16)

                batches(sp, load, 2)

            @block.vector
            def _(dve):
                def batch(it, u):
                    b = it * 2 + u
                    link = Chain(dve, chain, b * LINKS)
                    link(nc.vector.tensor_copy(stage[:, u, :, :], t["edges"][:, span(b * G, G), :]))
                    freed(dve, sm_done, (b - 1) * 2)
                    dve.wait_ge(rows_in[u], it * 16 + 16)
                    nc.vector.tensor_tensor(S[:, u, :, :], stage[:, u, :, LOC].unsqueeze(2).to_broadcast([P, G, P]),
                                            t["col_no"][:, :].unsqueeze(1).to_broadcast([P, G, P]), ALU.is_equal)
                    for g in range(G):
                        nc.vector.tensor_scalar(M[:, u, g, :], srow[:, u, g, :], stage[:, u, g, SRC:SRC + 1],
                                                stage[:, u, g, W0:W0 + 1], ALU.is_equal, ALU.mult)
                    for g in range(G):
                        last = nc.vector.scalar_tensor_tensor(unused[:, g, :], srow[:, u, g, :], stage[:, u, g, SRC:SRC + 1],
                                                              t["earlier"][:, :], ALU.is_equal, ALU.mult, accum_out=count[:, g:g + 1])
                    last.then_inc(made, 1)
                    dve.wait_ge(made, b + 1)
                    link(nc.vector.tensor_tensor(off[:, :], t["spare_row"][:, :], stage[:, u, :, SRC], ALU.subtract))
                    link(nc.vector.tensor_scalar(count[:, :], count[:, :], 0.0, None, ALU.is_gt))
                    link(nc.vector.tensor_tensor(off[:, :], off[:, :], count[:, :], ALU.mult))
                    for k in range(K0):
                        freed(dve, added[k], (b - 1) * 16 * (G // K0))
                    nc.vector.tensor_tensor(index[:, u, :], off[:, :], stage[:, u, :, SRC], ALU.add).then_inc(indexed, 1)

                batches(dve, batch, 2)

            @block.tensor
            def _(pe):
                def batch(it, u):
                    b = it * 2 + u
                    tile = tiles_of(nc, pe, t, b)
                    pe.wait_ge(made, b + 1)
                    for half in range(2):
                        freed(pe, sm_copied, b * 2 + (half - 1))
                        for g in range(4 * half, 4 * half + 4):
                            last = nc.tensor.matmul(p_sm[half][:, g % 4, :], S[:, u, g, :], M[:, u, g, :], start=True, stop=True)
                        last.then_inc(sm_done, 1)
                    for pair in range(4):
                        pe.wait_ge(sm_copied, b * 2 + (pair // 2 + 1))
                        freed(pe, sum_copied, b * 4 + (pair - 3))
                        for g in range(2 * pair, 2 * pair + 2):
                            last = nc.tensor.matmul(p_sum[pair][:, g % 2, :], SM[:, u, g, :],
                                                    t["agg"][:, bass.ds(tile[g], 1), 0:F].rearrange("p a f -> p (a f)"), start=True, stop=True)
                        last.then_inc(sum_done, 1)

                batches(pe, batch, 2)

            @block.scalar
            def _(act):
                def batch(it, u):
                    b = it * 2 + u
                    for half in range(2):
                        act.wait_ge(sm_done, b * 2 + (half + 1))
                        freed(act, sum_done, (b - 1) * 4)
                        nc.scalar.copy(SM[:, u, 4 * half:4 * half + 4, :], p_sm[half][:, :, :]).then_inc(sm_copied, 1)
                    for pair in range(4):
                        act.wait_ge(sum_done, b * 4 + (pair + 1))
                        for k in ((2 * pair) % K0, (2 * pair + 1) % K0):
                            freed(act, added[k], (b * 2 + (pair // 2 - 3)) * 16)
                        nc.scalar.copy(sums[:, u, 2 * pair:2 * pair + 2, :], p_sum[pair][:, :, :]).then_inc(sum_copied, 1)

                batches(act, batch, 2)

            @block.gpsimd
            def _(pool):
                def batch(it, u):
                    b = it * 2 + u
                    pool.wait_ge(indexed, b + 1)
                    for g in range(G):
                        k = g % K0
                        pool.wait_ge(sum_copied, b * 4 + (g // 2 + 1))
                        freed(pool, added[k], (b * 2 + g // K0) * 16)
                        pool.sem_inc(pace, 1)
                        nc.gpsimd.indirect_dma_start(t["sums"][k][:, :], bass.IndirectOffsetOnAxis(ap=index[:, u, g:g + 1], axis=0),
                                                     sums[:, u, g, :], None, compute_op=ALU.add).then_inc(added[k], 16)

                batches(pool, batch, 2)
                for k in range(K0):
                    pool.wait_ge(added[k], 16 * NBAT * (G // K0))


def finish_scatter(nc, t, ins):
    TC = 7
    ctx = ExitStack()
    with ctx:
        part = ctx.enter_context(nc.sbuf_tensor("f0_part", [P, 2, K0, TC, F], F32))
        bias = ctx.enter_context(nc.sbuf_tensor("f0_bias", [P, F], F32))
        sem = ctx.enter_context(semaphores(nc, "f0_"))
        bias_in, parts_in, part_used, chain = sem("bias_in"), [sem("parts_in0"), sem("parts_in1")], sem("part_used"), sem("chain")
        with nc.Block() as block:
            @block.sync
            def _(sp):
                sp.dma_start(bias[:, :], ins["L0_gnn_bias"].partition_broadcast(P)).then_inc(bias_in, 16)
                for c in range(NT // TC):
                    freed(sp, part_used, c - 1)
                    for k in range(K0):
                        rows = t["sums"][k][c * TC * P:(c + 1) * TC * P, :]
                        sp.dma_start(part[:, c % 2, k, :, :], rows.rearrange("(t p) f -> p t f", p=P)).then_inc(parts_in[c % 2], 16)

            @block.vector
            def _(dve):
                link = Chain(dve, chain)
                dve.wait_ge(bias_in, 16)
                for c in range(NT // TC):
                    x, some = t["x"][:, c * TC:(c + 1) * TC, :], part[:, c % 2]
                    link(nc.vector.tensor_tensor(x, x, bias[:, :].unsqueeze(1).to_broadcast([P, TC, F]), ALU.add))
                    dve.wait_ge(parts_in[c % 2], (c // 2 + 1) * 16 * K0)
                    link(nc.vector.tensor_tensor(some[:, 0:2], some[:, 0:2], some[:, 2:4], ALU.add))
                    link(nc.vector.tensor_tensor(some[:, 0], some[:, 0], some[:, 1], ALU.add))
                    nc.vector.tensor_tensor(x, x, some[:, 0], ALU.add).then_inc(part_used, 1)


def relation_edges(nc, t, ins):
    name = "e1_"
    ctx = ExitStack()
    with ctx:
        def sb(n, shape, dt=F32):
            return ctx.enter_context(nc.sbuf_tensor(name + n, shape, dt))

        sem = ctx.enter_context(semaphores(nc, name))

        U = 4
        stage = sb("stage", [P, 2, G, FIELDS])
        S = sb("S", [P, 2, G, P])
        index = sb("index", [P, U, G], I32)
        rows = sb("rows", [P, U, G, F])
        p_sum = [ctx.enter_context(nc.psum_tensor(name + f"psum{i}", [P, 2, F], F32)) for i in range(4)]
        gathered = [[sem(f"gathered{u}_{g}") for g in range(G)] for u in range(U)]
        staged, pace, indexed, made, sum_done, zeroed, added = (
            sem(n) for n in ("staged", "pace", "indexed", "made", "sum_done", "zeroed", "added"))
        with nc.Block() as block:
            @block.gpsimd
            def _(pool):
                def batch(it, u):
                    b = it * U + u
                    pool.wait_ge(indexed, b + 1)
                    freed(pool, sum_done, (b - (U - 1)) * 4)
                    pool.sem_inc(pace, 1)
                    for g in range(G):
                        nc.gpsimd.indirect_dma_start(rows[:, u, g, :], None, t["msg_table"][:, :],
                                                     bass.IndirectOffsetOnAxis(ap=index[:, u, g:g + 1], axis=0)).then_inc(gathered[u][g], 16)

                batches(pool, batch, U)

            @block.vector
            def _(dve):
                nc.vector.memset(t["agg"][:, :, :], 0.0).then_inc(zeroed, 1)

                def look_up(it, u):
                    for g in range(G):
                        freed(dve, gathered[u][g], it * 16)
                    nc.vector.tensor_copy(index[:, u, :], t["edges"][:, span((it * U + u) * G, G), IDX1]).then_inc(indexed, 1)

                def one_hot(it, u):
                    b = it * U + u
                    nc.vector.tensor_copy(stage[:, u % 2, :, :], t["edges"][:, span(b * G, G), :]).then_inc(staged, 1)
                    dve.wait_ge(staged, b * 2 + 1)
                    freed(dve, sum_done, (b - 1) * 4)
                    wide = [P, G, P]
                    nc.vector.tensor_tensor(S[:, u % 2, :, :], stage[:, u % 2, :, LOC].unsqueeze(2).to_broadcast(wide),
                                            t["col_no"][:, :].unsqueeze(1).to_broadcast(wide), ALU.is_equal).then_inc(staged, 1)
                    dve.wait_ge(staged, b * 2 + 2)
                    nc.vector.tensor_tensor(S[:, u % 2, :, :], S[:, u % 2, :, :], stage[:, u % 2, :, W1].unsqueeze(2).to_broadcast(wide),
                                            ALU.mult).then_inc(made, 1)

                def batch(it, u):
                    b = it * U + u
                    tile = tiles_of(nc, dve, t, b)
                    if exists(b + 2):
                        look_up(it + (u + 2) // U, (u + 2) % U)
                    if exists(b + 1):
                        one_hot(it + (u + 1) // U, (u + 1) % U)
                    for g in range(G):
                        if g % 2 == 0:
                            dve.wait_ge(sum_done, b * 4 + (g // 2 + 1))
                        row = t["agg"][:, bass.ds(tile[g], 1), 0:F].rearrange("p a f -> p (a f)")
                        for k in range(2):
                            cols = slice(k * F // 2, (k + 1) * F // 2)
                            freed(dve, added, (b * G + g) * 2 + (k - 1))
                            nc.vector.tensor_tensor(row[:, cols], row[:, cols], p_sum[g // 2][:, g % 2, cols], ALU.add).then_inc(added, 1)

                dve.wait_ge(zeroed, 1)
                look_up(0, 0)
                look_up(0, 1)
                one_hot(0, 0)
                batches(dve, batch, U)
                dve.wait_ge(added, NBAT * G * 2)
                nc.vector.scalar_tensor_tensor(t["x"][:, :, :], t["agg"][:, :, 0:F], 0.0, t["x"][:, :, :], ALU.max, ALU.add).then_inc(zeroed, 1)
                dve.wait_ge(zeroed, 2)

            @block.tensor
            def _(pe):
                def batch(it, u):
                    b = it * U + u
                    pe.wait_ge(made, b + 1)
                    for g in range(G):
                        if g % 2 == 0:
                            freed(pe, added, ((b - 1) * G + (g + 2)) * 2)
                        pe.wait_ge(gathered[u][g], it * 16 + 16)
                        last = nc.tensor.matmul(p_sum[g // 2][:, g % 2, :], S[:, u % 2, g, :], rows[:, u, g, :], start=True, stop=True)
                        if g % 2:
                            last.then_inc(sum_done, 1)

                batches(pe, batch, U)


def attention_edges(nc, t, ins, layer):
    name = f"a{layer}_"
    leaky = layer == 3
    ctx = ExitStack()
    with ctx:
        def sb(n, shape, dt=F32):
            return ctx.enter_context(nc.sbuf_tensor(name + n, shape, dt))

        def bank(n):
            return ctx.enter_context(nc.psum_tensor(name + n, [P, 512], F32))

        sem = ctx.enter_context(semaphores(nc, name))
        U = 4
        HG = H * G
        J = G + 1
        HJ = H * J
        V = slice(F, F + H)
        WL = F + H if leaky else W
        halves = slice(0, F // 2), slice(F // 2, WL)
        stage = sb("stage", [P, U, G, FIELDS])
        S, ST = sb("S", [P, U, G, P]), sb("ST", [P, G * P], BF16)
        index = sb("index", [P, U, G], I32)
        rows = sb("rows", [P, U, G, W])
        loc_row = sb("loc_row", [P, G * P])
        new_dst = sb("new_dst", [HJ, 2, P + 1])
        turned = sb("turned", [P, 2, H, J])
        up, top = sb("up", [HJ, P]), sb("top", [HJ, P])
        carried = sb("carried", [HJ, 2])
        split_up, split_down = sb("split_up", [1, 2, H, J]), sb("split_down", [1, 2, H, J])
        last_up, first_down = sb("last_up", [1, H, J]), sb("first_down", [1, H, J])
        join_up, join_down = sb("join_up", [1, 2, H, J]), sb("join_down", [1, HJ + 1])
        a = sb("a", [P, 2, HG])
        parts = sb("parts", [P, NT, 3, H], BF16)
        z = sb("z", [P, 2, HG + H])
        growth = sb("growth", [1, 2, H])
        scale = sb("scale", [P, H])
        bank_a, bank_top, bank_turn, bank_join = bank("bank_a"), bank("bank_top"), bank("bank_turn"), bank("bank_join")
        p_a, p_scale = bank_a[:, 0:3 * HG], bank_a[:, 3 * HG:3 * HG + H]
        p_top, p_turn = bank_top[:, 0:HJ], bank_turn[0:HJ, 0:P]
        p_last, p_first, p_carried = bank_join[0:1, 0:HJ], bank_join[0:1, HJ:2 * HJ], bank_join[0:HJ, 2 * HJ:2 * HJ + 2]
        p_sum = [bank(f"psum{i}") for i in range(4)]
        gathered = [sem(f"gathered{u}") for u in range(U)]
        loc_in, new_in = sem("loc_in"), [sem("new_in0"), sem("new_in1")]
        names = ["rows_set", "packed", "pace", "turn_pace", "indexed", "staged", "splits", "st_made", "st_half", "s_half", "made", "turned", "a_done",
                 "first_scans", "ends_in", "joined", "ends_turned", "scale_in", "carried_done", "carried_in", "up_done", "scanned", "top_done",
                 "raised", "z_ready", "exp_done", "weighed", "a_in", "split_off", "scale_done", "sum_done", "old_scaled", "added", "zeroed"]
        s = {n: sem(n) for n in names}

        def ahead(it, u, by):
            return it + (u + by) // U, (u + by) % U

        def flat1(ap):
            return ap.rearrange("p h j -> p (h j)")

        with nc.Block() as block:
            @block.sync
            def _(sp):
                def load(it, u):
                    b = it * U + u
                    freed(sp, s["scanned"], b - 1)
                    sp.dma_start(new_dst[:, u % 2, :], t["flag_rows"][span(b, 1)].rearrange("a h g e -> (a h g) e")).then_inc(new_in[u % 2], 16)
                    if leaky:
                        freed(sp, s["st_made"], b)
                        sp.dma_start(loc_row[:, :], flat(t["loc_step"][span(b * G, G), :]).partition_broadcast(P)).then_inc(loc_in, 16)

                batches(sp, load, U)

            @block.gpsimd
            def _(pool):
                nc.gpsimd.memset(rows[:, :, :, F:W], 0.0).then_inc(s["rows_set"], 1)
                pool.wait_ge(s["rows_set"], 1)

                def batch(it, u):
                    b = it * U + u
                    pool.wait_ge(s["indexed"], b + 1)
                    for g in range(G):
                        freed(pool, s["sum_done"], (b - U) * G + (g + 1))
                        pool.sem_inc(s["pace"], 1)
                        nc.gpsimd.indirect_dma_start(rows[:, u, g, 0:F + H], None, t["head_table"][:, :],
                                                     bass.IndirectOffsetOnAxis(ap=index[:, u, g:g + 1], axis=0)).then_inc(gathered[u], 16)

                batches(pool, batch, U)

            @block.scalar
            def _(act):
                act.wait_ge(s["zeroed"], 7)

                def take_in(it, u):
                    b = it * U + u
                    freed(act, s["z_ready"], (b - (U - 1)) * 2)
                    nc.scalar.copy(stage[:, u, :, :], t["edges"][:, span(b * G, G), :]).then_inc(s["staged"], 1)
                    freed(act, s["joined"], (b - 1) * 2)
                    for k, (split, lo) in enumerate(((split_up, 1), (split_down, 0))):
                        last = nc.scalar.copy(split[:, u % 2, :, lo:lo + G], t["split_row"][0:1, k, span(b * G, G)].unsqueeze(1).to_broadcast([1, H, G]))
                    last.then_inc(s["splits"], 1)
                    act.wait_ge(gathered[u], it * 16 * G + 16 * G)
                    freed(act, s["turned"], b - 1)
                    nc.scalar.copy(turned[:, u % 2, :, 0:G], rows[:, u, :, V].rearrange("p g h -> p h g")).then_inc(s["packed"], 1)

                def one_hots(it, u):
                    b = it * U + u
                    act.wait_ge(s["staged"], b + 1)
                    freed(act, s["sum_done"], (b - (U - 1)) * G)
                    for g in range(G):
                        last = nc.scalar.activation(S[:, u, g, :], t["col_no"][:, :], ACT.Abs, bias=stage[:, u, g, LOC:LOC + 1], scale=-1.0)
                    last.then_inc(s["s_half"], 1)
                    if leaky:
                        act.wait_ge(loc_in, b * 16 + 16)
                        nc.scalar.activation(loc_row[:, :], loc_row[:, :], ACT.Abs, bias=t["row_no"][:, 0:1], scale=-1.0).then_inc(s["st_half"], 1)
                    act.wait_ge(s["s_half"], b + 1)
                    nc.scalar.activation(S[:, u, :, :], S[:, u, :, :], ACT.Relu, bias=t["ones"][:, 0:1], scale=-1.0).then_inc(s["made"], 1)
                    if leaky:
                        act.wait_ge(s["st_half"], b + 1)
                        freed(act, s["a_done"], b)
                        nc.scalar.activation(ST[:, :], loc_row[:, :], ACT.Relu, bias=t["ones"][:, 0:1], scale=-1.0).then_inc(s["st_made"], 1)

                def take_ends(it, u):
                    b = it * U + u
                    act.wait_ge(s["ends_turned"], b + 1)
                    freed(act, s["joined"], b * 2)
                    nc.scalar.copy(last_up[:, :, 1:J], p_last.rearrange("p (h j) -> p h j", j=J)[:, :, 0:J - 1])
                    nc.scalar.copy(last_up[:, :, 0], join_up[:, (u + 1) % 2, :, G])
                    nc.scalar.copy(flat1(first_down[:, :, :]), p_first).then_inc(s["ends_in"], 1)

                def take_scale(it, u):
                    b = it * U + u
                    act.wait_ge(s["scale_done"], b + 1)
                    freed(act, s["old_scaled"], b * 3)
                    nc.scalar.activation(scale[:, :], p_scale, ACT.Identity, bias=t["ones"][:, 0:1]).then_inc(s["scale_in"], 1)

                def exponentials(it, u):
                    b = it * U + u
                    act.wait_ge(s["z_ready"], b * 2 + 2)
                    nc.scalar.activation(rows[:, u, :, V], z[:, 0, 0:HG].rearrange("p (g h) -> p g h", h=H), ACT.Exp).then_inc(s["exp_done"], 1)
                    nc.scalar.activation(z[0:1, 1, HG:], z[0:1, 0, HG:], ACT.Exp).then_inc(s["exp_done"], 1)

                def batch(it, u):
                    b = it * U + u
                    if exists(b + 1):
                        exponentials(*ahead(it, u, 1))
                    take_scale(it, u)
                    if exists(b + 2):
                        take_ends(*ahead(it, u, 2))
                    if exists(b + 3):
                        take_in(*ahead(it, u, 3))
                        one_hots(*ahead(it, u, 3))

                take_in(0, 0)
                one_hots(0, 0)
                take_ends(0, 0)
                take_in(0, 1)
                one_hots(0, 1)
                exponentials(0, 0)
                take_ends(0, 1)
                take_in(0, 2)
                one_hots(0, 2)
                batches(act, batch, U)

            @block.vector
            def _(dve):
                nc.vector.memset(t["agg"][:, :, :], 0.0).then_inc(s["zeroed"], 1)
                nc.vector.memset(z[:, :, :], 0.0).then_inc(s["zeroed"], 1)
                nc.vector.memset(join_up[:, :, :, :], -BIG).then_inc(s["zeroed"], 1)
                nc.vector.memset(turned[:, :, :, :], -BIG).then_inc(s["zeroed"], 1)
                nc.vector.memset(split_up[:, :, :, :], -BIG).then_inc(s["zeroed"], 1)
                nc.vector.memset(split_down[:, :, :, :], -BIG).then_inc(s["zeroed"], 1)
                nc.vector.memset(join_down[:, :], -BIG).then_inc(s["zeroed"], 1)

                def look_up(it, u):
                    freed(dve, gathered[u], it * 16 * G)
                    nc.vector.tensor_copy(index[:, u, :], t["edges"][:, span((it * U + u) * G, G), SRC]).then_inc(s["indexed"], 1)

                def scan_last(it, u):
                    b = it * U + u
                    new = new_dst[:, u % 2, :]
                    dve.wait_ge(s["turned"], b + 1)
                    dve.wait_ge(new_in[u % 2], it * (16 * U // 2) + 16 * (u // 2 + 1))
                    nc.vector.tensor_tensor_scan(up[:, :], new[:, 0:P], p_turn, -BIG, ALU.add, ALU.max).then_inc(s["first_scans"], 1)

                def scan_first(it, u):
                    b = it * U + u
                    new = new_dst[:, u % 2, :]
                    freed(dve, s["top_done"], b)
                    nc.vector.tensor_tensor_scan(top[:, ::-1], new[:, 1:P + 1][:, ::-1], p_turn[:, ::-1], -BIG, ALU.add, ALU.max).then_inc(s["first_scans"], 1)

                def join_steps(it, u):
                    b = it * U + u
                    dve.wait_ge(s["ends_in"], b + 1)
                    dve.wait_ge(s["splits"], b + 1)
                    freed(dve, s["carried_done"], b)
                    nc.vector.tensor_tensor_scan(flat1(join_up[:, u % 2, :, :]), flat1(split_up[:, u % 2, :, :]), flat1(last_up[:, :, :]),
                                                 -BIG, ALU.add, ALU.max).then_inc(s["joined"], 1)
                    nc.vector.tensor_tensor_scan(join_down[:, 0:HJ][:, ::-1], flat1(split_down[:, u % 2, :, :])[:, ::-1],
                                                 flat1(first_down[:, :, :])[:, ::-1], -BIG, ALU.add, ALU.max).then_inc(s["joined"], 1)

                def take_carried(it, u):
                    dve.wait_ge(s["carried_done"], it * U + u + 1)
                    nc.vector.tensor_copy(carried[:, :], p_carried).then_inc(s["carried_in"], 1)

                def scan_up(it, u):
                    b = it * U + u
                    dve.wait_ge(s["carried_in"], b + 1)
                    nc.vector.tensor_tensor_scan(up[:, :], new_dst[:, u % 2, 0:P], p_turn, carried[:, 0:1], ALU.add, ALU.max).then_inc(s["up_done"], 1)

                def scan_down(it, u):
                    b = it * U + u
                    dve.wait_ge(s["up_done"], b + 1)
                    nc.vector.tensor_tensor_scan(top[:, ::-1], new_dst[:, u % 2, 1:P + 1][:, ::-1], up[:, ::-1], carried[:, 1:2],
                                                 ALU.add, ALU.max).then_inc(s["scanned"], 1)

                def differences(it, u, following):
                    b = it * U + u
                    dve.wait_ge(s["joined"], b * 2 + 2)
                    dve.wait_ge(s["top_done"], b + 1)
                    dve.wait_ge(s["staged"], b + 1)
                    v = rows[:, u, :, V]
                    here, tops = z[:, 0, 0:HG].rearrange("p (g h) -> p g h", h=H), p_top.rearrange("p (h g) -> p g h", h=H)[:, 0:G, :]
                    top0, old = p_top[0:1, :].rearrange("p (h g) -> p h g", h=H)[:, :, 0], join_up[:, u % 2, :, 0]
                    if not leaky:
                        nc.vector.tensor_tensor(z[0:1, 0, HG:], old, top0, ALU.min).then_inc(s["raised"], 1)
                        nc.vector.tensor_tensor(rows[:, u, :, F + H:W], tops, stage[:, u, :, TAIL].unsqueeze(2).to_broadcast([P, G, H]), ALU.mult)
                        nc.vector.tensor_tensor(here, v, tops, ALU.subtract).then_inc(s["z_ready"], 1)
                        dve.wait_ge(s["raised"], b + 1)
                        nc.vector.tensor_tensor(z[0:1, 0, HG:], z[0:1, 0, HG:], top0, ALU.subtract).then_inc(s["z_ready"], 1)
                        if following:
                            scan_last(*following)
                            scan_first(*following)
                        return
                    dve.wait_ge(s["a_in"], b + 1)
                    here_a = a[:, u % 2, :]
                    by_step = here_a.rearrange("p (g h) -> p g h", h=H)
                    nc.vector.tensor_tensor(z[:, 1, 0:HG].rearrange("p (g h) -> p g h", h=H), tops, by_step, ALU.add)
                    nc.vector.tensor_tensor(z[0:1, 1, HG:], top0, here_a[0:1, 0:H], ALU.add)
                    nc.vector.tensor_tensor(z[0:1, 0, HG:], old, here_a[0:1, 0:H], ALU.add)
                    nc.vector.tensor_tensor(here, v, by_step, ALU.add).then_inc(s["raised"], 1)
                    if following:
                        scan_last(*following)
                    dve.wait_ge(s["raised"], b * 2 + 1)
                    nc.vector.scalar_tensor_tensor(z[:, :, :], z[:, :, :], 0.2, z[:, :, :], ALU.mult, ALU.max).then_inc(s["raised"], 1)
                    if exists(b + 3):
                        look_up(*ahead(it, u, 3))
                    dve.wait_ge(s["raised"], b * 2 + 2)
                    nc.vector.tensor_tensor(z[0:1, 0, HG:], z[0:1, 0, HG:], z[0:1, 1, HG:], ALU.min).then_inc(s["z_ready"], 1)
                    dve.wait_ge(s["z_ready"], b * 2 + 1)
                    nc.vector.tensor_tensor(z[:, 0, :], z[:, 0, :], z[:, 1, :], ALU.subtract).then_inc(s["z_ready"], 1)
                    if following:
                        scan_first(*following)

                def take_scores(it, u):
                    dve.wait_ge(s["a_done"], it * U + u + 1)
                    nc.vector.reduce_sum(a[:, u % 2, :].rearrange("p (g h) -> p g h", h=H),
                                         p_a.rearrange("p (g k h) -> p g h k", g=G, k=3), AX.X).then_inc(s["a_in"], 1)

                def weigh(it, u):
                    b = it * U + u
                    dve.wait_ge(s["exp_done"], b * 2 + 2)
                    nc.vector.tensor_scalar_add(growth[:, u % 2, :], z[0:1, 1, HG:], -1.0)
                    feats = rows[:, u, :, 0:F].rearrange("p g (h c) -> p g h c", h=H)
                    nc.vector.tensor_tensor(feats, feats, rows[:, u, :, V].unsqueeze(3).to_broadcast([P, G, H, C]), ALU.mult).then_inc(s["weighed"], 1)

                def add(it, u, tile, some):
                    b = it * U + u
                    for g in some:
                        here = t["agg"][:, bass.ds(tile[g], 1), :].rearrange("p a f -> p (a f)")
                        if g == 0:
                            dve.wait_ge(s["scale_in"], b + 1)
                            freed(dve, s["added"], b * G * 2)
                            old = here[:, 0:F].rearrange("p (h c) -> p h c", h=H)
                            for heads in (slice(0, H // 2), slice(H // 2, H)):
                                nc.vector.tensor_tensor(old[:, heads], old[:, heads], scale[:, heads].unsqueeze(2).to_broadcast([P, H // 2, C]),
                                                        ALU.mult).then_inc(s["old_scaled"], 1)
                            nc.vector.tensor_tensor(here[:, V], here[:, V], scale[:, :], ALU.mult).then_inc(s["old_scaled"], 1)
                        dve.wait_ge(s["sum_done"], b * G + (g + 1))
                        for k, cols in enumerate(halves):
                            if g == 0:
                                dve.wait_ge(s["old_scaled"], b * 3 + (1, 3)[k])
                            freed(dve, s["added"], (b * G + g) * 2 + (k - 1))
                            nc.vector.tensor_tensor(here[:, cols], here[:, cols], p_sum[g % 4][:, cols], ALU.add).then_inc(s["added"], 1)

                def batch(it, u):
                    b = it * U + u
                    if exists(b + 1):
                        weigh(*ahead(it, u, 1))
                    tile = tiles_of(nc, dve, t, b)
                    if exists(b + 2):
                        join_steps(*ahead(it, u, 2))
                    add(it, u, tile, (0, 1))
                    if exists(b + 2):
                        take_carried(*ahead(it, u, 2))
                    add(it, u, tile, (2,))
                    if exists(b + 2):
                        scan_up(*ahead(it, u, 2))
                    add(it, u, tile, (3,))
                    if exists(b + 2):
                        scan_down(*ahead(it, u, 2))
                    add(it, u, tile, (4,))
                    if not leaky and exists(b + 5):
                        look_up(*ahead(it, u, 5))
                    add(it, u, tile, (5,))
                    if leaky and exists(b + 2):
                        take_scores(*ahead(it, u, 2))
                    add(it, u, tile, (6, 7))
                    if exists(b + 2):
                        differences(*ahead(it, u, 2), ahead(it, u, 3) if exists(b + 3) else None)

                if leaky:
                    left, rest = t["dst_score"][:, :, :], t["src_score"]
                    for k in range(3):
                        nc.vector.tensor_copy(parts[:, :, k, :], left).then_inc(s["split_off"], 1)
                        dve.wait_ge(s["split_off"], 2 * k + 1)
                        if k < 2:
                            nc.vector.tensor_tensor(rest[:, :, :], left, parts[:, :, k, :], ALU.subtract).then_inc(s["split_off"], 1)
                            dve.wait_ge(s["split_off"], 2 * k + 2)
                            left = rest[:, :, :]
                dve.wait_ge(s["zeroed"], 7)
                for u in range(3 if leaky else U + 1):
                    look_up(u // U, u % U)
                scan_last(0, 0)
                scan_first(0, 0)
                for u in range(2):
                    if u:
                        weigh(0, 0)
                    join_steps(0, u)
                    take_carried(0, u)
                    scan_up(0, u)
                    scan_down(0, u)
                    if leaky:
                        take_scores(0, u)
                    differences(0, u, (0, u + 1))
                batches(dve, batch, U)

            @block.tensor
            def _(pe):
                def turn(it, u):
                    pe.wait_ge(s["packed"], it * U + u + 1)
                    pe.sem_inc(s["turn_pace"], 1)
                    nc.tensor.transpose(p_turn, turned[:, u % 2, :, :].rearrange("p h g -> p (h g)"), t["ident"][:, :]).then_inc(s["turned"], 1)

                def dst_scores(it, u, tile):
                    b = it * U + u
                    pe.wait_ge(s["st_made"], b + 1)
                    freed(pe, s["a_in"], b)
                    freed(pe, s["scale_in"], b - 1)
                    for g in range(G):
                        last = nc.tensor.matmul(p_a[:, g * 3 * H:(g + 1) * 3 * H], ST[:, g * P:(g + 1) * P],
                                                parts[:, bass.ds(tile[g], 1), :, :].rearrange("p a k h -> p (a k h)"), start=True, stop=True)
                    last.then_inc(s["a_done"], 1)

                def turn_ends(it, u):
                    b = it * U + u
                    pe.wait_ge(s["first_scans"], b * 2 + 2)
                    pe.sem_inc(s["turn_pace"], 1)
                    nc.tensor.transpose(p_last, up[:, P - 1:P], t["ident"][0:HJ, 0:HJ])
                    nc.tensor.transpose(p_first, top[:, 0:1], t["ident"][0:HJ, 0:HJ]).then_inc(s["ends_turned"], 1)

                def turn_joined(it, u):
                    b = it * U + u
                    pe.wait_ge(s["joined"], b * 2 + 2)
                    pe.sem_inc(s["turn_pace"], 1)
                    nc.tensor.transpose(p_carried[:, 0:1], flat1(join_up[:, u % 2, :, :]), t["ident"][0:1, 0:1])
                    nc.tensor.transpose(p_carried[:, 1:2], join_down[:, 1:HJ + 1], t["ident"][0:1, 0:1]).then_inc(s["carried_done"], 1)

                def turn_maxima(it, u):
                    b = it * U + u
                    pe.wait_ge(s["scanned"], b + 1)
                    pe.sem_inc(s["turn_pace"], 1)
                    nc.tensor.transpose(p_top, top[:, :], t["ident"][0:HJ, 0:HJ]).then_inc(s["top_done"], 1)

                def sums(it, u, some):
                    b = it * U + u
                    if some[0] == 0:
                        pe.wait_ge(s["made"], b + 1)
                        pe.wait_ge(s["weighed"], b + 1)
                    for g in some:
                        freed(pe, s["added"], (b * G + (g - 3)) * 2)
                        nc.tensor.matmul(p_sum[g % 4][:, 0:WL], S[:, u, g, :], rows[:, u, g, 0:WL], start=True, stop=True).then_inc(s["sum_done"], 1)
                        if g != G // 2 - 1:
                            continue
                        if leaky and exists(b + 1):
                            pe.wait_ge(s["a_in"], b + 2)
                        nc.tensor.matmul(p_scale, S[0:1, u, 0, :], growth[:, u % 2, :], start=True, stop=True).then_inc(s["scale_done"], 1)

                def batch(it, u):
                    b = it * U + u
                    sums(it, u, range(0, G // 2))
                    if exists(b + 2):
                        turn_ends(*ahead(it, u, 2))
                        if leaky:
                            tile = tiles_of(nc, pe, t, b + 2)
                        turn_joined(*ahead(it, u, 2))
                        if leaky:
                            dst_scores(*ahead(it, u, 2), tile)
                    sums(it, u, range(G // 2, G))
                    if exists(b + 2):
                        turn_maxima(*ahead(it, u, 2))
                    if exists(b + 3):
                        turn(*ahead(it, u, 3))

                turn(0, 0)
                if leaky:
                    pe.wait_ge(s["split_off"], 5)
                for u in range(2):
                    turn_ends(0, u)
                    turn_joined(0, u)
                    if leaky:
                        dst_scores(0, u, tiles_of(nc, pe, t, u))
                    turn_maxima(0, u)
                    turn(0, u + 1)
                batches(pe, batch, U)


def finish_global(nc, t, ins):
    ctx = ExitStack()
    with ctx:
        def sb(n, shape, dt=F32):
            return ctx.enter_context(nc.sbuf_tensor("f2_" + n, shape, dt))

        sem = ctx.enter_context(semaphores(nc, "f2_"))

        h = sb("h", [P, NT, F])
        bias = sb("bias", [P, F])
        m, own, q, top, low = (sb(n, [P, NT, H]) for n in ("m", "own", "q", "top", "low"))
        best, best_all, part, inv = (sb(n, [P, H]) for n in ("best", "best_all", "part", "inv"))
        pz = ctx.enter_context(nc.psum_tensor("f2_pz", [P, 512], F32))
        h_in, bias_in, chain, best_ready, all_ready, exp_in, exp_out, part_ready, z_ready = (
            sem(n) for n in ("h_in", "bias_in", "chain", "best_ready", "all_ready", "exp_in", "exp_out", "part_ready", "z_ready"))
        everywhere = [P, NT, H]
        with nc.Block() as block:
            @block.sync
            def _(sp):
                sp.dma_start(h[:, :, :], t["head_table"].rearrange("(t p) f -> p t f", p=P)[:, :, 0:F]).then_inc(h_in, 16)
                sp.dma_start(bias[:, :], ins["L2_gnn_b"].partition_broadcast(P)).then_inc(bias_in, 16)

            @block.vector
            def _(dve):
                link = Chain(dve, chain)
                agg, x = t["agg"], t["x"]
                den, tail = agg[:, :, F:F + H], agg[:, :, F + H:W]
                link(nc.vector.tensor_scalar(m[:, :, :], den, 0.0, -BIG, ALU.is_equal, ALU.mult))
                link(nc.vector.tensor_tensor(m[:, :, :], m[:, :, :], tail, ALU.add))
                link(nc.vector.tensor_tensor(top[:, :, :], m[:, :, :], t["src_score"][:, :, :], ALU.max))
                link(nc.vector.tensor_tensor(m[:, :, :], m[:, :, :], top[:, :, :], ALU.subtract))
                nc.vector.tensor_tensor(own[:, :, :], t["src_score"][:, :, :], top[:, :, :], ALU.subtract).then_inc(exp_in, 1)
                link(nc.vector.tensor_tensor(q[:, :, :], top[:, :, :], t["dst_score"][:, :, :], ALU.add))
                link(nc.vector.tensor_tensor(q[:, :, :], q[:, :, :], t["valid"][:, :].rearrange("p (t h) -> p t h", h=H), ALU.add))
                nc.vector.tensor_reduce(best[:, :], q[:, :, :].rearrange("p t h -> p h t"), AX.X, ALU.max).then_inc(best_ready, 1)
                dve.wait_ge(all_ready, 1)
                nc.vector.tensor_tensor(q[:, :, :], q[:, :, :], best_all[:, :].unsqueeze(1).to_broadcast(everywhere), ALU.subtract).then_inc(exp_in, 1)
                dve.wait_ge(exp_out, 3)
                link(nc.vector.tensor_tensor(low[:, :, :], den, m[:, :, :], ALU.mult))
                link(nc.vector.tensor_tensor(low[:, :, :], low[:, :, :], own[:, :, :], ALU.add))
                link(nc.vector.tensor_tensor(low[:, :, :], low[:, :, :], q[:, :, :], ALU.mult))
                nc.vector.reduce_sum(part[:, :], low[:, :, :].rearrange("p t h -> p h t"), AX.X).then_inc(part_ready, 1)
                dve.wait_ge(z_ready, 1)
                link(nc.vector.reciprocal(inv[:, :], pz[:, 0:H]))
                link(nc.vector.tensor_tensor(q[:, :, :], q[:, :, :], inv[:, :].unsqueeze(1).to_broadcast(everywhere), ALU.mult))
                link(nc.vector.tensor_tensor(m[:, :, :], m[:, :, :], q[:, :, :], ALU.mult))
                link(nc.vector.tensor_tensor(own[:, :, :], own[:, :, :], q[:, :, :], ALU.mult))

                def by_head(x_):
                    return x_.rearrange("p t (h c) -> p t h c", h=H)

                heads = [P, NT, H, C]
                feats = agg[:, :, 0:F]
                dve.wait_ge(h_in, 16)
                dve.wait_ge(bias_in, 16)
                link(nc.vector.tensor_tensor(by_head(feats), by_head(feats), m[:, :, :].unsqueeze(3).to_broadcast(heads), ALU.mult))
                link(nc.vector.tensor_tensor(by_head(h[:, :, :]), by_head(h[:, :, :]), own[:, :, :].unsqueeze(3).to_broadcast(heads), ALU.mult))
                link(nc.vector.tensor_tensor(h[:, :, :], h[:, :, :], feats, ALU.add))
                link(nc.vector.tensor_tensor(h[:, :, :], h[:, :, :], bias[:, :].unsqueeze(1).to_broadcast([P, NT, F]), ALU.add))
                link(nc.vector.tensor_tensor(x[:, :, :], x[:, :, :], h[:, :, :], ALU.add))

            @block.gpsimd
            def _(pool):
                pool.wait_ge(best_ready, 1)
                nc.gpsimd.partition_all_reduce(best_all[:, :], best[:, :], P, RMAX).then_inc(all_ready, 1)

            @block.scalar
            def _(act):
                act.wait_ge(exp_in, 1)
                nc.scalar.activation(m[:, :, :], m[:, :, :], ACT.Exp).then_inc(exp_out, 1)
                nc.scalar.activation(own[:, :, :], own[:, :, :], ACT.Exp).then_inc(exp_out, 1)
                act.wait_ge(exp_in, 2)
                nc.scalar.activation(q[:, :, :], q[:, :, :], ACT.Exp).then_inc(exp_out, 1)

            @block.tensor
            def _(pe):
                pe.wait_ge(part_ready, 1)
                nc.tensor.matmul(pz[:, 0:H], t["ones"][:, :], part[:, :], start=True, stop=True).then_inc(z_ready, 1)


def finish_local(nc, t, ins, out):
    TC = 7
    ctx = ExitStack()
    with ctx:
        bias = ctx.enter_context(nc.sbuf_tensor("f3_bias", [P, F], F32))
        inv = ctx.enter_context(nc.sbuf_tensor("f3_inv", [P, NT, H], F32))
        sem = ctx.enter_context(semaphores(nc, "f3_"))
        bias_in, chain, finished, stored = sem("bias_in"), sem("chain"), sem("finished"), sem("stored")
        with nc.Block() as block:
            @block.sync
            def _(sp):
                sp.dma_start(bias[:, :], ins["L3_gnn_bias"].partition_broadcast(P)).then_inc(bias_in, 16)
                for c in range(NT // TC):
                    sp.wait_ge(finished, c + 1)
                    full = min(TC, NT - 1 - c * TC)
                    rows = slice(c * TC * P, (c * TC + full) * P)
                    sp.dma_start(out[rows, :].rearrange("(t p) f -> p t f", p=P), t["x"][:, c * TC:c * TC + full, :]).then_inc(stored, 16)
                sp.dma_start(out[(NT - 1) * P:N, :], t["x"][0:LAST, NT - 1, :]).then_inc(stored, 16)
                sp.wait_ge(stored, 16 * (NT // TC + 1))

            @block.vector
            def _(dve):
                link = Chain(dve, chain)
                link(nc.vector.tensor_scalar_add(inv[:, :, :], t["agg"][:, :, F:F + H], 1e-16))
                link(nc.vector.reciprocal(inv[:, :, :], inv[:, :, :]))
                dve.wait_ge(bias_in, 16)
                for c in range(NT // TC):
                    some = slice(c * TC, (c + 1) * TC)
                    feats, x = t["agg"][:, some, 0:F], t["x"][:, some, :]
                    by_head = feats.rearrange("p t (h c) -> p t h c", h=H)
                    link(nc.vector.tensor_tensor(by_head, by_head, inv[:, some, :].unsqueeze(3).to_broadcast([P, TC, H, C]), ALU.mult))
                    link(nc.vector.tensor_tensor(feats, feats, bias[:, :].unsqueeze(1).to_broadcast([P, TC, F]), ALU.add))
                    nc.vector.scalar_tensor_tensor(x, feats, 0.0, x, ALU.max, ALU.add).then_inc(finished, 1)


def program(nc, ins, out):
    ctx = ExitStack()
    with ctx:
        def sb(name, shape, dt=F32):
            return ctx.enter_context(nc.sbuf_tensor(name, shape, dt))

        def dram(name, shape, dt=F32):
            return nc.dram_tensor(name, shape, dt, kind="Internal").ap()

        t = {
            "x": sb("x", [P, NT, F]),
            "edges": sb("edges", [P, NSR, FIELDS]),
            "split_row": sb("split_row", [1, 2, NSR]),
            "split_dram": dram("split_dram", (2, NSR)), "flag_rows": dram("flag_rows", (NBAT, H, G + 1, P + 1)),
            "tile_row": sb("tile_row", [1, NSR], I32),
            "ones": sb("ones", [P, P]), "ident": sb("ident", [P, P]), "earlier": sb("earlier", [P, P]),
            "col_no": sb("col_no", [P, P]), "row_no": sb("row_no", [P, G]), "spare_row": sb("spare_row", [P, G]),
            "valid": sb("valid", [P, NT * H]),
            "dst_blk": dram("dst_blk", (NB, P), I32), "src_blk": dram("src_blk", (NB, P), I32),
            "type_blk": dram("type_blk", (NB, P), I32),
            "w0_blk": dram("w0_blk", (NB, P)), "w1_blk": dram("w1_blk", (NB, P)),
            "tile_dram": dram("tile_dram", (NSR,), I32),
            "dst_step": dram("dst_step", (NSR * P + 1,)), "flag_step": dram("flag_step", (NSR * P + 1,)),
            "loc_step": dram("loc_step", (NSR, P)), "src_step": dram("src_step", (NSR, P)),
        }
        t["agg"] = sb("agg", [P, NT, W])
        t["dst_score"], t["src_score"] = sb("dst_score", [P, NT, H]), sb("src_score", [P, NT, H])
        t["msg_table"] = dram("msg_table", (R * NP, F))
        t["sums"] = [dram(f"sums{k}", (NP + P, F)) for k in range(K0)]
        t["head_table"] = dram("head_table", (NP, F + H))
        prepare(nc, t, ins)
        nodes(nc, t, ins, 0)
        scatter_edges(nc, t, ins)
        finish_scatter(nc, t, ins)
        nodes(nc, t, ins, 1)
        relation_edges(nc, t, ins)
        nodes(nc, t, ins, 2)
        attention_edges(nc, t, ins, 2)
        finish_global(nc, t, ins)
        nodes(nc, t, ins, 3)
        attention_edges(nc, t, ins, 3)
        finish_local(nc, t, ins, out)


INPUTS = ["x", "src", "dst", "edge_type_16", "edge_weight", "edge_weight1", "L0_gnn_weight", "L0_gnn_bias",
          "L1_gnn_weight", "L1_gnn_gate_weight", "L2_gnn_W", "L2_gnn_att", "L2_gnn_b", "L3_gnn_W",
          "L3_gnn_att_src", "L3_gnn_att_dst", "L3_gnn_bias"]


def kernel(**inputs):
    import numpy as np
    import concourse.bacc as bacc
    from concourse.bass_utils import run_bass_kernel_spmd

    nc = bacc.Bacc("TRN2", target_bir_lowering=False, num_devices=1)
    arrays, ins = {}, {}
    for name in INPUTS:
        a = np.ascontiguousarray(inputs[name])
        arrays[f"in_{name}"] = a
        ins[name] = nc.dram_tensor(f"in_{name}", a.shape, mybir.dt.from_np(a.dtype), kind="ExternalInput").ap()
    out = nc.dram_tensor("result", (N, F), F32, kind="ExternalOutput").ap()
    program(nc, ins, out)
    return run_bass_kernel_spmd(nc, [arrays], core_ids=[0]).results[0]["result"]
```
